# Optimizing a Trainium2 kernel written in Bass

```python
import numpy as np
import jax
import jax.numpy as jnp

def _softmax(x, axis=-1):
    return jax.nn.softmax(x, axis=axis)

def _gelu(x):
    return jax.nn.gelu(x, approximate=True)

def _silu(x):
    return jax.nn.silu(x)

def _sigmoid(x):
    return jax.nn.sigmoid(x)

def _layernorm(x, axis=-1, eps=1e-05):
    m = jnp.mean(x, axis=axis, keepdims=True)
    v = jnp.var(x, axis=axis, keepdims=True)
    return (x - m) / jnp.sqrt(v + eps)

def _scatter_add(tgt, idx, src, axis=0):
    return tgt.at[idx].add(src)

def _segment_sum(src, seg, n):
    return jax.ops.segment_sum(src, seg, n)
kernel_name = 'mk_adj_resnorm_d2_adj_r2_02f29c'

def setup_inputs(seed: int=0):
    np.random.seed(seed)
    _w = jnp.asarray

    def _rec_inputs():
        import jax
        import jax.numpy as jnp
        _gk = jax.random.key(seed)
        x = -0.0002928 + 1 * jax.random.normal(jax.random.fold_in(_gk, 1), (4096, 256), jnp.float32)
        _a = jax.random.bernoulli(jax.random.fold_in(_gk, 2), 0.00390625, (4096, 4096))
        _a = jnp.logical_or(_a, jnp.swapaxes(_a, -1, -2))
        _a = jnp.logical_or(_a, jnp.eye(4096, dtype=bool))
        _af = _a.astype(jnp.float32)
        adj = _af
        return (x, adj)
    x, adj = _rec_inputs()

    def _L0_gnn_setup():
        import jax, jax.numpy as jnp
        import numpy as np
        N = 4096
        F_IN = 256
        F_OUT = 256
        DENSITY = 0.01
        key = jax.random.key(seed)
        k_x, k_adj, k_w, k_b = jax.random.split(key, 4)
        input_features = jax.random.normal(k_x, (N, F_IN), dtype=jnp.float32)
        adj = (jax.random.uniform(k_adj, (N, N)) < DENSITY).astype(jnp.float32)
        idx = jnp.arange(N)
        adj = adj.at[idx, idx].set(1.0)
        W = jax.random.normal(k_w, (F_IN, F_OUT), dtype=jnp.float32) / np.sqrt(F_IN)
        b = jax.random.normal(k_b, (F_OUT,), dtype=jnp.float32) * 0.01
        return {'input_features': input_features, 'adj': adj, 'W': W, 'b': b}
    _L0_gnn_all = _L0_gnn_setup()
    _L0_gnn_in = {k: v for k, v in _L0_gnn_all.items() if k in ('W', 'b')}
    del _L0_gnn_all

    def _L1_gnn_setup():
        import jax, jax.numpy as jnp
        import numpy as np
        N = 2048
        DIM_IN = 256
        DIM_Q = 256
        DIM_K = 256
        N_GRAPHS = 32
        key = jax.random.key(seed)
        ks = jax.random.split(key, 9)
        x = jax.random.normal(ks[0], (N, DIM_IN), dtype=jnp.float32)
        b = jax.random.normal(ks[1], (N, N), dtype=jnp.float32)
        edge_encoding = jax.random.normal(ks[2], (N, N), dtype=jnp.float32)
        ptr = jnp.arange(N_GRAPHS + 1, dtype=jnp.int64) * (N // N_GRAPHS)
        s_in = 1.0 / np.sqrt(DIM_IN)
        Wq = jax.random.normal(ks[3], (DIM_Q, DIM_IN), dtype=jnp.float32) * s_in
        bq = jnp.zeros((DIM_Q,), dtype=jnp.float32)
        Wk = jax.random.normal(ks[4], (DIM_K, DIM_IN), dtype=jnp.float32) * s_in
        bk = jnp.zeros((DIM_K,), dtype=jnp.float32)
        Wv = jax.random.normal(ks[5], (DIM_K, DIM_IN), dtype=jnp.float32) * s_in
        bv = jnp.zeros((DIM_K,), dtype=jnp.float32)
        return {'x': x, 'b': b, 'edge_encoding': edge_encoding, 'ptr': ptr, 'Wq': Wq, 'bq': bq, 'Wk': Wk, 'bk': bk, 'Wv': Wv, 'bv': bv}
    _L1_gnn_all = _L1_gnn_setup()
    _L1_gnn_in = {k: v for k, v in _L1_gnn_all.items() if k in ('ptr', 'Wq', 'bq', 'Wk', 'bk', 'Wv', 'bv')}
    del _L1_gnn_all
    return {'x': x, 'adj': adj, 'L0_gnn_W': _L0_gnn_in['W'], 'L0_gnn_b': _L0_gnn_in['b'], 'L1_gnn_ptr': _L1_gnn_in['ptr'], 'L1_gnn_Wq': _L1_gnn_in['Wq'], 'L1_gnn_bq': _L1_gnn_in['bq'], 'L1_gnn_Wk': _L1_gnn_in['Wk'], 'L1_gnn_bk': _L1_gnn_in['bk'], 'L1_gnn_Wv': _L1_gnn_in['Wv'], 'L1_gnn_bv': _L1_gnn_in['bv']}

def reference(x, adj, L0_gnn_W, L0_gnn_b, L1_gnn_ptr, L1_gnn_Wq, L1_gnn_bq, L1_gnn_Wk, L1_gnn_bk, L1_gnn_Wv, L1_gnn_bv):
    import jax
    import jax.numpy as jnp

    def _L0_gnn_ref(input_features, adj, W, b):
        import jax, jax.numpy as jnp
        import numpy as np
        N = 4096
        F_IN = 256
        F_OUT = 256
        DENSITY = 0.01
        A = (adj != 0).astype(input_features.dtype)
        hidden = input_features @ W + b
        deg = jnp.sum(A, axis=0)
        return A @ hidden / deg[:, None]

    def _L1_gnn_ref(x, b, edge_encoding, ptr, Wq, bq, Wk, bk, Wv, bv):
        import jax, jax.numpy as jnp
        import numpy as np
        N = 2048
        DIM_IN = 256
        DIM_Q = 256
        DIM_K = 256
        N_GRAPHS = 32
        n = x.shape[0]
        graph_id = jnp.searchsorted(ptr, jnp.arange(n), side='right') - 1
        mask = graph_id[:, None] == graph_id[None, :]
        query = x @ Wq.T + bq
        key = x @ Wk.T + bk
        value = x @ Wv.T + bv
        scale = 1.0 / jnp.sqrt(jnp.float32(query.shape[-1]))
        a = jnp.where(mask, query @ key.T * scale, 0.0)
        scores = (a + b + edge_encoding) * jnp.where(mask, 1.0, -1000000.0)
        softmax = jax.nn.softmax(scores, axis=-1) * mask
        return softmax @ value
    x = _layernorm(x + _L0_gnn_ref(x, adj, L0_gnn_W, L0_gnn_b), axis=-1)
    x = _layernorm(x + _L1_gnn_ref(x, adj, adj, L1_gnn_ptr, L1_gnn_Wq, L1_gnn_bq, L1_gnn_Wk, L1_gnn_bk, L1_gnn_Wv, L1_gnn_bv), axis=-1)
    return x

_drawn_inputs = setup_inputs


def setup_inputs(seed=0):
    import zlib

    import numpy as np

    out = dict(_drawn_inputs(seed))
    spreads = {'L1_gnn_bq': (0.0, 2.0), 'L1_gnn_bk': (0.0, 2.0), 'L1_gnn_bv': (0.0, 0.1)}
    factors = {'L0_gnn_b': 5.663}
    for name, (base, spread) in spreads.items():
        noise = np.random.default_rng([zlib.crc32(name.encode()), seed]).standard_normal(out[name].shape)
        drawn = base * np.exp(spread * noise) if base else spread * noise
        out[name] = jnp.asarray(drawn.astype(out[name].dtype))
    for name, factor in factors.items():
        out[name] = (out[name] * factor).astype(out[name].dtype)
    return out
```

```python
import concourse.bass as bass
from concourse import mybir
from contextlib import ExitStack


def gnn_then_graph_attention(nc, x, adj, W0, b0, ptr, Wq, bq, Wk, bk, Wv, bv, out):
    F32, F32R, BF16, I32 = mybir.dt.float32, mybir.dt.float32r, mybir.dt.bfloat16, mybir.dt.int32
    ALU, ACT, AX = mybir.AluOpType, mybir.ActivationFunctionType, mybir.AxisListType

    P = 128
    N, F = x.shape
    NPTR = ptr.shape[0]
    KT = F // P
    RT = N // P
    ST = 8
    NS = RT // ST
    CW = 512
    NC = N // CW
    JT = CW // P
    SLOTS = 4
    SCALE = float(F) ** -0.5
    EPS = 1e-5
    MASKED = 1e30
    NEG = -1e6

    adj_chunks = adj.rearrange("(s t p) (c w) -> s c p t w", t=ST, p=P, w=CW)
    x_tiles = x.rearrange("(t p) f -> p t f", p=P)
    out_tiles = out.rearrange("(t p) f -> t p f", p=P)
    adj_rows = adj.rearrange("(t p) j -> t p j", p=P)

    ctx = ExitStack()
    with ctx:
        def sem(name):
            return ctx.enter_context(nc.semaphore(name))

        def tensors(stack):
            return lambda name, shape, dt: stack.enter_context(nc.sbuf_tensor(name, shape, dt))

        sb = tensors(ctx)
        y = sb("y", [P, RT, F], F32)
        ident = sb("ident", [P, P], F32)
        identb = sb("identb", [P, P], BF16)
        degp = sb("degp", [P, RT, NS], F32)
        deg = sb("deg", [P, RT], F32)
        rdeg = sb("rdeg", [P, RT], F32)
        zerob = sb("zerob", [P, CW], BF16)
        ps = ctx.enter_context(nc.psum_tensor("ps", [P, 8, 512], F32))

        layer1 = ExitStack()
        sb1 = tensors(layer1)
        hid = sb1("hid", [P, RT, 2 * F], F32R)
        adjb = sb1("adjb", [P, SLOTS, ST, CW], F32)
        anat = sb1("anat", [P, 2, ST, CW], BF16)
        at = sb1("at", [P, JT, ST * P], F32R)
        layer1.close()
        early = ExitStack()
        sbe = tensors(early)
        hid_ = sbe("hid_", [P, RT, 2 * F], F32R)
        adjb_ = sbe("adjb_", [P, SLOTS, ST, CW], F32)
        xT_hi = sbe("xT_hi", [P, 2, KT, 4 * P], F32R)
        xT_lo = sbe("xT_lo", [P, 2, KT, 4 * P], F32R)
        hsum = sbe("hsum", [P, 4, F], F32)
        w0f = sbe("w0f", [P, KT, F], F32)
        w0_hi = sbe("w0_hi", [P, KT, F], F32R)
        w0_lo = sbe("w0_lo", [P, KT, F], F32R)
        b0b = sbe("b0b", [P, F], F32)
        early.close()

        general = ExitStack()
        sbg = tensors(general)
        xT = sbg("xT", [P, KT, N], F32)
        v = sbg("v", [P, RT, F + 1], F32)
        gid_row = sbg("gid_row", [P, N], F32)
        gid_col = sbg("gid_col", [P, RT], F32)
        adjr = sbg("adjr", [P, N], F32)
        sc = sbg("sc", [P, N], F32)
        pT = sbg("pT", [P, RT, P], F32)
        tT = sbg("tT", [P, KT, P], F32)
        inside = sbg("inside", [P, CW], F32)
        same = sbg("same", [P, CW], F32)
        wqf = sbg("wqf", [P, KT, F], F32)
        wkf = sbg("wkf", [P, KT, F], F32)
        wvf = sbg("wvf", [P, KT, F], F32)
        gmat = sbg("gmat", [P, KT, F], F32)
        wvT = sbg("wvT", [P, KT, F + 1], F32)
        bqc = sbg("bqc", [P, KT], F32)
        bkc = sbg("bkc", [P, KT], F32)
        gvec = sbg("gvec", [P, KT], F32)
        bvb = sbg("bvb", [P, F + 1], F32)
        crow = sbg("crow", [P, RT], F32)
        ptri = sbg("ptri", [64, 1], I32)
        ptrf = sbg("ptrf", [64, 1], F32)
        iota = adjr[0:64, :].bitcast(I32)
        geq = sc[0:64, :]
        ones = sbg("ones", [P, P], F32)
        settled = sbg("settled", [P, 1], F32)
        bkc2 = sbg("bkc2", [P, KT], F32)
        stat = sbg("stat", [P, 16], F32)
        res = sbg("res", [P, F], F32)
        fin = sbg("fin", [P, F], F32)
        bstat = sbg("bstat", [P, 6], F32)
        general.close()

        lnb = ExitStack()
        sbl = tensors(lnb)
        xre = sbl("xre", [P, RT, F], F32)
        bst = sbl("bst", [P, RT, 6], F32)
        lnt = sbl("lnt", [P, 6, RT], F32)
        lnb.close()

        ident_ready = sem("ident_ready")
        identb_ready = sem("identb_ready")
        ident_zeroed = sem("ident_zeroed")
        x_loaded = [sem(f"x_loaded{q}") for q in range(4)]
        w0_loaded = sem("w0_loaded")
        w0_hi_ready = sem("w0_hi_ready")
        w0_split = sem("w0_split")
        xt_done = sem("xt_done")
        xt_hi_ready = sem("xt_hi_ready")
        xt_lo_ready = sem("xt_lo_ready")
        hid_done = sem("hid_done")
        hsum_ready = sem("hsum_ready")
        hid_hi_ready = sem("hid_hi_ready")
        hid_lo_ready = sem("hid_lo_ready")
        slot_loaded = [sem(f"slot_loaded{q}") for q in range(SLOTS)]
        a_ready = sem("a_ready")
        a_used = sem("a_used")
        t_done = sem("t_done")
        at_ready = [sem(f"at_ready{j}") for j in range(JT)]
        mm_done = sem("mm_done")
        acc_free = sem("acc_free")
        y_raw = sem("y_raw")
        y_stats = sem("y_stats")
        xre_loaded = sem("xre_loaded")
        deg_ready = sem("deg_ready")
        ln = sem("ln")
        std_ready = sem("std_ready")
        xn_ready = sem("xn_ready")

        g_loaded = sem("g_loaded")
        g_ones = sem("g_ones")
        g_iota = sem("g_iota")
        g_ptrf = sem("g_ptrf")
        g_geq = sem("g_geq")
        g_bb = sem("g_bb")
        g_wps = sem("g_wps")
        g_wsb = sem("g_wsb")
        g_gid_ps = sem("g_gid_ps")
        g_gid = sem("g_gid")
        g_xt_ps = sem("g_xt_ps")
        g_xt = sem("g_xt")
        g_v_ps = sem("g_v_ps")
        g_v = sem("g_v")
        g_adj = sem("g_adj")
        g_t_ps = sem("g_t_ps")
        g_t = sem("g_t")
        g_s_ps = sem("g_s_ps")
        g_chain = sem("g_chain")
        g_max = sem("g_max")
        g_exp = sem("g_exp")
        g_p = sem("g_p")
        g_pt_ps = sem("g_pt_ps")
        g_pt = sem("g_pt")
        g_o_ps = sem("g_o_ps")
        g_var = sem("g_var")
        g_std = sem("g_std")
        g_fin = sem("g_fin")
        g_stored = sem("g_stored")
        g_out = sem("g_out")

        block = ctx.enter_context(nc.Block())

        def hid_bank(g, q):
            return 4 + 2 * (g % 2) + q // 2, (q % 2) * F

        def column_chunk(s, n):
            if isinstance(s, int) and s >= 2:
                return n
            return (n + 2 * (s & 1)) & (NC - 1)

        @block.sync
        def _(sp):
            sp.dma_start(w0f[:], W0.rearrange("(k p) f -> p k f", p=P)).then_inc(w0_loaded, 16)
            sp.dma_start(b0b[:], b0[None, :].to_broadcast((P, F))).then_inc(w0_loaded, 16)
            for q in range(4):
                sp.dma_start(y[:, ST * q:ST * (q + 1), :], x_tiles[:, ST * q:ST * (q + 1), :]).then_inc(x_loaded[q], 16)
            for s in range(NS):
                for n in range(NC):
                    if NC * s + n >= SLOTS:
                        sp.wait_ge(a_ready, NC * s + n - SLOTS + 1)
                    sp.dma_start(adjb[:, n % SLOTS], adj_chunks[s, column_chunk(s, n)]).then_inc(slot_loaded[n % SLOTS], 16)
            sp.wait_ge(mm_done, JT * NC * NS)
            sp.dma_start(xre[:], x_tiles).then_inc(xre_loaded, 16)

            sp.wait_ge(xn_ready, RT)
            sp.dma_start(wqf[:], Wq.rearrange("(k p) f -> p k f", p=P)).then_inc(g_loaded, 16)
            sp.dma_start(wkf[:], Wk.rearrange("(k p) f -> p k f", p=P)).then_inc(g_loaded, 16)
            sp.dma_start(wvf[:], Wv.rearrange("(k p) f -> p k f", p=P)).then_inc(g_loaded, 16)
            with nc.allow_non_contiguous_dma("two short columns"):
                sp.dma_start(bqc[:], bq.rearrange("(k p) -> p k", p=P)).then_inc(g_loaded, 16)
                sp.dma_start(bkc[:], bk.rearrange("(k p) -> p k", p=P)).then_inc(g_loaded, 16)
            sp.dma_start(bvb[:, 0:F], bv[None, :].to_broadcast((P, F))).then_inc(g_loaded, 16)
            sp.dma_start(ptri[0:NPTR, :], ptr[:, None]).then_inc(g_loaded, 16)
            with sp.Fori(0, RT) as i:
                sp.wait_ge(g_max, i + 1)
                sp.dma_start(adjr[:], adj_rows[i]).then_inc(g_adj, 16)
                sp.wait_ge(g_fin, i + 2)
                sp.dma_start(out_tiles[i], fin[:]).then_inc(g_out, 16)
                sp.wait_ge(g_out, 16 * i + 16)
                sp.sem_inc(g_stored, 1)

        @block.gpsimd
        def _(pool):
            nc.gpsimd.memset(ident[:], 0.0).then_inc(ident_zeroed, 1)
            nc.gpsimd.memset(zerob[:], 0.0).then_inc(ident_zeroed, 1)
            pool.wait_ge(ident_zeroed, 2)
            nc.gpsimd.affine_select(out=ident[:], in_=ident[:], compare_op=ALU.not_equal, fill=1.0, base=0,
                                    pattern=[[-1, P]], channel_multiplier=1).then_inc(ident_ready, 1)
            pool.wait_ge(xn_ready, RT)
            nc.gpsimd.memset(ones[:], 1.0).then_inc(g_ones, 1)
            nc.gpsimd.iota(iota[0:NPTR, :], pattern=[[1, N]], base=0, channel_multiplier=0).then_inc(g_iota, 1)

        @block.tensor
        def _(pe):
            pe.wait_ge(ident_ready, 1)

            def transpose_x(g):
                if g % 2 == 0:
                    pe.wait_ge(x_loaded[g // 2], 16)
                if g >= 2:
                    pe.wait_ge(xt_lo_ready, 2 * (g - 1))
                for k in range(KT):
                    for q in range(4):
                        last = nc.tensor.transpose(ps[:, 2 * (g % 2) + k, q * P:(q + 1) * P],
                                                   y[:, 4 * g + q, k * P:(k + 1) * P], ident[:])
                    last.then_inc(xt_done, 1)

            def hidden(g):
                if g == 0:
                    pe.wait_ge(w0_split, 2)
                pe.wait_ge(xt_lo_ready, 2 * (g + 1))
                if g >= 2:
                    pe.wait_ge(hsum_ready, 4 * (g - 1))
                for q in range(4):
                    bank, col = hid_bank(g, q)
                    passes = [(xT, w, k) for xT, w in ((xT_hi, w0_hi), (xT_hi, w0_lo), (xT_lo, w0_hi)) for k in range(KT)]
                    for i, (xt, w, k) in enumerate(passes):
                        last = nc.tensor.matmul(ps[:, bank, col:col + F], xt[:, g % 2, k, q * P:(q + 1) * P], w[:, k, :],
                                                start=(i == 0), stop=(i == len(passes) - 1))
                    last.then_inc(hid_done, 1)

            transpose_x(0)
            for g in range(RT // 4):
                if g + 1 < RT // 4:
                    transpose_x(g + 1)
                hidden(g)

            pe.wait_ge(identb_ready, 1)
            pe.wait_ge(hsum_ready, RT)
            pe.wait_ge(hid_lo_ready, RT)

            def transposes(k, par, j):
                pe.wait_ge(a_ready, k + 1)
                for t in range(ST):
                    last = nc.tensor.transpose(ps[:, 4 + j, :].bitcast(BF16)[:, t * P:(t + 1) * P],
                                               anat[:, par, t, j * P:(j + 1) * P], identb[:])
                last.then_inc(t_done, 1)

            def products(k, c, j):
                pe.wait_ge(at_ready[j], k + 1)
                for t in range(ST):
                    for half in range(2):
                        last = nc.tensor.matmul(ps[:, t // 2, (t % 2) * F:(t % 2 + 1) * F],
                                                at[:, j, t * P:(t + 1) * P],
                                                hid[:, JT * c + j, half * F:(half + 1) * F],
                                                start=False, stop=False, skip_group_check=True)
                last.then_inc(mm_done, 1)

            def clear_sums():
                for b in range(4):
                    nc.tensor.matmul(ps[:, b, :], identb[:], zerob[:], start=True, stop=True, skip_group_check=True)

            def chunk(s, n, par, ahead=True):
                for j in range(JT):
                    products(NC * s + n, column_chunk(s, n), j)
                    if ahead:
                        transposes(NC * s + n + 1, 1 - par, j)

            for j in range(JT):
                transposes(0, 0, j)
            clear_sums()
            with pe.Fori(0, NS - 1) as s:
                with pe.Fori(0, NC, 2) as n:
                    chunk(s, n, 0)
                    chunk(s, n + 1, 1)
                pe.wait_ge(acc_free, 4 * (s + 1))
                clear_sums()
            with pe.Fori(0, NC - 2, 2) as n:
                chunk(NS - 1, n, 0)
                chunk(NS - 1, n + 1, 1)
            chunk(NS - 1, NC - 2, 0)
            chunk(NS - 1, NC - 1, 1, ahead=False)

            pe.wait_ge(xn_ready, RT)
            pe.wait_ge(g_loaded, 16 * 7)
            pe.wait_ge(g_ones, 1)
            pe.wait_ge(g_bb, 1)
            pe.wait_ge(acc_free, 4 * NS)
            for m in range(KT):
                for k in range(KT):
                    nc.tensor.matmul(ps[:, m, 0:F], wqf[:, k, m * P:(m + 1) * P], wkf[:, k, :],
                                     start=(k == 0), stop=(k == KT - 1))
                for k in range(KT):
                    nc.tensor.transpose(ps[:, 2 + m, k * P:(k + 1) * P], wvf[:, k, m * P:(m + 1) * P], ident[:])
                for col, w, b in ((m, wkf, bqc), (2 + m, wqf, bkc)):
                    for k in range(KT):
                        nc.tensor.matmul(ps[:, 4, col:col + 1], w[:, k, m * P:(m + 1) * P], b[:, k:k + 1],
                                         start=(k == 0), stop=(k == KT - 1))
            for k in range(KT):
                last = nc.tensor.matmul(ps[:, 4, 4:5], ones[:], bkc2[:, k:k + 1], start=(k == 0), stop=(k == KT - 1))
            last.then_inc(g_wps, 1)
            pe.wait_ge(g_geq, 1)
            for t in range(RT):
                last = nc.tensor.matmul(ps[:, 5, t:t + 1], geq[0:NPTR, t * P:(t + 1) * P], ones[0:NPTR, 0:1],
                                        start=True, stop=True)
            last.then_inc(g_gid_ps, 1)
            for c in range(NC):
                pe.wait_ge(g_gid, c + 1)
                nc.tensor.matmul(ps[:, 6, :], ones[0:NPTR, :], geq[0:NPTR, c * CW:(c + 1) * CW],
                                 start=True, stop=True).then_inc(g_gid_ps, 1)
            for g in range(RT // 4):
                for k in range(KT):
                    if g >= 1:
                        pe.wait_ge(g_xt, 2 * (g - 1) + k + 1)
                    else:
                        pe.wait_ge(g_wsb, 1)
                    for q in range(4):
                        last = nc.tensor.transpose(ps[:, k, q * P:(q + 1) * P], y[:, 4 * g + q, k * P:(k + 1) * P], ident[:])
                    last.then_inc(g_xt_ps, 1)
            pe.wait_ge(g_xt, 2 * (RT // 4))
            for t in range(RT):
                if t >= 2:
                    pe.wait_ge(g_v, t - 1)
                for k in range(KT):
                    last = nc.tensor.matmul(ps[:, 2 + t % 2, 0:F + 1], xT[:, k, t * P:(t + 1) * P], wvT[:, k, :],
                                            start=(k == 0), stop=(k == KT - 1))
                last.then_inc(g_v_ps, 1)
            pe.wait_ge(g_v, RT)
            with pe.Fori(0, RT) as i:
                pe.wait_ge(g_fin, i + 1)
                for m in range(KT):
                    for k in range(KT):
                        last = nc.tensor.matmul(ps[:, 0, m * P:(m + 1) * P], gmat[:, k, m * P:(m + 1) * P],
                                                xT[:, k, bass.ts(i, P)], start=(k == 0), stop=(k == KT - 1))
                last.then_inc(g_t_ps, 1)
                pe.wait_ge(g_t, i + 1)
                for c in range(NC):
                    for k in range(KT):
                        last = nc.tensor.matmul(ps[:, c, :], tT[:, k, :], xT[:, k, c * CW:(c + 1) * CW],
                                                start=(k == 0), stop=(k == KT - 1))
                    last.then_inc(g_s_ps, 1)
                pe.wait_ge(g_p, i + 1)
                for c in range(NC):
                    for q in range(JT):
                        j = JT * c + q
                        last = nc.tensor.transpose(ps[:, c, q * P:(q + 1) * P], sc[:, j * P:(j + 1) * P], ident[:])
                    last.then_inc(g_pt_ps, 1)
                pe.wait_ge(g_pt, NC * i + NC)
                for j in range(RT):
                    last = nc.tensor.matmul(ps[:, 0, 0:F], pT[:, j, :], v[:, j, 0:F], start=(j == 0), stop=(j == RT - 1))
                last.then_inc(g_o_ps, 1)

        @block.scalar
        def _(act):
            act.wait_ge(w0_loaded, 32)
            nc.scalar.copy(w0_hi[:], w0f[:]).then_inc(w0_split, 1)
            act.wait_ge(ident_ready, 1)
            nc.scalar.copy(identb[:], ident[:]).then_inc(identb_ready, 1)

            def xt_hi(g):
                for k in range(KT):
                    act.wait_ge(xt_done, 2 * g + k + 1)
                    if g >= 2:
                        act.wait_ge(hid_done, 4 * (g - 1))
                    nc.scalar.copy(xT_hi[:, g % 2, k, :], ps[:, 2 * (g % 2) + k, :]).then_inc(xt_hi_ready, 1)

            xt_hi(0)
            for g in range(RT // 4):
                if g + 1 < RT // 4:
                    xt_hi(g + 1)
                for q in range(4):
                    t = 4 * g + q
                    act.wait_ge(hsum_ready, t + 1)
                    nc.scalar.copy(hid[:, t, 0:F], hsum[:, q, :]).then_inc(hid_hi_ready, 1)

            def evacuate(s, n, j):
                k = NC * s + n
                act.wait_ge(t_done, JT * k + j + 1)
                if not (isinstance(k, int) and k == 0):
                    act.wait_ge(mm_done, JT * (k - 1) + j + 1)
                c = column_chunk(s, n)
                nc.scalar.activation(at[:, j, :], ps[:, 4 + j, :].bitcast(BF16), ACT.Copy,
                                     accum_out=degp[:, JT * c + j, s:s + 1]).then_inc(at_ready[j], 1)

            def take_sums(s):
                act.wait_ge(mm_done, JT * NC * (s + 1))
                for b in (0, 2):
                    nc.scalar.copy(y[:, ST * s + 2 * b:ST * s + 2 * b + 2, :],
                                   ps[:, b, :].rearrange("p (t f) -> p t f", f=F)).then_inc(acc_free, 1)

            act.wait_ge(hid_done, RT)
            for s in range(NS):
                for n in range(NC):
                    for j in range(JT - 1):
                        evacuate(s, n, j)
                    if s >= 1 and n == 0:
                        take_sums(s - 1)
            take_sums(NS - 1)

            act.wait_ge(ln, 3)
            nc.scalar.activation(lnt[:, 3, :], lnt[:, 2, :], ACT.Sqrt).then_inc(std_ready, 1)

            act.wait_ge(g_wps, 1)
            for m in range(KT):
                act.wait_ge(xn_ready, RT)
                nc.scalar.mul(gmat[:, m, :], ps[:, m, 0:F], SCALE)
                nc.scalar.copy(wvT[:, m, 0:F], ps[:, 2 + m, 0:F])
            nc.scalar.mul(gvec[:], ps[:, 4, 0:KT], SCALE)
            nc.scalar.mul(wvT[:, :, F], ps[:, 4, 2:2 + KT], SCALE)
            nc.scalar.mul(bvb[:, F:F + 1], ps[:, 4, 4:5], SCALE).then_inc(g_wsb, 1)
            for g in range(RT // 4):
                for k in range(KT):
                    act.wait_ge(g_xt_ps, 2 * g + k + 1)
                    nc.scalar.copy(xT[:, k, g * CW:(g + 1) * CW], ps[:, k, :]).then_inc(g_xt, 1)
            with act.Fori(0, RT) as i:
                act.wait_ge(g_t_ps, i + 1)
                for m in range(KT):
                    last = nc.scalar.activation(tT[:, m, :], ps[:, 0, m * P:(m + 1) * P], ACT.Identity, bias=gvec[:, m:m + 1])
                last.then_inc(g_t, 1)
                act.wait_ge(g_max, i + 2)
                nc.scalar.activation(sc[:], sc[:], ACT.Exp, bias=stat[:, 0:1], accum_out=stat[:, 1:2]).then_inc(g_exp, 1)
                for c in range(NC):
                    act.wait_ge(g_pt_ps, NC * i + c + 1)
                    nc.scalar.copy(pT[:, JT * c:JT * (c + 1), :], ps[:, c, :].rearrange("p (t w) -> p t w", w=P)).then_inc(g_pt, 1)
                act.wait_ge(g_var, i + 1)
                nc.scalar.activation(stat[:, 5:6], stat[:, 4:5], ACT.Sqrt).then_inc(g_std, 1)

        @block.vector
        def _(dve):
            dve.wait_ge(w0_split, 1)
            nc.vector.tensor_tensor(w0_lo[:], w0f[:], w0_hi[:].bitcast(F32), ALU.subtract).then_inc(w0_split, 1)

            def xt_lo(g):
                for k in range(KT):
                    dve.wait_ge(xt_hi_ready, 2 * g + k + 1)
                    if g >= 2:
                        dve.wait_ge(hid_done, 4 * (g - 1))
                    nc.vector.tensor_tensor(xT_lo[:, g % 2, k, :], ps[:, 2 * (g % 2) + k, :],
                                            xT_hi[:, g % 2, k, :].bitcast(F32), ALU.subtract).then_inc(xt_lo_ready, 1)

            xt_lo(0)
            for g in range(RT // 4):
                if g + 1 < RT // 4:
                    xt_lo(g + 1)
                for q in range(4):
                    t = 4 * g + q
                    bank, col = hid_bank(g, q)
                    dve.wait_ge(hid_done, 4 * g + q // 2 * 2 + 2)
                    if g >= 1:
                        dve.wait_ge(hid_lo_ready, t - 3)
                    last = nc.vector.tensor_tensor(hsum[:, q, :], ps[:, bank, col:col + F], b0b[:], ALU.add)
                    last.then_inc(hsum_ready, 1)
                for q in range(4):
                    t = 4 * g + q
                    dve.wait_ge(hid_hi_ready, t + 1)
                    nc.vector.tensor_tensor(hid[:, t, F:2 * F], hsum[:, q, :], hid[:, t, 0:F].bitcast(F32),
                                            ALU.subtract).then_inc(hid_lo_ready, 1)

            def make_a(s, n):
                k = NC * s + n
                dve.wait_ge(slot_loaded[n % SLOTS], 16 * (k // SLOTS + 1))
                if k >= 2:
                    dve.wait_ge(t_done, JT * (k - 1))
                nc.vector.tensor_scalar(anat[:, n % 2], adjb[:, n % SLOTS], 0.0, None, ALU.not_equal).then_inc(a_ready, 1)

            def evacuate(s, n):
                k, j = NC * s + n, JT - 1
                dve.wait_ge(t_done, JT * k + j + 1)
                if k >= 1:
                    dve.wait_ge(mm_done, JT * (k - 1) + j + 1)
                c = column_chunk(s, n)
                nc.vector.tensor_scalar(at[:, j, :], ps[:, 4 + j, :].bitcast(BF16), 1.0, None, ALU.mult, ALU.add,
                                        accum_out=degp[:, JT * c + j, s:s + 1]).then_inc(at_ready[j], 1)

            def take_sums(s):
                dve.wait_ge(mm_done, JT * NC * (s + 1))
                for b in (1, 3):
                    nc.vector.tensor_copy(y[:, ST * s + 2 * b:ST * s + 2 * b + 2, :],
                                          ps[:, b, :].rearrange("p (t f) -> p t f", f=F)).then_inc(acc_free, 1)

            dve.wait_ge(hid_done, RT)
            for s in range(NS):
                for n in range(NC):
                    k = NC * s + n
                    if k >= 2:
                        evacuate((k - 2) // NC, (k - 2) % NC)
                    if s >= 1 and n == 2:
                        take_sums(s - 1)
                    make_a(s, n)
            evacuate(NS - 1, NC - 2)
            evacuate(NS - 1, NC - 1)
            take_sums(NS - 1)

            for j in range(JT):
                dve.wait_ge(at_ready[j], NC * NS)
            dve.wait_ge(acc_free, 4 * NS)
            nc.vector.reduce_sum(deg[:], degp[:], AX.X).then_inc(deg_ready, 1)
            dve.wait_ge(deg_ready, 1)
            nc.vector.reciprocal(rdeg[:], deg[:]).then_inc(deg_ready, 1)
            dve.wait_ge(deg_ready, 2)
            dve.wait_ge(xre_loaded, 16)
            with dve.Fori(0, RT) as t:
                nc.vector.scalar_tensor_tensor(y[:, t, :], y[:, t, :], rdeg[:, bass.ds(t, 1)], xre[:, t, :],
                                               ALU.mult, ALU.add).then_inc(y_raw, 1)
                dve.wait_ge(y_raw, t + 1)
                nc.vector.bn_stats(bst[:, t, :], y[:, t, :]).then_inc(y_stats, 1)
            dve.wait_ge(y_stats, RT)
            d, m2, var, sd, mean, rs = (lnt[:, q, :] for q in range(6))
            nc.vector.tensor_tensor(d, bst[:, :, 1], bst[:, :, 4], ALU.subtract)
            nc.vector.tensor_tensor(m2, bst[:, :, 2], bst[:, :, 5], ALU.add)
            nc.vector.tensor_tensor(mean, bst[:, :, 1], bst[:, :, 4], ALU.add).then_inc(ln, 1)
            dve.wait_ge(ln, 1)
            nc.vector.tensor_scalar(m2, m2, 1.0 / F, EPS, ALU.mult, ALU.add)
            nc.vector.tensor_scalar(mean, mean, 0.5, None, ALU.mult)
            nc.vector.scalar_tensor_tensor(d, d, 0.25, d, ALU.mult, ALU.mult).then_inc(ln, 1)
            dve.wait_ge(ln, 2)
            nc.vector.tensor_tensor(var, d, m2, ALU.add).then_inc(ln, 1)
            dve.wait_ge(std_ready, 1)
            nc.vector.reciprocal(rs, sd).then_inc(ln, 1)
            dve.wait_ge(ln, 4)
            nc.vector.tensor_tensor(rs, rs, var, ALU.mult).then_inc(ln, 1)
            dve.wait_ge(ln, 5)
            nc.vector.tensor_tensor(rs, rs, sd, ALU.add).then_inc(ln, 1)
            dve.wait_ge(ln, 6)
            nc.vector.tensor_scalar(rs, rs, 0.5, None, ALU.mult).then_inc(ln, 1)
            dve.wait_ge(ln, 7)
            nc.vector.reciprocal(rs, rs).then_inc(ln, 1)
            dve.wait_ge(ln, 8)
            with dve.Fori(0, RT) as t:
                nc.vector.tensor_scalar(y[:, t, :], y[:, t, :], lnt[:, 4, bass.ds(t, 1)], lnt[:, 5, bass.ds(t, 1)],
                                        ALU.subtract, ALU.mult).then_inc(xn_ready, 1)

            dve.wait_ge(g_loaded, 16 * 7)
            dve.wait_ge(xn_ready, RT)
            nc.vector.tensor_tensor(bkc2[:], bqc[:], bkc[:], ALU.mult).then_inc(g_bb, 1)
            nc.vector.tensor_copy(ptrf[0:NPTR, :], ptri[0:NPTR, :]).then_inc(g_ptrf, 1)
            dve.wait_ge(g_ptrf, 1)
            dve.wait_ge(g_iota, 1)
            nc.vector.tensor_scalar(geq[0:NPTR, :], iota[0:NPTR, :], ptrf[0:NPTR, 0:1], None, ALU.is_ge).then_inc(g_geq, 1)
            dve.wait_ge(g_gid_ps, 1)
            nc.vector.tensor_copy(gid_col[:], ps[:, 5, 0:RT]).then_inc(g_gid, 1)
            for c in range(NC):
                dve.wait_ge(g_gid_ps, c + 2)
                nc.vector.tensor_copy(gid_row[:, c * CW:(c + 1) * CW], ps[:, 6, :]).then_inc(g_gid, 1)
            dve.wait_ge(g_wsb, 1)
            for t in range(RT):
                dve.wait_ge(g_v_ps, t + 1)
                nc.vector.tensor_tensor(v[:, t, :], ps[:, 2 + t % 2, 0:F + 1], bvb[:], ALU.add).then_inc(g_v, 1)
            dve.wait_ge(g_gid, NC + 1)
            dve.wait_ge(g_v, RT)
            nc.vector.tensor_copy(crow[:], v[:, :, F]).then_inc(g_chain, 1)
            dve.wait_ge(g_chain, 1)
            nc.vector.memset(stat[:], 0.0).then_inc(g_max, 1)
            nc.vector.memset(fin[:], 0.0).then_inc(g_fin, 1)
            LINKS = 3 * NC + 8
            with dve.Fori(0, RT) as i:
                links = [0]

                def link(ins):
                    links[0] += 1
                    ins.then_inc(g_chain, 1)
                    dve.wait_ge(g_chain, i * LINKS + (links[0] + 1))

                gid_i, c_i = gid_col[:, bass.ds(i, 1)], crow[:, bass.ds(i, 1)]
                dve.wait_ge(g_adj, 16 * i + 16)
                for c in range(NC):
                    cols = slice(c * CW, (c + 1) * CW)
                    dve.wait_ge(g_s_ps, NC * i + c + 1)
                    link(nc.vector.scalar_tensor_tensor(inside[:], ps[:, c, :], c_i, adjr[:, cols], ALU.add, ALU.add))
                    nc.vector.tensor_scalar(sc[:, cols], adjr[:, cols], 2 * NEG, None, ALU.mult)
                    nc.vector.tensor_scalar(same[:], gid_row[:, cols], gid_i, None, ALU.is_equal)
                    link(nc.vector.tensor_tensor(inside[:], inside[:], adjr[:, cols], ALU.add))
                    nc.vector.memset(settled[:], 0.0)
                    link(nc.vector.copy_predicated(sc[:, cols], same[:].bitcast(I32), inside[:]))
                nc.vector.tensor_reduce(stat[:, 0:1], sc[:], AX.X, ALU.max, negate=True).then_inc(g_max, 1)
                dve.wait_ge(g_exp, i + 1)
                nc.vector.scalar_tensor_tensor(sc[:], gid_row[:], gid_i, sc[:], ALU.is_equal, ALU.mult).then_inc(g_p, 1)
                link(nc.vector.reciprocal(stat[:, 3:4], stat[:, 1:2]))
                dve.wait_ge(g_o_ps, i + 1)
                link(nc.vector.scalar_tensor_tensor(res[:], ps[:, 0, 0:F], stat[:, 3:4], y[:, i, :], ALU.mult, ALU.add))
                link(nc.vector.bn_stats(bstat[:], res[:]))
                nc.vector.memset(settled[:], 0.0)
                link(nc.vector.bn_aggr(stat[:, 6:8], bstat[:]))
                nc.vector.tensor_scalar(stat[:, 4:5], stat[:, 7:8], EPS, None, ALU.add).then_inc(g_var, 1)
                dve.wait_ge(g_std, i + 1)
                link(nc.vector.reciprocal(stat[:, 9:10], stat[:, 5:6]))
                link(nc.vector.scalar_tensor_tensor(stat[:, 9:10], stat[:, 9:10], stat[:, 4:5], stat[:, 5:6], ALU.mult, ALU.add))
                link(nc.vector.tensor_scalar(stat[:, 9:10], stat[:, 9:10], 0.5, None, ALU.mult))
                link(nc.vector.reciprocal(stat[:, 10:11], stat[:, 9:10]))
                nc.vector.tensor_scalar(fin[:], res[:], stat[:, 6:7], stat[:, 10:11], ALU.subtract, ALU.mult).then_inc(g_fin, 1)
                assert links[0] == LINKS, links


def kernel(x, adj, L0_gnn_W, L0_gnn_b, L1_gnn_ptr, L1_gnn_Wq, L1_gnn_bq, L1_gnn_Wk, L1_gnn_bk, L1_gnn_Wv, L1_gnn_bv):
    import numpy as np
    import concourse.bacc as bacc
    from concourse.bass_utils import run_bass_kernel_spmd

    nc = bacc.Bacc("TRN2", target_bir_lowering=False, num_devices=1)
    arrays, args = {}, []
    for name, a in dict(x=x, adj=adj, W0=L0_gnn_W, b0=L0_gnn_b, ptr=L1_gnn_ptr, Wq=L1_gnn_Wq, bq=L1_gnn_bq,
                        Wk=L1_gnn_Wk, bk=L1_gnn_bk, Wv=L1_gnn_Wv, bv=L1_gnn_bv).items():
        a = np.ascontiguousarray(a)
        arrays[f"in_{name}"] = a
        args.append(nc.dram_tensor(f"in_{name}", a.shape, mybir.dt.from_np(a.dtype), kind="ExternalInput").ap())
    out = nc.dram_tensor("out", tuple(x.shape), mybir.dt.float32, kind="ExternalOutput").ap()
    gnn_then_graph_attention(nc, *args, out)
    r = run_bass_kernel_spmd(nc, [arrays], core_ids=[0])
    return r.results[0]["out"]
```

```python
import concourse.bass as bass
from concourse import mybir
from contextlib import ExitStack


def gnn_then_graph_attention(nc, x, adj, W0, b0, ptr, Wq, bq, Wk, bk, Wv, bv, out):
    F32, F32R, BF16, I32 = mybir.dt.float32, mybir.dt.float32r, mybir.dt.bfloat16, mybir.dt.int32
    ALU, ACT, AX = mybir.AluOpType, mybir.ActivationFunctionType, mybir.AxisListType

    P = 128
    N, F = x.shape
    NPTR = ptr.shape[0]
    GRAPH = 2048 // (NPTR - 1)
    KT = F // P
    RT = N // P
    ST = 8
    NS = RT // ST
    CW = 512
    NC = N // CW
    JT = CW // P
    SLOTS = 4
    DT = (NPTR - 1) * GRAPH // P
    DN = N - DT * P
    DC = DN // CW
    PAIRS = DT // 2
    assert DT == RT // 2 and 2 * GRAPH == P
    SCALE = float(F) ** -0.5
    EPS = 1e-5
    OUTSIDE = 1e30
    NEG = -1e6
    BLOCKS = (2, 3, 0, 1)

    adj_chunks = adj.rearrange("(s t p) (c w) -> s c p t w", t=ST, p=P, w=CW)
    x_tiles = x.rearrange("(t p) f -> p t f", p=P)
    out_tiles = out.rearrange("(t p) f -> t p f", p=P)
    out_pairs = out.rearrange("(m e p) f -> m p e f", e=2, p=P)
    adj_rows = adj.rearrange("(t p) j -> t p j", p=P)
    adj_blocks = adj.rearrange("(t p) (u q) -> t u p q", p=P, q=P)

    def column_chunk(s, n):
        return (n + (2 if isinstance(s, int) and BLOCKS[s] == 1 else 0)) & (NC - 1)

    def has_outside(s, n):
        return BLOCKS[s] < 2 or n < NC - DC

    def outside_count(s, n):
        return sum(has_outside(a, b) for a in range(NS) for b in range(NC) if (a, b) <= (s, n))

    ctx = ExitStack()
    with ctx:
        def sem(name):
            return ctx.enter_context(nc.semaphore(name))

        def tensors(stack):
            return lambda name, shape, dt: stack.enter_context(nc.sbuf_tensor(name, shape, dt))

        sb = tensors(ctx)
        y = sb("y", [P, RT, F], F32)
        ident = sb("ident", [P, P], F32)
        identb = sb("identb", [P, P], BF16)
        zerob = sb("zerob", [P, CW], BF16)
        degp = sb("degp", [P, RT, NS], F32)
        deg = sb("deg", [P, RT], F32)
        rdeg = sb("rdeg", [P, RT], F32)
        least = sb("least", [P, RT, NC], F32)
        zpart = sb("zpart", [P, RT, NC], F32)
        ebias = sb("ebias", [P, SLOTS, ST], F32)
        g_hi = sb("g_hi", [P, KT, F], F32R)
        g_lo = sb("g_lo", [P, KT, F], F32R)
        wv_hi = sb("wv_hi", [P, KT, F + 2], F32R)
        wv_lo = sb("wv_lo", [P, KT, F + 2], F32R)
        gv = sb("gv", [P, KT], F32)
        bqbk = sb("bqbk", [P, 1], F32)
        bvs = sb("bvs", [P, F], F32)
        bn = sb("bn", [P, 16 + 2 + 4, 6], F32)
        tiny = sb("tiny", [P, 128], F32)
        rowc = sb("rowc", [P, 128], F32)
        consts = sb("consts", [P, 5, 4], F32)
        settled = sb("settled", [P, 4], F32)
        irregular = sb("irregular", [1, 1], I32)
        ps = ctx.enter_context(nc.psum_tensor("ps", [P, 8, 512], F32))

        layer1 = ExitStack()
        sb1 = tensors(layer1)
        hid = sb1("hid", [P, RT, 2 * F], F32R)
        adjb = sb1("adjb", [P, SLOTS, ST, CW], F32)
        anat = sb1("anat", [P, 2, ST, CW], BF16)
        at = sb1("at", [P, JT, ST * P], F32R)
        layer1.close()
        early = ExitStack()
        sbe = tensors(early)
        sbe("hid_", [P, RT, 2 * F], F32R)
        sbe("adjb_", [P, SLOTS, ST, CW], F32)
        sbe("anat_", [P, ST, CW], BF16)
        hsum = sbe("hsum", [P, 4, F], F32)
        w0_hi = sbe("w0_hi", [P, KT, F], F32R)
        w0_lo = sbe("w0_lo", [P, KT, F], F32R)
        xT_hi = sbe("xT_hi", [P, 2, KT, 4 * P], F32R)
        xT_lo = sbe("xT_lo", [P, 2, KT, 4 * P], F32R)
        early.close()
        wq_in, wk_in, wv_in = (adjb[:, 3, q, :].rearrange("p (k f) -> p k f", k=KT) for q in range(3))
        vecs = adjb[:, 3, 3, :]
        bq_in, bk_in, bb_in = vecs[:, 0:2], vecs[:, 2:4], vecs[:, 4:6]
        ptr_f, ptr_d = vecs[0:NPTR, 6:7], vecs[0:NPTR, 7:8]
        ptr_in, ptr_want = vecs[0:NPTR, 8:9].bitcast(I32), vecs[0:NPTR, 9:10].bitcast(I32)
        ones_in = adjb[:, 3, 4, 0:P]
        wcols = adjb[:, 3, 5, 0:8]
        b0b = adjb[:, 3, 6, 0:F]
        w0f = adjb[:, 3, 7, :].rearrange("p (k f) -> p k f", k=KT)

        regular = ExitStack()
        sbr = tensors(regular)
        xd_hi = sbr("xd_hi", [P, KT, DN], F32R)
        xd_lo = sbr("xd_lo", [P, KT, DN], F32R)
        vd = sbr("vd", [P, DN // P, 2 * F], F32R)
        td_hi = sbr("td_hi", [P, KT, 2 * P], F32R)
        td_lo = sbr("td_lo", [P, KT, 2 * P], F32R)
        res = sbr("res", [P, 4, F], F32)
        fin = sbr("fin", [P, 4, F], F32)
        ts_hi = sbr("ts_hi", [P, KT, 2 * P], F32R)
        ts_lo = sbr("ts_lo", [P, KT, 2 * P], F32R)
        xs_again = sbr("xs_again", [P, DT, F], F32)
        adjd = sbr("adjd", [P, 2, DN], F32)
        ptd_hi = sbr("ptd_hi", [P, 2, CW], F32R)
        ptd_lo = sbr("ptd_lo", [P, 2, CW], F32R)
        sadj = sbr("sadj", [P, 2, P], F32)
        sadjm = sbr("sadjm", [P, 2, P], F32)
        cross = sbr("cross", [P, 2, P], F32)
        xs = sbr("xs", [P, 2, F], F32)
        regular_fill = sbr("regular_fill", [P, 2 * ST * CW - 2 * DN - 4 * CW - 6 * P - 2 * F], F32)
        xst_hi = sbr("xst_hi", [P, KT, 2 * P], F32R)
        xst_lo = sbr("xst_lo", [P, KT, 2 * P], F32R)
        vs_hi = sbr("vs_hi", [P, 2, F], F32R)
        vs_lo = sbr("vs_lo", [P, 2, F], F32R)
        sp_ = sbr("sp_", [P, 2, P], F32)
        pts_hi = sbr("pts_hi", [P, 2 * P], F32R)
        pts_lo = sbr("pts_lo", [P, 2 * P], F32R)
        rs = sbr("rs", [P, 2, F], F32)
        a_fill = sbr("a_fill", [P, 4096 - 4 * KT * P - 4 * F - 2 * P - 4 * P - 2 * F], F32)
        scd = sbr("scd", [P, 2, DN], F32)
        regular.close()
        again = adjb[:, 0, :, :].rearrange("p t w -> p (t w)").rearrange("p (t f) -> p t f", f=F)

        general = ExitStack()
        sbg = tensors(general)
        xT = sbg("xT", [P, KT, N], F32)
        v = sbg("v", [P, RT, F + 1], F32)
        gid_row = sbg("gid_row", [P, N], F32)
        gid_col = sbg("gid_col", [P, RT], F32)
        adjr = sbg("adjr", [P, N], F32)
        sc = sbg("sc", [P, N], F32)
        pT = sbg("pT", [P, RT, P], F32)
        tT = sbg("tT", [P, KT, P], F32)
        inside = sbg("inside", [P, CW], F32)
        same = sbg("same", [P, CW], F32)
        wqf = sbg("wqf", [P, KT, F], F32)
        wkf = sbg("wkf", [P, KT, F], F32)
        wvf = sbg("wvf", [P, KT, F], F32)
        gmat = sbg("gmat", [P, KT, F], F32)
        wvT = sbg("wvT", [P, KT, F + 1], F32)
        bqc = sbg("bqc", [P, KT], F32)
        bkc = sbg("bkc", [P, KT], F32)
        gvec = sbg("gvec", [P, KT], F32)
        gbv = sbg("bvb", [P, F + 1], F32)
        crow = sbg("crow", [P, RT], F32)
        ptri = sbg("ptri", [64, 1], I32)
        ptrf = sbg("ptrf", [64, 1], F32)
        iota = adjr[0:64, :].bitcast(I32)
        geq = sc[0:64, :]
        ones = sbg("ones", [P, P], F32)
        gsettled = sbg("gsettled", [P, 1], F32)
        bkc2 = sbg("bkc2", [P, KT], F32)
        stat = sbg("stat", [P, 16], F32)
        gres = sbg("gres", [P, F], F32)
        gfin = sbg("gfin", [P, F], F32)
        bstat = sbg("bstat", [P, 6], F32)
        general.close()

        lnb = ExitStack()
        sbl = tensors(lnb)
        xre = sbl("xre", [P, RT, F], F32)
        bst = sbl("bst", [P, RT, 6], F32)
        lnt = sbl("lnt", [P, 6, RT], F32)
        lnb.close()

        ident_ready = sem("ident_ready")
        identb_ready = sem("identb_ready")
        ident_zeroed = sem("ident_zeroed")
        x_loaded = [sem(f"x_loaded{q}") for q in range(4)]
        w0_loaded = sem("w0_loaded")
        w0_hi_ready = sem("w0_hi_ready")
        w0_split = sem("w0_split")
        xt_done = sem("xt_done")
        xt_hi_ready = sem("xt_hi_ready")
        xt_lo_ready = sem("xt_lo_ready")
        hid_done = sem("hid_done")
        hsum_ready = sem("hsum_ready")
        hid_hi_ready = sem("hid_hi_ready")
        hid_lo_ready = sem("hid_lo_ready")
        slot_loaded = [sem(f"slot_loaded{q}") for q in range(SLOTS)]
        a_ready = sem("a_ready")
        a_used = sem("a_used")
        t_done = sem("t_done")
        at_ready = [sem(f"at_ready{j}") for j in range(JT)]
        mm_done = sem("mm_done")
        acc_free = sem("acc_free")
        y_raw = sem("y_raw")
        y_stats = sem("y_stats")
        xre_loaded = sem("xre_loaded")
        deg_ready = sem("deg_ready")
        ln = sem("ln")
        std_ready = sem("std_ready")
        xn_ready = sem("xn_ready")

        g_loaded = sem("g_loaded")
        g_ones = sem("g_ones")
        g_iota = sem("g_iota")
        g_ptrf = sem("g_ptrf")
        g_geq = sem("g_geq")
        g_bb = sem("g_bb")
        g_wps = sem("g_wps")
        g_wsb = sem("g_wsb")
        g_gid_ps = sem("g_gid_ps")
        g_gid = sem("g_gid")
        g_xt_ps = sem("g_xt_ps")
        g_xt = sem("g_xt")
        g_v_ps = sem("g_v_ps")
        g_v = sem("g_v")
        g_adj = sem("g_adj")
        g_t_ps = sem("g_t_ps")
        g_t = sem("g_t")
        g_s_ps = sem("g_s_ps")
        g_chain = sem("g_chain")
        g_max = sem("g_max")
        g_exp = sem("g_exp")
        g_p = sem("g_p")
        g_pt_ps = sem("g_pt_ps")
        g_pt = sem("g_pt")
        g_o_ps = sem("g_o_ps")
        g_var = sem("g_var")
        g_std = sem("g_std")
        g_fin = sem("g_fin")
        g_stored = sem("g_stored")
        g_out = sem("g_out")

        weights_loaded = sem("weights_loaded")
        ones_ready = sem("ones_ready")
        weights_sums = sem("weights_sums")
        weights_products = sem("weights_products")
        weights_hi = sem("weights_hi")
        weights_split = sem("weights_split")
        ptr_step = sem("ptr_step")
        ptr_far = sem("ptr_far")
        branch_ready = sem("branch_ready")
        outside_cleared = sem("outside_cleared")
        masked = sem("masked")
        least_ready = sem("least_ready")
        ebias_ready = sem("ebias_ready")
        outside_done = sem("outside_done")

        again_loaded = sem("again_loaded")
        small_again_loaded = sem("small_again_loaded")
        consts_ready = sem("consts_ready")
        cross_ready = sem("cross_ready")
        d_res = sem("d_res")
        d_bn = sem("d_bn")
        pool_step = sem("pool_step")
        d_rstd = sem("d_rstd")
        d_x_first = sem("d_x_first")
        d_x = sem("d_x")
        small_deg_ready = sem("small_deg_ready")
        xd_ps = sem("xd_ps")
        xd_hi_ready = sem("xd_hi_ready")
        xd_lo_ready = sem("xd_lo_ready")
        vd_ps = sem("vd_ps")
        vd_hi_ready = sem("vd_hi_ready")
        vd_lo_ready = sem("vd_lo_ready")
        vd_free = sem("vd_free")
        mout_step = sem("mout_step")
        mout_exp = sem("mout_exp")
        adjd_loaded = [sem(f"adjd_loaded{e}") for e in range(2)]
        sadj_loaded = sem("sadj_loaded")
        sadj_masked = sem("sadj_masked")
        t_ps = sem("t_ps")
        t_hi = sem("t_hi")
        t_lo = sem("t_lo")
        s_ps = sem("s_ps")
        scores = sem("scores")
        max_step = sem("max_step")
        probs = sem("probs")
        out_exp = sem("out_exp")
        z_step = sem("z_step")
        pt_ps = sem("pt_ps")
        pt_hi = sem("pt_hi")
        pt_lo = sem("pt_lo")
        pv_done = sem("pv_done")
        o_step = sem("o_step")
        res_d = sem("res_d")
        res_s = sem("res_s")
        bn_ready = sem("bn_ready")
        rstd_ready = sem("rstd_ready")
        normed = sem("normed")
        fin_free = sem("fin_free")
        stored = sem("stored")
        rs_ready = sem("rs_ready")
        rs_bn = sem("rs_bn")
        rs_rstd = sem("rs_rstd")
        xs_ready = sem("xs_ready")
        xs_kept = sem("xs_kept")
        xst_ps = sem("xst_ps")
        xst_hi_ready = sem("xst_hi_ready")
        xst_lo_ready = sem("xst_lo_ready")
        ts_ps = sem("ts_ps")
        ts_hi_ready = sem("ts_hi_ready")
        ts_lo_ready = sem("ts_lo_ready")
        vs_ps = sem("vs_ps")
        vs_hi_ready = sem("vs_hi_ready")
        vs_lo_ready = sem("vs_lo_ready")
        ss_ps = sem("ss_ps")
        sscores = sem("sscores")
        smax_step = sem("smax_step")
        sprobs = sem("sprobs")
        sout_exp = sem("sout_exp")
        sz_step = sem("sz_step")
        spt_ps = sem("spt_ps")
        spt_hi = sem("spt_hi")
        spt_lo = sem("spt_lo")
        spv_done = sem("spv_done")
        so_step = sem("so_step")

        block = ctx.enter_context(nc.Block())

        def hid_bank(g, q):
            return 4 + 2 * (g % 2) + q // 2, (q % 2) * F

        DG = DT // 4
        def dense_stat(e, name):
            at_, n = dict(z4=(0, 4), mx4=(4, 4), mx=(8, 1), m=(9, 1), bias=(10, 1), out=(11, 1), zs=(12, 1),
                          z=(13, 1), rz=(14, 1))[name]
            return tiny[:, 16 * e + at_:16 * e + at_ + n]

        def small_stat(name, u=None):
            at_ = 32 + 2 * ("mx", "t", "m", "bias", "dm", "out", "zs", "z", "rz").index(name)
            return tiny[:, at_:at_ + 2] if u is None else tiny[:, at_ + u:at_ + u + 1]

        rstd_d, shift_d = tiny[:, 50:66], tiny[:, 66:82]
        rstd_s, shift_s = tiny[:, 82:84], tiny[:, 84:86]
        rstd_r, shift_r = tiny[:, 86:90], tiny[:, 90:94]
        scratch = [[tiny[:, 94 + 12 * par + 4 * q:98 + 12 * par + 4 * q] for q in range(3)] for par in range(2)]
        mout, zout, cd, cs, lowest = rowc[:, 0:RT], rowc[:, RT:2 * RT], rowc[:, 64:80], rowc[:, 80:82], rowc[:, 96:96 + RT]

        @block.sync
        def _(sp):
            sp.dma_start(w0f, W0.rearrange("(k p) f -> p k f", p=P)).then_inc(w0_loaded, 16)
            sp.dma_start(b0b, b0[None, :].to_broadcast((P, F))).then_inc(w0_loaded, 16)
            for q in range(4):
                sp.dma_start(y[:, ST * q:ST * (q + 1), :], x_tiles[:, ST * q:ST * (q + 1), :]).then_inc(x_loaded[q], 16)
            for w, dram in ((wq_in, Wq), (wk_in, Wk), (wv_in, Wv)):
                sp.dma_start(w, dram.rearrange("(k p) f -> p k f", p=P)).then_inc(weights_loaded, 16)
            with nc.allow_non_contiguous_dma("short columns"):
                sp.dma_start(bq_in, bq.rearrange("(k p) -> p k", p=P)).then_inc(weights_loaded, 16)
                sp.dma_start(bk_in, bk.rearrange("(k p) -> p k", p=P)).then_inc(weights_loaded, 16)
                sp.dma_start(ptr_in, ptr[:, None]).then_inc(weights_loaded, 16)
            sp.dma_start(bvs[:], bv[None, :].to_broadcast((P, F))).then_inc(weights_loaded, 16)
            for s in range(NS):
                for n in range(NC):
                    k = NC * s + n
                    if k >= SLOTS:
                        before = divmod(k - SLOTS, NC)
                        sp.wait_ge(a_ready, k - SLOTS + 1)
                        if has_outside(*before):
                            sp.wait_ge(outside_done, outside_count(*before))
                    if k == SLOTS - 1:
                        sp.wait_ge(weights_split, 2)
                        sp.wait_ge(branch_ready, 1)
                    sp.dma_start(adjb[:, n % SLOTS], adj_chunks[BLOCKS[s], column_chunk(s, n)]).then_inc(slot_loaded[n % SLOTS], 16)

            sp.wait_ge(branch_ready, 1)
            flag = sp.value_load(irregular[0:1, 0:1], min_val=0, max_val=1)
            with sp.If(flag == 0):
                outside_all = outside_count(NS - 1, NC - 1)
                sp.wait_ge(outside_done, outside_all - 3)
                sp.dma_start(again, x_tiles[:, DT:RT, :]).then_inc(again_loaded, 16)
                sp.wait_ge(outside_done, outside_all - 2)
                sp.dma_start(xs_again[:], x_tiles[:, 0:DT, :]).then_inc(small_again_loaded, 16)
                sp.wait_ge(outside_done, outside_all)

                def load_dense(i, e):
                    sp.dma_start(adjd[:, e, :], adj_rows[i + DT, :, DT * P:N]).then_inc(adjd_loaded[e], 16)

                def load_small(m):
                    for u in range(2):
                        sp.dma_start(sadj[:, u, :], adj_blocks[2 * m + u, 2 * m + u]).then_inc(sadj_loaded, 16)

                def store(m):
                    sp.wait_ge(normed, 4 * m + 8)
                    sp.dma_start(out_pairs[m + PAIRS], fin[:, 0:2, :]).then_inc(stored, 16)
                    sp.dma_start(out_pairs[m], fin[:, 2:4, :]).then_inc(stored, 16)
                    sp.wait_ge(stored, 32 * m + 32)
                    sp.sem_inc(fin_free, 1)

                def body(m, first=False, last=False):
                    if not last:
                        sp.wait_ge(sadj_masked, m + 1)
                        load_small(m + 1)
                        for e in range(2):
                            sp.wait_ge(scores, 8 * m + 4 * e + 4)
                            load_dense(2 * m + 2 + e, e)
                    if not first:
                        store(m - 1)

                load_dense(0, 0)
                load_dense(1, 1)
                load_small(0)
                body(0, first=True)
                with sp.Fori(1, PAIRS - 1) as m:
                    body(m)
                body(PAIRS - 1, last=True)
                store(PAIRS - 1)
            with sp.Else():
                sp.wait_ge(mm_done, JT * NC * NS)
                sp.dma_start(xre[:], x_tiles).then_inc(xre_loaded, 16)
                sp.wait_ge(xn_ready, RT)
                sp.dma_start(wqf[:], Wq.rearrange("(k p) f -> p k f", p=P)).then_inc(g_loaded, 16)
                sp.dma_start(wkf[:], Wk.rearrange("(k p) f -> p k f", p=P)).then_inc(g_loaded, 16)
                sp.dma_start(wvf[:], Wv.rearrange("(k p) f -> p k f", p=P)).then_inc(g_loaded, 16)
                with nc.allow_non_contiguous_dma("two short columns"):
                    sp.dma_start(bqc[:], bq.rearrange("(k p) -> p k", p=P)).then_inc(g_loaded, 16)
                    sp.dma_start(bkc[:], bk.rearrange("(k p) -> p k", p=P)).then_inc(g_loaded, 16)
                sp.dma_start(gbv[:, 0:F], bv[None, :].to_broadcast((P, F))).then_inc(g_loaded, 16)
                sp.dma_start(ptri[0:NPTR, :], ptr[:, None]).then_inc(g_loaded, 16)
                with sp.Fori(0, RT) as i:
                    sp.wait_ge(g_max, i + 1)
                    sp.dma_start(adjr[:], adj_rows[i]).then_inc(g_adj, 16)
                    sp.wait_ge(g_fin, i + 2)
                    sp.dma_start(out_tiles[i], gfin[:]).then_inc(g_out, 16)
                    sp.wait_ge(g_out, 16 * i + 16)
                    sp.sem_inc(g_stored, 1)

        @block.gpsimd
        def _(pool):
            nc.gpsimd.memset(ident[:], 0.0).then_inc(ident_zeroed, 1)
            nc.gpsimd.memset(zerob[:], 0.0).then_inc(ident_zeroed, 1)
            nc.gpsimd.memset(ones_in, 1.0).then_inc(ones_ready, 1)
            nc.gpsimd.iota(ptr_want, pattern=[[0, 1]], base=0, channel_multiplier=GRAPH).then_inc(ones_ready, 1)
            pool.wait_ge(ident_zeroed, 2)
            nc.gpsimd.affine_select(out=ident[:], in_=ident[:], compare_op=ALU.not_equal, fill=1.0, base=0,
                                    pattern=[[-1, P]], channel_multiplier=1).then_inc(ident_ready, 1)
            nc.gpsimd.memset(least[:], OUTSIDE).then_inc(outside_cleared, 1)
            nc.gpsimd.memset(zpart[:], 0.0).then_inc(outside_cleared, 1)
            for q, value in enumerate((float(F // 4) ** 0.5, F * EPS, float(F) ** 0.5, -0.5)):
                last = nc.gpsimd.memset(consts[:, q, :], value)
            last.then_inc(consts_ready, 1)
            pool.wait_ge(slot_loaded[0], 16)
            nc.gpsimd.tensor_scalar(anat[:, 0], adjb[:, 0], 0.0, 1.0, ALU.is_equal, ALU.is_lt).then_inc(a_ready, 1)
            for s in (BLOCKS.index(0), BLOCKS.index(1)):
                for n in range(2):
                    pool.wait_ge(a_ready, NC * s + n + 1)
                    for h in range(2):
                        rows, w = slice(h * GRAPH, (h + 1) * GRAPH), adjb[h * GRAPH:(h + 1) * GRAPH, n]
                        for q in range(JT):
                            last = nc.gpsimd.memset(w[:, JT * n + q, q * P + h * GRAPH:q * P + (h + 1) * GRAPH], OUTSIDE)
                    last.then_inc(masked, 1)

            pool.wait_ge(branch_ready, 1)
            flag = pool.value_load(irregular[0:1, 0:1], min_val=0, max_val=1)
            with pool.If(flag == 0):
                pool.wait_ge(consts_ready, 1)
                half_d, f_eps, root_f, minus_half = (consts[:, q, :] for q in range(4))

                def reciprocal_std(group, par, n, stats, rstd, shift, ready):
                    d, v, mean = (q[:, 0:n] for q in scratch[par])
                    step = [6 * group]

                    def link(ins):
                        step[0] = step[0] + 1
                        ins.then_inc(pool_step, 1)
                        pool.wait_ge(pool_step, step[0])

                    tt = nc.gpsimd.tensor_tensor
                    tt(d, stats[:, :, 1], stats[:, :, 4], ALU.subtract)
                    tt(v, stats[:, :, 2], stats[:, :, 5], ALU.add)
                    link(tt(mean, stats[:, :, 1], stats[:, :, 4], ALU.add))
                    tt(d, d, half_d[:, 0:n], ALU.mult)
                    tt(v, v, f_eps[:, 0:n], ALU.add)
                    link(tt(mean, mean, minus_half[:, 0:n], ALU.mult))
                    link(tt(d, d, d, ALU.mult))
                    link(tt(v, v, d, ALU.add))
                    link(tt(rstd, v, minus_half[:, 0:n], ALU.pow))
                    link(tt(rstd, rstd, root_f[:, 0:n], ALU.mult))
                    tt(shift, mean, rstd, ALU.mult).then_inc(ready, 1)

                def mask_small(m):
                    pool.wait_ge(sadj_loaded, 32 * m + 32)
                    if not (isinstance(m, int) and m == 0):
                        pool.wait_ge(sscores, m)
                    nc.gpsimd.tensor_tensor(sadjm[:], sadj[:], cross[:], ALU.add).then_inc(sadj_masked, 1)

                for g in range(DG):
                    pool.wait_ge(d_bn, 4 * g + 4)
                    reciprocal_std(g, g % 2, 4, bn[:, 4 * g:4 * g + 4, :], rstd_d[:, 4 * g:4 * g + 4],
                                   shift_d[:, 4 * g:4 * g + 4], d_rstd)
                pool.wait_ge(outside_done, outside_count(NS - 1, NC - 1))
                nc.gpsimd.memset(cross[:], 0.0).then_inc(cross_ready, 1)
                pool.wait_ge(cross_ready, 1)
                nc.gpsimd.memset(cross[0:GRAPH, :, GRAPH:P], -OUTSIDE)
                nc.gpsimd.memset(cross[GRAPH:P, :, 0:GRAPH], -OUTSIDE).then_inc(cross_ready, 1)
                pool.wait_ge(cross_ready, 2)
                pool.wait_ge(rs_bn, 2)
                reciprocal_std(DG, 0, 2, bn[:, 16:18, :], rstd_s, shift_s, rs_rstd)
                mask_small(0)
                nc.gpsimd.memset(fin[:, 0, 0:1], 0.0).then_inc(normed, 4)
                nc.gpsimd.memset(fin[:, 1, 0:1], 0.0).then_inc(fin_free, 1)

                def results_std(m, group, par):
                    pool.wait_ge(bn_ready, 4 * m + 4)
                    reciprocal_std(group, par, 4, bn[:, 18:22, :], rstd_r, shift_r, rstd_ready)

                def body(m, first=False, last=False):
                    if not first:
                        results_std(m - 1, DG + 2 * m, 0)
                    if not last:
                        pool.wait_ge(rs_bn, 2 * m + 4)
                        reciprocal_std(DG + 1 + 2 * m, 1, 2, bn[:, 16:18, :], rstd_s, shift_s, rs_rstd)
                        mask_small(m + 1)

                body(0, first=True)
                with pool.Fori(1, PAIRS - 1) as m:
                    body(m)
                body(PAIRS - 1, last=True)
                results_std(PAIRS - 1, DG + 2 * PAIRS - 1, 1)
            with pool.Else():
                pool.wait_ge(xn_ready, RT)
                nc.gpsimd.memset(ones[:], 1.0).then_inc(g_ones, 1)
                nc.gpsimd.iota(iota[0:NPTR, :], pattern=[[1, N]], base=0, channel_multiplier=0).then_inc(g_iota, 1)

        @block.tensor
        def _(pe):
            def hi_lo_passes(operands):
                (a_hi, a_lo), (b_hi, b_lo) = operands
                return [(a, b, k) for a, b in ((a_hi, b_hi), (a_hi, b_lo), (a_lo, b_hi)) for k in range(KT)]

            def product(out_, passes, stationary, moving):
                for i, (a, b, k) in enumerate(passes):
                    last = nc.tensor.matmul(out_, stationary(a, k), moving(b, k), start=(i == 0), stop=(i == len(passes) - 1))
                return last

            pe.wait_ge(ident_ready, 1)

            def transpose_x(g):
                if g % 2 == 0:
                    pe.wait_ge(x_loaded[g // 2], 16)
                if g >= 2:
                    pe.wait_ge(xt_lo_ready, 2 * (g - 1))
                for k in range(KT):
                    for q in range(4):
                        last = nc.tensor.transpose(ps[:, 2 * (g % 2) + k, q * P:(q + 1) * P],
                                                   y[:, 4 * g + q, k * P:(k + 1) * P], ident[:])
                    last.then_inc(xt_done, 1)

            def hidden(g):
                if g == 0:
                    pe.wait_ge(w0_split, 2)
                pe.wait_ge(xt_lo_ready, 2 * (g + 1))
                if g >= 2:
                    pe.wait_ge(hsum_ready, 2 * (g - 1))
                for q in range(4):
                    bank, col = hid_bank(g, q)
                    product(ps[:, bank, col:col + F], hi_lo_passes(((xT_hi, xT_lo), (w0_hi, w0_lo))),
                            lambda xt, k: xt[:, g % 2, k, q * P:(q + 1) * P],
                            lambda w, k: w[:, k, :]).then_inc(hid_done, 1)

            def weights():
                pe.wait_ge(weights_loaded, 16 * 7)
                pe.wait_ge(ones_ready, 2)
                pe.wait_ge(xt_lo_ready, KT * RT // 4)
                pe.wait_ge(weights_products, 1)
                for m in range(KT):
                    cols = slice(m * P, (m + 1) * P)
                    for k in range(KT):
                        nc.tensor.matmul(ps[:, 0, m * F:(m + 1) * F], wq_in[:, k, cols], wk_in[:, k, :],
                                         start=(k == 0), stop=(k == KT - 1))
                    for k in range(KT):
                        nc.tensor.transpose(ps[:, 1, m * F + k * P:m * F + (k + 1) * P], wv_in[:, k, cols], ident[:])
                for m in range(KT):
                    cols = slice(m * P, (m + 1) * P)
                    for col, w, b in ((m, wk_in, bq_in), (KT + m, wq_in, bk_in)):
                        for k in range(KT):
                            nc.tensor.matmul(ps[:, 2, col:col + 1], w[:, k, cols], b[:, k:k + 1],
                                             start=(k == 0), stop=(k == KT - 1))
                for k in range(KT):
                    nc.tensor.matmul(ps[:, 2, 4:5], ones_in, bb_in[:, k:k + 1], start=(k == 0), stop=(k == KT - 1))
                pe.wait_ge(ptr_far, 1)
                nc.tensor.matmul(ps[0:1, 2, 5:6], ones_in[0:NPTR, 0:1], ptr_d, start=True, stop=True).then_inc(weights_sums, 1)

            transpose_x(0)
            for g in range(RT // 4):
                if g + 1 < RT // 4:
                    transpose_x(g + 1)
                hidden(g)
            weights()

            pe.wait_ge(identb_ready, 1)
            pe.wait_ge(hsum_ready, RT // 2)

            def transposes(k, par, j):
                pe.wait_ge(a_ready, k + 1)
                for t in range(ST):
                    last = nc.tensor.transpose(ps[:, 4 + j, :].bitcast(BF16)[:, t * P:(t + 1) * P],
                                               anat[:, par, t, j * P:(j + 1) * P], identb[:])
                last.then_inc(t_done, 1)

            def products(k, c, j):
                pe.wait_ge(at_ready[j], k + 1)
                for t in range(ST):
                    for half in range(2):
                        last = nc.tensor.matmul(ps[:, t // 2, (t % 2) * F:(t % 2 + 1) * F],
                                                at[:, j, t * P:(t + 1) * P],
                                                hid[:, JT * c + j, half * F:(half + 1) * F],
                                                start=False, stop=False, skip_group_check=True)
                last.then_inc(mm_done, 1)

            def clear_sums():
                for b in range(4):
                    nc.tensor.matmul(ps[:, b, :], identb[:], zerob[:], start=True, stop=True, skip_group_check=True)

            def chunk(s, n, par, ahead=True):
                for j in range(JT):
                    products(NC * s + n, column_chunk(s, n), j)
                    if ahead:
                        transposes(NC * s + n + 1, 1 - par, j)

            for j in range(JT):
                transposes(0, 0, j)
            pe.wait_ge(weights_split, 2)
            clear_sums()
            pe.wait_ge(hid_lo_ready, RT // 2)
            with pe.Fori(0, NS - 1) as s:
                with pe.Fori(0, NC, 2) as n:
                    chunk(s, n, 0)
                    chunk(s, n + 1, 1)
                pe.wait_ge(acc_free, 4 * (s + 1))
                clear_sums()
            with pe.Fori(0, NC - 2, 2) as n:
                chunk(NS - 1, n, 0)
                chunk(NS - 1, n + 1, 1)
            chunk(NS - 1, NC - 2, 0)
            chunk(NS - 1, NC - 1, 1, ahead=False)

            pe.wait_ge(branch_ready, 1)
            flag = pe.value_load(irregular[0:1, 0:1], min_val=0, max_val=1)
            with pe.If(flag == 0):
                dense_x = (xd_hi, xd_lo)

                def transpose_dense(g):
                    if g < 2:
                        pe.wait_ge(d_x_first, 4 * g + 4)
                    else:
                        pe.wait_ge(d_x, 4 * g - 4)
                    for k in range(KT):
                        if g >= 2:
                            pe.wait_ge(xd_lo_ready, 2 * (g - 2) + k + 1)
                        for q in range(4):
                            last = nc.tensor.transpose(ps[:, 4 + 2 * (g % 2) + k, q * P:(q + 1) * P],
                                                       y[:, DT + 4 * g + q, k * P:(k + 1) * P], ident[:])
                        last.then_inc(xd_ps, 1)

                def dense_value(g):
                    pe.wait_ge(xd_lo_ready, 2 * g + 2)
                    for q in range(4):
                        t = 4 * g + q
                        if t >= 4:
                            pe.wait_ge(vd_free, t - 3)
                        product(ps[:, q, 0:F + 2], hi_lo_passes((dense_x, (wv_hi, wv_lo))),
                                lambda a, k: a[:, k, t * P:(t + 1) * P], lambda b, k: b[:, k, :]).then_inc(vd_ps, 1)

                def dense_t(m):
                    for f in range(KT):
                        last = product(ps[:, 7, f * 2 * P:(f + 1) * 2 * P], hi_lo_passes(((g_hi, g_lo), dense_x)),
                                       lambda a, k: a[:, k, f * P:(f + 1) * P],
                                       lambda b, k: b[:, k, bass.ts(m, 2 * P)])
                    last.then_inc(t_ps, 1)

                def dense_scores(m, e, first):
                    pe.wait_ge(t_lo, m + 1)
                    for c in range(DC):
                        if not first or e:
                            pe.wait_ge(scores, 8 * m + 4 * e + c - 3)
                        if e:
                            pe.wait_ge((xst_lo_ready, ts_lo_ready, vs_lo_ready, vs_lo_ready)[c],
                                       (m + 1, m + 1, 2 * m + 1, 2 * m + 2)[c])
                        elif not first and c < 2:
                            pe.wait_ge((sscores, spt_lo)[c], m)
                        if first and not e:
                            pe.wait_ge(vd_free, DT - 3 + c)
                        product(ps[:, c, :], hi_lo_passes(((td_hi, td_lo), dense_x)),
                                lambda a, k: a[:, k, e * P:(e + 1) * P],
                                lambda b, k: b[:, k, c * CW:(c + 1) * CW]).then_inc(s_ps, 1)

                def pt(j, e, c, first):
                    pe.wait_ge(probs, 4 * j + c + 1)
                    if not first or c >= 2:
                        pe.wait_ge(pt_lo, 4 * j + c - 1)
                    for q in range(JT):
                        last = nc.tensor.transpose(ps[:, 4 + c % 2, q * P:(q + 1) * P],
                                                   scd[:, e, c * CW + q * P:c * CW + (q + 1) * P], ident[:])
                    last.then_inc(pt_ps, 1)

                def pv(j, c, first):
                    pe.wait_ge(pt_lo, 4 * j + c + 1)
                    if c == 0 and not first:
                        pe.wait_ge(res_d, j)
                    for q in range(JT):
                        v_q = vd[:, JT * c + q, :]
                        for i, (p_, v_) in enumerate(((ptd_hi, v_q[:, 0:F]), (ptd_hi, v_q[:, F:2 * F]), (ptd_lo, v_q[:, 0:F]))):
                            last = nc.tensor.matmul(ps[:, 6, 0:F], p_[:, c % 2, q * P:(q + 1) * P], v_,
                                                    start=(c == 0 and q == 0 and i == 0),
                                                    stop=(c == DC - 1 and q == JT - 1 and i == 2))
                    last.then_inc(pv_done, 1)

                def small_transposes(m):
                    pe.wait_ge(xs_ready, 2 * m + 2)
                    pe.wait_ge(scores, 8 * m + 1)
                    for k in range(KT):
                        for u in range(2):
                            last = nc.tensor.transpose(ps[:, 0, (2 * k + u) * P:(2 * k + u + 1) * P],
                                                       xs[:, u, k * P:(k + 1) * P], ident[:])
                    last.then_inc(xst_ps, 1)

                def small_projections(m):
                    small_x = (xst_hi, xst_lo)
                    pe.wait_ge(xst_lo_ready, m + 1)
                    pe.wait_ge(scores, 8 * m + 4)
                    for f in range(KT):
                        last = product(ps[:, 1, f * 2 * P:(f + 1) * 2 * P], hi_lo_passes(((g_hi, g_lo), small_x)),
                                       lambda a, k: a[:, k, f * P:(f + 1) * P], lambda b, k: b[:, k, :])
                    last.then_inc(ts_ps, 1)
                    for u in range(2):
                        product(ps[:, 2 + u, 0:F + 2], hi_lo_passes((small_x, (wv_hi, wv_lo))),
                                lambda a, k: a[:, k, u * P:(u + 1) * P], lambda b, k: b[:, k, :]).then_inc(vs_ps, 1)

                def small_scores(m):
                    pe.wait_ge(ts_lo_ready, m + 1)
                    pe.wait_ge(scores, 8 * m + 5)
                    for u in range(2):
                        last = product(ps[:, 0, u * 2 * P:(u + 1) * 2 * P], hi_lo_passes(((ts_hi, ts_lo), (xst_hi, xst_lo))),
                                       lambda a, k: a[:, k, u * P:(u + 1) * P], lambda b, k: b[:, k, :])
                    last.then_inc(ss_ps, 1)

                def small_pt(m):
                    pe.wait_ge(sprobs, 2 * m + 2)
                    pe.wait_ge(scores, 8 * m + 6)
                    for u in range(2):
                        last = nc.tensor.transpose(ps[:, 1, u * P:(u + 1) * P], sp_[:, u, :], ident[:])
                    last.then_inc(spt_ps, 1)

                def small_pv(m):
                    pe.wait_ge(spt_lo, m + 1)
                    for u in range(2):
                        cols = slice(u * P, (u + 1) * P)
                        for i, (p_, v_) in enumerate(((pts_hi, vs_hi), (pts_hi, vs_lo), (pts_lo, vs_hi))):
                            last = nc.tensor.matmul(ps[:, 7, u * F:(u + 1) * F], p_[:, cols], v_[:, u, :],
                                                    start=(i == 0), stop=(i == 2))
                    last.then_inc(spv_done, 1)

                def attend(j, e, first=False, between=None, late=None):
                    pv(j, 0, first)
                    pt(j, e, 2, first)
                    pv(j, 1, first)
                    if between:
                        between()
                    pt(j, e, 3, first)
                    if late:
                        late()
                    pv(j, 2, first)
                    pv(j, 3, first)

                def start_attend(j, e, first=False):
                    pt(j, e, 0, first)
                    pt(j, e, 1, first)

                def body(m, first=False, last=False):
                    dense_scores(m, 0, first)
                    if not first:
                        small_pv(m - 1)
                    small_transposes(m)
                    if first:
                        small_projections(m)
                    else:
                        attend(2 * m - 1, 1, between=lambda: small_projections(m))
                    start_attend(2 * m, 0, first=first)
                    dense_scores(m, 1, first)
                    if not last:
                        if not first:
                            pe.wait_ge(res_s, 2 * m)
                        dense_t(m + 1)
                    small_scores(m)
                    attend(2 * m, 0, first=first, late=lambda: small_pt(m))
                    start_attend(2 * m + 1, 1)

                for j in range(JT):
                    pe.wait_ge(at_ready[j], NC * NS)
                transpose_dense(0)
                transpose_dense(1)
                pe.wait_ge(acc_free, 4 * NS)
                dense_value(0)
                transpose_dense(2)
                dense_value(1)
                transpose_dense(3)
                dense_value(2)
                pe.wait_ge(xd_lo_ready, 2 * DG)
                dense_t(0)
                dense_value(3)
                body(0, first=True)
                with pe.Fori(1, PAIRS - 1) as m:
                    body(m)
                body(PAIRS - 1, last=True)
                attend(2 * PAIRS - 1, 1)
                pe.wait_ge(t_lo, PAIRS)
                small_pv(PAIRS - 1)
            with pe.Else():
                pe.wait_ge(xn_ready, RT)
                pe.wait_ge(g_loaded, 16 * 7)
                pe.wait_ge(g_ones, 1)
                pe.wait_ge(g_bb, 1)
                pe.wait_ge(acc_free, 4 * NS)
                for m in range(KT):
                    for k in range(KT):
                        nc.tensor.matmul(ps[:, m, 0:F], wqf[:, k, m * P:(m + 1) * P], wkf[:, k, :],
                                         start=(k == 0), stop=(k == KT - 1))
                    for k in range(KT):
                        nc.tensor.transpose(ps[:, 2 + m, k * P:(k + 1) * P], wvf[:, k, m * P:(m + 1) * P], ident[:])
                    for col, w, b in ((m, wkf, bqc), (2 + m, wqf, bkc)):
                        for k in range(KT):
                            nc.tensor.matmul(ps[:, 4, col:col + 1], w[:, k, m * P:(m + 1) * P], b[:, k:k + 1],
                                             start=(k == 0), stop=(k == KT - 1))
                for k in range(KT):
                    last = nc.tensor.matmul(ps[:, 4, 4:5], ones[:], bkc2[:, k:k + 1], start=(k == 0), stop=(k == KT - 1))
                last.then_inc(g_wps, 1)
                pe.wait_ge(g_geq, 1)
                for t in range(RT):
                    last = nc.tensor.matmul(ps[:, 5, t:t + 1], geq[0:NPTR, t * P:(t + 1) * P], ones[0:NPTR, 0:1],
                                            start=True, stop=True)
                last.then_inc(g_gid_ps, 1)
                for c in range(NC):
                    pe.wait_ge(g_gid, c + 1)
                    nc.tensor.matmul(ps[:, 6, :], ones[0:NPTR, :], geq[0:NPTR, c * CW:(c + 1) * CW],
                                     start=True, stop=True).then_inc(g_gid_ps, 1)
                for g in range(RT // 4):
                    for k in range(KT):
                        if g >= 1:
                            pe.wait_ge(g_xt, 2 * (g - 1) + k + 1)
                        else:
                            pe.wait_ge(g_wsb, 1)
                        for q in range(4):
                            last = nc.tensor.transpose(ps[:, k, q * P:(q + 1) * P], y[:, 4 * g + q, k * P:(k + 1) * P], ident[:])
                        last.then_inc(g_xt_ps, 1)
                pe.wait_ge(g_xt, 2 * (RT // 4))
                for t in range(RT):
                    if t >= 2:
                        pe.wait_ge(g_v, t - 1)
                    for k in range(KT):
                        last = nc.tensor.matmul(ps[:, 2 + t % 2, 0:F + 1], xT[:, k, t * P:(t + 1) * P], wvT[:, k, :],
                                                start=(k == 0), stop=(k == KT - 1))
                    last.then_inc(g_v_ps, 1)
                pe.wait_ge(g_v, RT)
                with pe.Fori(0, RT) as i:
                    pe.wait_ge(g_fin, i + 1)
                    for m in range(KT):
                        for k in range(KT):
                            last = nc.tensor.matmul(ps[:, 0, m * P:(m + 1) * P], gmat[:, k, m * P:(m + 1) * P],
                                                    xT[:, k, bass.ts(i, P)], start=(k == 0), stop=(k == KT - 1))
                    last.then_inc(g_t_ps, 1)
                    pe.wait_ge(g_t, i + 1)
                    for c in range(NC):
                        for k in range(KT):
                            last = nc.tensor.matmul(ps[:, c, :], tT[:, k, :], xT[:, k, c * CW:(c + 1) * CW],
                                                    start=(k == 0), stop=(k == KT - 1))
                        last.then_inc(g_s_ps, 1)
                    pe.wait_ge(g_p, i + 1)
                    for c in range(NC):
                        for q in range(JT):
                            j = JT * c + q
                            last = nc.tensor.transpose(ps[:, c, q * P:(q + 1) * P], sc[:, j * P:(j + 1) * P], ident[:])
                        last.then_inc(g_pt_ps, 1)
                    pe.wait_ge(g_pt, NC * i + NC)
                    for j in range(RT):
                        last = nc.tensor.matmul(ps[:, 0, 0:F], pT[:, j, :], v[:, j, 0:F], start=(j == 0), stop=(j == RT - 1))
                    last.then_inc(g_o_ps, 1)

        @block.scalar
        def _(act):
            act.wait_ge(w0_loaded, 32)
            nc.scalar.copy(w0_hi[:], w0f).then_inc(w0_split, 1)
            act.wait_ge(ident_ready, 1)
            nc.scalar.copy(identb[:], ident[:]).then_inc(identb_ready, 1)

            def xt_hi(g):
                for k in range(KT):
                    act.wait_ge(xt_done, 2 * g + k + 1)
                    if g >= 2:
                        act.wait_ge(hid_done, 4 * (g - 1))
                    nc.scalar.copy(xT_hi[:, g % 2, k, :], ps[:, 2 * (g % 2) + k, :]).then_inc(xt_hi_ready, 1)

            xt_hi(0)
            for g in range(RT // 4):
                if g + 1 < RT // 4:
                    xt_hi(g + 1)
                for h in range(2):
                    act.wait_ge(hsum_ready, 2 * g + h + 1)
                    t = 4 * g + 2 * h
                    nc.scalar.copy(hid[:, t:t + 2, 0:F], hsum[:, 2 * h:2 * h + 2, :]).then_inc(hid_hi_ready, 1)
            act.wait_ge(weights_sums, 1)
            nc.scalar.mul(g_hi[:], ps[:, 0, :].rearrange("p (k f) -> p k f", f=F), SCALE / 2)
            nc.scalar.copy(wv_hi[:, :, 0:F], ps[:, 1, :].rearrange("p (k f) -> p k f", f=F))
            nc.scalar.mul(wcols[:, 0:5], ps[:, 2, 0:5], SCALE).then_inc(weights_hi, 1)

            def evacuate(s, n, j):
                k = NC * s + n
                act.wait_ge(t_done, JT * k + j + 1)
                if k >= 1:
                    act.wait_ge(mm_done, JT * (k - 1) + j + 1)
                nc.scalar.activation(at[:, j, :], ps[:, 4 + j, :].bitcast(BF16), ACT.Copy,
                                     accum_out=degp[:, JT * column_chunk(s, n) + j, s:s + 1]).then_inc(at_ready[j], 1)

            def outside(s, n, tiles):
                if not has_outside(s, n):
                    return
                if tiles[0] == 0:
                    act.wait_ge(ebias_ready, outside_count(s, n))
                for t in tiles:
                    row = ST * BLOCKS[s] + t
                    w = adjb[:, n % SLOTS, t, :]
                    last = nc.scalar.activation(w, w, ACT.Exp, scale=2 * NEG,
                                                bias=ebias[:, n % SLOTS, t:t + 1], accum_out=zpart[:, row, n:n + 1])
                if tiles[-1] == ST - 1:
                    last.then_inc(outside_done, 1)

            def take_sums(s):
                act.wait_ge(mm_done, JT * NC * (s + 1))
                row = ST * BLOCKS[s]
                for b in (0, 2):
                    nc.scalar.copy(y[:, row + 2 * b:row + 2 * b + 2, :],
                                   ps[:, b, :].rearrange("p (t f) -> p t f", f=F)).then_inc(acc_free, 1)

            act.wait_ge(hid_done, RT)
            act.wait_ge(outside_cleared, 2)
            for s in range(NS):
                for n in range(NC):
                    evacuate(s, n, 0)
                    outside(s, n, range(0, 3))
                    evacuate(s, n, 1)
                    if s >= 1 and n == 0:
                        evacuate(s, n, 2)
                        take_sums(s - 1)
                    outside(s, n, range(3, 6))
                    if not (s >= 1 and n == 0):
                        evacuate(s, n, 2)
                    outside(s, n, range(6, ST))

            act.wait_ge(branch_ready, 1)
            flag = act.value_load(irregular[0:1, 0:1], min_val=0, max_val=1)
            with act.If(flag == 0):
                def normalise_dense(g):
                    act.wait_ge(d_rstd, g + 1)
                    for q in range(4):
                        t = 4 * g + q
                        nc.scalar.activation(y[:, DT + t, :], y[:, DT + t, :], ACT.Identity, scale=rstd_d[:, t:t + 1],
                                             bias=shift_d[:, t:t + 1]).then_inc(d_x, 1)

                def split_dense(g):
                    for k in range(KT):
                        act.wait_ge(xd_ps, 2 * g + k + 1)
                        nc.scalar.copy(xd_hi[:, k, g * CW:(g + 1) * CW], ps[:, 4 + 2 * (g % 2) + k, :]).then_inc(xd_hi_ready, 1)

                def value_dense(g):
                    for q in range(4):
                        t = 4 * g + q
                        act.wait_ge(vd_ps, t + 1)
                        nc.scalar.copy(vd[:, t, 0:F], ps[:, q, 0:F]).then_inc(vd_hi_ready, 1)

                def split_t(m):
                    act.wait_ge(t_ps, m + 1)
                    for f in range(KT):
                        last = nc.scalar.activation(td_hi[:, f, :], ps[:, 7, f * 2 * P:(f + 1) * 2 * P], ACT.Identity,
                                                    bias=gv[:, f:f + 1])
                    last.then_inc(t_hi, 1)

                def pt_split(j, c):
                    act.wait_ge(pt_ps, 4 * j + c + 1)
                    nc.scalar.copy(ptd_hi[:, c % 2, :], ps[:, 4 + c % 2, :]).then_inc(pt_hi, 1)

                def exp_dense(i, e, c):
                    if c == 0:
                        act.wait_ge(max_step, 3 * i + 3)
                    cols = scd[:, e, c * CW:(c + 1) * CW]
                    nc.scalar.activation(cols, cols, ACT.Exp, bias=dense_stat(e, "bias"),
                                         accum_out=dense_stat(e, "z4")[:, c:c + 1]).then_inc(probs, 1)

                def exp_outside(i, e):
                    nc.scalar.activation(dense_stat(e, "out"), dense_stat(e, "m"), ACT.Exp, scale=-1.0,
                                         bias=mout[:, bass.ds(i + DT, 1)]).then_inc(out_exp, 1)

                def small_x(m):
                    act.wait_ge(rs_rstd, m + 1)
                    if not (isinstance(m, int) and m == 0):
                        act.wait_ge(xst_ps, m)
                    for u in range(2):
                        nc.scalar.activation(xs[:, u, :], rs[:, u, :], ACT.Identity, scale=rstd_s[:, u:u + 1],
                                             bias=shift_s[:, u:u + 1]).then_inc(xs_ready, 1)
                    for u in range(2):
                        nc.scalar.activation(y[:, 2 * m + u, :], rs[:, u, :], ACT.Identity, scale=rstd_s[:, u:u + 1],
                                             bias=shift_s[:, u:u + 1]).then_inc(xs_kept, 1)

                def small_pt_split(m):
                    act.wait_ge(spt_ps, m + 1)
                    nc.scalar.copy(pts_hi[:], ps[:, 1, 0:2 * P]).then_inc(spt_hi, 1)

                def small_split(m):
                    act.wait_ge(ts_ps, m + 1)
                    for f in range(KT):
                        last = nc.scalar.activation(ts_hi[:, f, :], ps[:, 1, f * 2 * P:(f + 1) * 2 * P], ACT.Identity,
                                                    bias=gv[:, f:f + 1])
                    last.then_inc(ts_hi_ready, 1)
                    for u in range(2):
                        act.wait_ge(vs_ps, 2 * m + u + 1)
                        nc.scalar.copy(vs_hi[:, u, :], ps[:, 2 + u, 0:F]).then_inc(vs_hi_ready, 1)

                def small_exp(m):
                    act.wait_ge(smax_step, 4 * m + 4)
                    for u in range(2):
                        nc.scalar.activation(sp_[:, u, :], sp_[:, u, :], ACT.Exp, scale=2.0, bias=small_stat("bias", u),
                                             accum_out=small_stat("zs", u)).then_inc(sprobs, 1)
                    nc.scalar.activation(small_stat("out"), small_stat("dm"), ACT.Exp).then_inc(sout_exp, 1)

                def normalise_results(m):
                    act.wait_ge(rstd_ready, m + 1)
                    act.wait_ge(fin_free, m + 1)
                    for q in range(4):
                        nc.scalar.activation(fin[:, q, :], res[:, q, :], ACT.Identity, scale=rstd_r[:, q:q + 1],
                                             bias=shift_r[:, q:q + 1]).then_inc(normed, 1)

                def body(m, first=False, last=False):
                    if not first:
                        pt_split(2 * m - 1, 0)
                        pt_split(2 * m - 1, 1)
                        small_x(m)
                    act.wait_ge(xst_ps, m + 1)
                    nc.scalar.copy(xst_hi[:], ps[:, 0, :].rearrange("p (k w) -> p k w", k=KT)).then_inc(xst_hi_ready, 1)
                    exp_dense(2 * m, 0, 0)
                    exp_dense(2 * m, 0, 1)
                    if not first:
                        pt_split(2 * m - 1, 2)
                    exp_dense(2 * m, 0, 2)
                    exp_dense(2 * m, 0, 3)
                    exp_outside(2 * m, 0)
                    small_split(m)
                    if not first:
                        pt_split(2 * m - 1, 3)
                    pt_split(2 * m, 0)
                    pt_split(2 * m, 1)
                    if not first:
                        normalise_results(m - 1)
                    if not last:
                        split_t(m + 1)
                    for c in range(DC):
                        exp_dense(2 * m + 1, 1, c)
                    exp_outside(2 * m + 1, 1)
                    pt_split(2 * m, 2)
                    small_exp(m)
                    pt_split(2 * m, 3)
                    small_pt_split(m)

                split_dense(0)
                take_sums(NS - 1)
                split_dense(1)
                normalise_dense(2)
                normalise_dense(3)
                act.wait_ge(mout_step, 3)
                nc.scalar.activation(least[:], least[:], ACT.Exp, scale=2 * NEG).then_inc(mout_exp, 1)
                value_dense(0)
                split_dense(2)
                value_dense(1)
                split_dense(3)
                value_dense(2)
                split_t(0)
                value_dense(3)
                small_x(0)
                body(0, first=True)
                with act.Fori(1, PAIRS - 1) as m:
                    body(m)
                body(PAIRS - 1, last=True)
                for c in range(DC):
                    pt_split(2 * PAIRS - 1, c)
                normalise_results(PAIRS - 1)
            with act.Else():
                take_sums(NS - 1)
                act.wait_ge(ln, 3)
                nc.scalar.activation(lnt[:, 3, :], lnt[:, 2, :], ACT.Sqrt).then_inc(std_ready, 1)

                act.wait_ge(g_wps, 1)
                for m in range(KT):
                    act.wait_ge(xn_ready, RT)
                    nc.scalar.mul(gmat[:, m, :], ps[:, m, 0:F], SCALE)
                    nc.scalar.copy(wvT[:, m, 0:F], ps[:, 2 + m, 0:F])
                nc.scalar.mul(gvec[:], ps[:, 4, 0:KT], SCALE)
                nc.scalar.mul(wvT[:, :, F], ps[:, 4, 2:2 + KT], SCALE)
                nc.scalar.mul(gbv[:, F:F + 1], ps[:, 4, 4:5], SCALE).then_inc(g_wsb, 1)
                for g in range(RT // 4):
                    for k in range(KT):
                        act.wait_ge(g_xt_ps, 2 * g + k + 1)
                        nc.scalar.copy(xT[:, k, g * CW:(g + 1) * CW], ps[:, k, :]).then_inc(g_xt, 1)
                with act.Fori(0, RT) as i:
                    act.wait_ge(g_t_ps, i + 1)
                    for m in range(KT):
                        last = nc.scalar.activation(tT[:, m, :], ps[:, 0, m * P:(m + 1) * P], ACT.Identity, bias=gvec[:, m:m + 1])
                    last.then_inc(g_t, 1)
                    act.wait_ge(g_max, i + 2)
                    nc.scalar.activation(sc[:], sc[:], ACT.Exp, bias=stat[:, 0:1], accum_out=stat[:, 1:2]).then_inc(g_exp, 1)
                    for c in range(NC):
                        act.wait_ge(g_pt_ps, NC * i + c + 1)
                        nc.scalar.copy(pT[:, JT * c:JT * (c + 1), :], ps[:, c, :].rearrange("p (t w) -> p t w", w=P)).then_inc(g_pt, 1)
                    act.wait_ge(g_var, i + 1)
                    nc.scalar.activation(stat[:, 5:6], stat[:, 4:5], ACT.Sqrt).then_inc(g_std, 1)

        @block.vector
        def _(dve):
            dve.wait_ge(w0_split, 1)
            nc.vector.tensor_tensor(w0_lo[:], w0f, w0_hi[:].bitcast(F32), ALU.subtract).then_inc(w0_split, 1)

            def xt_lo(g):
                for k in range(KT):
                    dve.wait_ge(xt_hi_ready, 2 * g + k + 1)
                    if g >= 2:
                        dve.wait_ge(hid_done, 4 * (g - 1))
                    nc.vector.tensor_tensor(xT_lo[:, g % 2, k, :], ps[:, 2 * (g % 2) + k, :],
                                            xT_hi[:, g % 2, k, :].bitcast(F32), ALU.subtract).then_inc(xt_lo_ready, 1)

            def weights_products_and_ptr():
                dve.wait_ge(weights_loaded, 16 * 7)
                dve.wait_ge(ones_ready, 2)
                nc.vector.tensor_tensor(bb_in, bq_in, bk_in, ALU.mult).then_inc(weights_products, 1)
                nc.vector.tensor_copy(ptr_f, ptr_in).then_inc(ptr_step, 1)
                nc.vector.tensor_copy(ptr_d, ptr_want).then_inc(ptr_step, 1)
                dve.wait_ge(ptr_step, 2)
                nc.vector.tensor_tensor(ptr_f, ptr_f, ptr_d, ALU.subtract).then_inc(ptr_step, 1)
                dve.wait_ge(ptr_step, 3)
                nc.vector.tensor_tensor(ptr_d, ptr_f, ptr_f, ALU.mult).then_inc(ptr_far, 1)

            xt_lo(0)
            for g in range(RT // 4):
                if g + 1 < RT // 4:
                    xt_lo(g + 1)
                if g == 4:
                    weights_products_and_ptr()
                for h in range(2):
                    bank, _ = hid_bank(g, 2 * h)
                    dve.wait_ge(hid_done, 4 * g + 2 * h + 2)
                    if g >= 1:
                        dve.wait_ge(hid_lo_ready, 2 * g + h - 1)
                    nc.vector.tensor_tensor(hsum[:, 2 * h:2 * h + 2, :], ps[:, bank, :].rearrange("p (t f) -> p t f", f=F),
                                            b0b[:, None, :].to_broadcast((P, 2, F)), ALU.add).then_inc(hsum_ready, 1)
                for h in range(2):
                    t = 4 * g + 2 * h
                    dve.wait_ge(hid_hi_ready, 2 * g + h + 1)
                    nc.vector.tensor_tensor(hid[:, t:t + 2, F:2 * F], hsum[:, 2 * h:2 * h + 2, :],
                                            hid[:, t:t + 2, 0:F].bitcast(F32), ALU.subtract).then_inc(hid_lo_ready, 1)
            dve.wait_ge(weights_hi, 1)
            for m in range(KT):
                nc.vector.scalar_tensor_tensor(g_lo[:, m, :], ps[:, 0, m * F:(m + 1) * F], SCALE / 2,
                                               g_hi[:, m, :].bitcast(F32), ALU.mult, ALU.subtract)
                nc.vector.tensor_tensor(wv_lo[:, m, 0:F], ps[:, 1, m * F:(m + 1) * F], wv_hi[:, m, 0:F].bitcast(F32), ALU.subtract)
            nc.vector.memset(wv_hi[:, :, F + 1].bitcast(F32), 0.0)
            nc.vector.memset(wv_lo[:, :, F + 1].bitcast(F32), 0.0)
            nc.vector.tensor_scalar(gv[:], wcols[:, 0:KT], 0.5, None, ALU.mult)
            nc.vector.tensor_scalar(bqbk[:], wcols[:, 4:5], 1.0, None, ALU.mult)
            nc.vector.tensor_scalar(irregular[:], ps[0:1, 2, 5:6], 1.0, None, ALU.min).then_inc(branch_ready, 1)
            nc.vector.tensor_copy(wv_hi[:, :, F], wcols[:, KT:2 * KT]).then_inc(weights_split, 1)
            dve.wait_ge(weights_split, 1)
            nc.vector.tensor_tensor(wv_lo[:, :, F], wcols[:, KT:2 * KT], wv_hi[:, :, F].bitcast(F32), ALU.subtract).then_inc(weights_split, 1)

            def make_a(s, n):
                k = NC * s + n
                dve.wait_ge(slot_loaded[n % SLOTS], 16 * (k // SLOTS + 1))
                if k == 1:
                    dve.wait_ge(a_ready, 1)
                if k >= 2:
                    dve.wait_ge(t_done, JT * (k - 1))
                nc.vector.tensor_scalar(anat[:, n % 2], adjb[:, n % SLOTS], 0.0, None, ALU.not_equal).then_inc(a_ready, 1)

            def outside(s, n):
                if not has_outside(s, n):
                    return
                if BLOCKS[s] < 2 and n < 2:
                    dve.wait_ge(masked, 2 * (s - BLOCKS.index(0)) + n + 1)
                rows = slice(ST * BLOCKS[s], ST * (BLOCKS[s] + 1))
                nc.vector.tensor_reduce(least[:, rows, n], adjb[:, n % SLOTS], AX.X, ALU.min).then_inc(least_ready, 1)
                dve.wait_ge(least_ready, outside_count(s, n))
                nc.vector.tensor_scalar(ebias[:, n % SLOTS, :], least[:, rows, n], -2 * NEG, None, ALU.mult).then_inc(ebias_ready, 1)

            def evacuate(s, n):
                k, j = NC * s + n, JT - 1
                dve.wait_ge(t_done, JT * k + j + 1)
                if k >= 1:
                    dve.wait_ge(mm_done, JT * (k - 1) + j + 1)
                nc.vector.tensor_scalar(at[:, j, :], ps[:, 4 + j, :].bitcast(BF16), 1.0, None, ALU.mult, ALU.add,
                                        accum_out=degp[:, JT * column_chunk(s, n) + j, s:s + 1]).then_inc(at_ready[j], 1)

            def take_sums(s):
                dve.wait_ge(mm_done, JT * NC * (s + 1))
                row = ST * BLOCKS[s]
                for b in (1, 3):
                    nc.vector.tensor_copy(y[:, row + 2 * b:row + 2 * b + 2, :],
                                          ps[:, b, :].rearrange("p (t f) -> p t f", f=F)).then_inc(acc_free, 1)

            dve.wait_ge(outside_cleared, 2)
            for s in range(NS):
                for n in range(NC):
                    k = NC * s + n
                    if k >= 2:
                        evacuate(*divmod(k - 2, NC))
                    if s >= 1 and n == 2:
                        take_sums(s - 1)
                    if k >= 1:
                        make_a(s, n)
                    if k == 1:
                        dve.wait_ge(slot_loaded[0], 16)
                        outside(0, 0)
                    if k >= 1:
                        outside(s, n)

            dve.wait_ge(branch_ready, 1)
            flag = dve.value_load(irregular[0:1, 0:1], min_val=0, max_val=1)
            with dve.If(flag == 0):
                stt, tt, ts = nc.vector.scalar_tensor_tensor, nc.vector.tensor_tensor, nc.vector.tensor_scalar

                def dense_residual(g):
                    for q in range(4):
                        t = DT + 4 * g + q
                        stt(y[:, t, :], y[:, t, :], rdeg[:, t:t + 1], again[:, 4 * g + q, :], ALU.mult, ALU.add).then_inc(d_res, 1)
                    for q in range(4):
                        t = 4 * g + q
                        dve.wait_ge(d_res, t + 1)
                        nc.vector.bn_stats(bn[:, t, :], y[:, DT + t, :]).then_inc(d_bn, 1)

                def normalise_dense(g):
                    dve.wait_ge(d_rstd, g + 1)
                    for q in range(4):
                        t = 4 * g + q
                        ts(y[:, DT + t, :], y[:, DT + t, :], rstd_d[:, t:t + 1], shift_d[:, t:t + 1],
                           ALU.mult, ALU.add).then_inc(d_x_first, 1)

                def split_dense(g):
                    for k in range(KT):
                        dve.wait_ge(xd_hi_ready, 2 * g + k + 1)
                        cols = slice(g * CW, (g + 1) * CW)
                        tt(xd_lo[:, k, cols], ps[:, 4 + 2 * (g % 2) + k, :], xd_hi[:, k, cols].bitcast(F32),
                           ALU.subtract).then_inc(xd_lo_ready, 1)

                def value_dense(g):
                    for q in range(4):
                        t = 4 * g + q
                        dve.wait_ge(vd_hi_ready, t + 1)
                        tt(vd[:, t, F:2 * F], ps[:, q, 0:F], vd[:, t, 0:F].bitcast(F32), ALU.subtract)
                        tt(cd[:, t:t + 1], ps[:, q, F:F + 1], bqbk[:], ALU.add).then_inc(vd_free, 1)

                def split_t(m):
                    dve.wait_ge(t_hi, m + 1)
                    for f in range(KT):
                        last = stt(td_lo[:, f, :], ps[:, 7, f * 2 * P:(f + 1) * 2 * P], gv[:, f:f + 1],
                                   td_hi[:, f, :].bitcast(F32), ALU.add, ALU.subtract)
                    last.then_inc(t_lo, 1)

                def make_scores(i, e, m, between=None):
                    dve.wait_ge(adjd_loaded[e], 16 * m + 16)
                    for c in range(DC):
                        cols = slice(c * CW, (c + 1) * CW)
                        dve.wait_ge(s_ps, 4 * i + c + 1)
                        nc.vector.memset(settled[:, c:c + 1], 0.0)
                        nc.vector.tensor_tensor_reduce(out=scd[:, e, cols], in0=ps[:, c, :], in1=adjd[:, e, cols], scale=2.0,
                                                       scalar=-3e38, op0=ALU.add, op1=ALU.max,
                                                       accum_out=dense_stat(e, "mx4")[:, c:c + 1]).then_inc(scores, 1)
                        if between and c == 0:
                            between()
                    dve.wait_ge(scores, 4 * i + 4)
                    c_i = cd[:, bass.ds(i, 1)]
                    nc.vector.reduce_max(dense_stat(e, "mx"), dense_stat(e, "mx4"), AX.X).then_inc(max_step, 1)
                    dve.wait_ge(max_step, 3 * i + 1)
                    ts(dense_stat(e, "m"), dense_stat(e, "mx"), c_i, mout[:, bass.ds(i + DT, 1)], ALU.add, ALU.max).then_inc(max_step, 1)
                    dve.wait_ge(max_step, 3 * i + 2)
                    tt(dense_stat(e, "bias"), c_i, dense_stat(e, "m"), ALU.subtract).then_inc(max_step, 1)

                def split_pt(j, c):
                    dve.wait_ge(pt_hi, 4 * j + c + 1)
                    tt(ptd_lo[:, c % 2, :], ps[:, 4 + c % 2, :], ptd_hi[:, c % 2, :].bitcast(F32), ALU.subtract).then_inc(pt_lo, 1)

                def sums_dense(j, e):
                    dve.wait_ge(out_exp, j + 1)
                    nc.vector.reduce_sum(dense_stat(e, "zs"), dense_stat(e, "z4"), AX.X).then_inc(z_step, 1)
                    dve.wait_ge(z_step, 3 * j + 1)
                    stt(dense_stat(e, "z"), dense_stat(e, "out"), zout[:, bass.ds(j + DT, 1)], dense_stat(e, "zs"),
                        ALU.mult, ALU.add).then_inc(z_step, 1)
                    dve.wait_ge(z_step, 3 * j + 2)
                    nc.vector.reciprocal(dense_stat(e, "rz"), dense_stat(e, "z")).then_inc(z_step, 1)

                def finish_dense(j, e):
                    dve.wait_ge(pv_done, 4 * j + 4)
                    dve.wait_ge(normed, 2 * (j - e) + e + 1)
                    stt(res[:, e, :], bvs[:], dense_stat(e, "zs"), ps[:, 6, 0:F], ALU.mult, ALU.add).then_inc(res_d, 1)
                    dve.wait_ge(z_step, 3 * j + 3)
                    dve.wait_ge(res_d, j + 1)
                    stt(res[:, e, :], res[:, e, :], dense_stat(e, "rz"), y[:, j + DT, :], ALU.mult, ALU.add).then_inc(o_step, 1)

                def results_stats(m):
                    dve.wait_ge(o_step, 2 * m + 2)
                    dve.wait_ge(so_step, 2 * m + 2)
                    for q in range(4):
                        nc.vector.bn_stats(bn[:, 18 + q, :], res[:, q, :]).then_inc(bn_ready, 1)

                def small_residual(m, first=False):
                    dve.wait_ge(small_again_loaded, 16)
                    if not first:
                        dve.wait_ge(xs_kept, 2 * m)
                    for u in range(2):
                        stt(rs[:, u, :], y[:, 2 * m + u, :], rdeg[:, bass.ds(2 * m + u, 1)], xs_again[:, 2 * m + u, :],
                            ALU.mult, ALU.add).then_inc(rs_ready, 1)
                    for u in range(2):
                        dve.wait_ge(rs_ready, 2 * m + u + 1)
                        nc.vector.bn_stats(bn[:, 16 + u, :], rs[:, u, :]).then_inc(rs_bn, 1)

                def small_split_x(m):
                    dve.wait_ge(xst_hi_ready, m + 1)
                    tt(xst_lo[:], ps[:, 0, :].rearrange("p (k w) -> p k w", k=KT), xst_hi[:].bitcast(F32),
                       ALU.subtract).then_inc(xst_lo_ready, 1)

                def small_split(m):
                    dve.wait_ge(ts_hi_ready, m + 1)
                    for f in range(KT):
                        last = stt(ts_lo[:, f, :], ps[:, 1, f * 2 * P:(f + 1) * 2 * P], gv[:, f:f + 1],
                                   ts_hi[:, f, :].bitcast(F32), ALU.add, ALU.subtract)
                    last.then_inc(ts_lo_ready, 1)
                    for u in range(2):
                        dve.wait_ge(vs_hi_ready, 2 * m + u + 1)
                        tt(vs_lo[:, u, :], ps[:, 2 + u, 0:F], vs_hi[:, u, :].bitcast(F32), ALU.subtract)
                        tt(cs[:, u:u + 1], ps[:, 2 + u, F:F + 1], bqbk[:], ALU.add).then_inc(vs_lo_ready, 1)

                def small_scores(m):
                    dve.wait_ge(ss_ps, m + 1)
                    dve.wait_ge(sadj_masked, m + 1)
                    for u in range(2):
                        last = tt(sp_[:, u, :], ps[:, 0, u * 3 * P:u * 3 * P + P], sadjm[:, u, :], ALU.add)
                    last.then_inc(sscores, 1)
                    dve.wait_ge(sscores, m + 1)
                    dve.wait_ge(vs_lo_ready, 2 * m + 2)
                    nc.vector.reduce_max(small_stat("mx"), sp_[:], AX.X).then_inc(smax_step, 1)
                    dve.wait_ge(smax_step, 4 * m + 1)
                    mout_m = mout[:, bass.ds(2 * m, 2)]
                    stt(small_stat("t"), small_stat("mx"), 2.0, cs, ALU.mult, ALU.add).then_inc(smax_step, 1)
                    dve.wait_ge(smax_step, 4 * m + 2)
                    tt(small_stat("m"), small_stat("t"), mout_m, ALU.max).then_inc(smax_step, 1)
                    dve.wait_ge(smax_step, 4 * m + 3)
                    tt(small_stat("dm"), mout_m, small_stat("m"), ALU.subtract)
                    tt(small_stat("bias"), cs, small_stat("m"), ALU.subtract).then_inc(smax_step, 1)

                def small_split_pt(m):
                    dve.wait_ge(spt_hi, m + 1)
                    tt(pts_lo[:], ps[:, 1, 0:2 * P], pts_hi[:].bitcast(F32), ALU.subtract).then_inc(spt_lo, 1)

                def finish_small(m):
                    dve.wait_ge(sout_exp, m + 1)
                    tt(small_stat("z"), small_stat("out"), zout[:, bass.ds(2 * m, 2)], ALU.mult).then_inc(sz_step, 1)
                    dve.wait_ge(sz_step, 3 * m + 1)
                    tt(small_stat("z"), small_stat("z"), small_stat("zs"), ALU.add).then_inc(sz_step, 1)
                    dve.wait_ge(sz_step, 3 * m + 2)
                    nc.vector.reciprocal(small_stat("rz"), small_stat("z")).then_inc(sz_step, 1)
                    dve.wait_ge(spv_done, m + 1)
                    dve.wait_ge(normed, 4 * m + 4)
                    for u in range(2):
                        stt(res[:, 2 + u, :], bvs[:], small_stat("zs", u), ps[:, 7, u * F:(u + 1) * F], ALU.mult, ALU.add).then_inc(res_s, 1)
                    dve.wait_ge(sz_step, 3 * m + 3)
                    dve.wait_ge(xs_kept, 2 * m + 2)
                    for u in range(2):
                        dve.wait_ge(res_s, 2 * m + u + 1)
                        stt(res[:, 2 + u, :], res[:, 2 + u, :], small_stat("rz", u), y[:, 2 * m + u, :], ALU.mult, ALU.add).then_inc(so_step, 1)

                def body(m, first=False, last=False):
                    if not first:
                        split_pt(2 * m - 1, 0)
                        split_pt(2 * m - 1, 1)
                        make_scores(2 * m, 0, m, between=lambda: sums_dense(2 * m - 1, 1))
                        small_split_x(m)
                        finish_small(m - 1)
                        split_pt(2 * m - 1, 2)
                        small_split(m)
                        split_pt(2 * m - 1, 3)
                        finish_dense(2 * m - 1, 1)
                        results_stats(m - 1)
                    else:
                        make_scores(2 * m, 0, m)
                        small_split_x(m)
                        small_split(m)
                    split_pt(2 * m, 0)
                    make_scores(2 * m + 1, 1, m, between=lambda: split_pt(2 * m, 1))
                    if not last:
                        split_t(m + 1)
                    small_scores(m)
                    split_pt(2 * m, 2)
                    if not last:
                        small_residual(m + 1)
                    split_pt(2 * m, 3)
                    small_split_pt(m)
                    sums_dense(2 * m, 0)
                    finish_dense(2 * m, 0)

                for j in range(JT):
                    dve.wait_ge(at_ready[j], NC * NS - 2)
                nc.vector.reduce_sum(deg[:, DT:RT], degp[:, DT:RT, :], AX.X).then_inc(deg_ready, 1)
                dve.wait_ge(deg_ready, 1)
                nc.vector.reciprocal(rdeg[:, DT:RT], deg[:, DT:RT]).then_inc(deg_ready, 1)
                dve.wait_ge(deg_ready, 2)
                dve.wait_ge(again_loaded, 16)
                evacuate(NS - 1, NC - 2)
                dense_residual(0)
                dense_residual(1)
                normalise_dense(0)
                evacuate(NS - 1, NC - 1)
                dense_residual(2)
                normalise_dense(1)
                dense_residual(3)
                split_dense(0)
                take_sums(NS - 1)
                split_dense(1)
                nc.vector.tensor_reduce(lowest, least[:], AX.X, ALU.min).then_inc(mout_step, 1)
                dve.wait_ge(mout_step, 1)
                ts(mout, lowest, 2 * NEG, None, ALU.mult).then_inc(mout_step, 1)
                tt(least[:], least[:], lowest[:, :, None].to_broadcast((P, RT, NC)), ALU.subtract).then_inc(mout_step, 1)
                dve.wait_ge(acc_free, 4 * NS)
                for j in range(JT):
                    dve.wait_ge(at_ready[j], NC * NS)
                nc.vector.reduce_sum(deg[:, 0:DT], degp[:, 0:DT, :], AX.X).then_inc(small_deg_ready, 1)
                dve.wait_ge(small_deg_ready, 1)
                nc.vector.reciprocal(rdeg[:, 0:DT], deg[:, 0:DT]).then_inc(small_deg_ready, 1)
                dve.wait_ge(small_deg_ready, 2)
                value_dense(0)
                split_dense(2)
                small_residual(0, first=True)
                value_dense(1)
                split_dense(3)
                dve.wait_ge(mout_exp, 1)
                tt(zpart[:], zpart[:], least[:], ALU.mult).then_inc(mout_step, 1)
                dve.wait_ge(mout_step, 4)
                nc.vector.reduce_sum(zout, zpart[:], AX.X).then_inc(mout_step, 1)
                value_dense(2)
                split_t(0)
                value_dense(3)
                dve.wait_ge(vd_free, DT)
                dve.wait_ge(mout_step, 5)
                body(0, first=True)
                with dve.Fori(1, PAIRS - 1) as m:
                    body(m)
                body(PAIRS - 1, last=True)
                sums_dense(2 * PAIRS - 1, 1)
                for c in range(DC):
                    split_pt(2 * PAIRS - 1, c)
                finish_dense(2 * PAIRS - 1, 1)
                finish_small(PAIRS - 1)
                results_stats(PAIRS - 1)
            with dve.Else():
                evacuate(NS - 1, NC - 2)
                evacuate(NS - 1, NC - 1)
                for j in range(JT):
                    dve.wait_ge(at_ready[j], NC * NS)
                nc.vector.reduce_sum(deg[:], degp[:], AX.X).then_inc(deg_ready, 1)
                dve.wait_ge(deg_ready, 1)
                nc.vector.reciprocal(rdeg[:], deg[:]).then_inc(deg_ready, 1)
                dve.wait_ge(deg_ready, 2)
                take_sums(NS - 1)
                dve.wait_ge(acc_free, 4 * NS)
                dve.wait_ge(xre_loaded, 16)
                with dve.Fori(0, RT) as t:
                    nc.vector.scalar_tensor_tensor(y[:, t, :], y[:, t, :], rdeg[:, bass.ds(t, 1)], xre[:, t, :],
                                                   ALU.mult, ALU.add).then_inc(y_raw, 1)
                    dve.wait_ge(y_raw, t + 1)
                    nc.vector.bn_stats(bst[:, t, :], y[:, t, :]).then_inc(y_stats, 1)
                dve.wait_ge(y_stats, RT)
                d, m2, var, sd, mean, rsd = (lnt[:, q, :] for q in range(6))
                nc.vector.tensor_tensor(d, bst[:, :, 1], bst[:, :, 4], ALU.subtract)
                nc.vector.tensor_tensor(m2, bst[:, :, 2], bst[:, :, 5], ALU.add)
                nc.vector.tensor_tensor(mean, bst[:, :, 1], bst[:, :, 4], ALU.add).then_inc(ln, 1)
                dve.wait_ge(ln, 1)
                nc.vector.tensor_scalar(m2, m2, 1.0 / F, EPS, ALU.mult, ALU.add)
                nc.vector.tensor_scalar(mean, mean, 0.5, None, ALU.mult)
                nc.vector.scalar_tensor_tensor(d, d, 0.25, d, ALU.mult, ALU.mult).then_inc(ln, 1)
                dve.wait_ge(ln, 2)
                nc.vector.tensor_tensor(var, d, m2, ALU.add).then_inc(ln, 1)
                dve.wait_ge(std_ready, 1)
                nc.vector.reciprocal(rsd, sd).then_inc(ln, 1)
                dve.wait_ge(ln, 4)
                nc.vector.tensor_tensor(rsd, rsd, var, ALU.mult).then_inc(ln, 1)
                dve.wait_ge(ln, 5)
                nc.vector.tensor_tensor(rsd, rsd, sd, ALU.add).then_inc(ln, 1)
                dve.wait_ge(ln, 6)
                nc.vector.tensor_scalar(rsd, rsd, 0.5, None, ALU.mult).then_inc(ln, 1)
                dve.wait_ge(ln, 7)
                nc.vector.reciprocal(rsd, rsd).then_inc(ln, 1)
                dve.wait_ge(ln, 8)
                with dve.Fori(0, RT) as t:
                    nc.vector.tensor_scalar(y[:, t, :], y[:, t, :], lnt[:, 4, bass.ds(t, 1)], lnt[:, 5, bass.ds(t, 1)],
                                            ALU.subtract, ALU.mult).then_inc(xn_ready, 1)

                dve.wait_ge(g_loaded, 16 * 7)
                dve.wait_ge(xn_ready, RT)
                nc.vector.tensor_tensor(bkc2[:], bqc[:], bkc[:], ALU.mult).then_inc(g_bb, 1)
                nc.vector.tensor_copy(ptrf[0:NPTR, :], ptri[0:NPTR, :]).then_inc(g_ptrf, 1)
                dve.wait_ge(g_ptrf, 1)
                dve.wait_ge(g_iota, 1)
                nc.vector.tensor_scalar(geq[0:NPTR, :], iota[0:NPTR, :], ptrf[0:NPTR, 0:1], None, ALU.is_ge).then_inc(g_geq, 1)
                dve.wait_ge(g_gid_ps, 1)
                nc.vector.tensor_copy(gid_col[:], ps[:, 5, 0:RT]).then_inc(g_gid, 1)
                for c in range(NC):
                    dve.wait_ge(g_gid_ps, c + 2)
                    nc.vector.tensor_copy(gid_row[:, c * CW:(c + 1) * CW], ps[:, 6, :]).then_inc(g_gid, 1)
                dve.wait_ge(g_wsb, 1)
                for t in range(RT):
                    dve.wait_ge(g_v_ps, t + 1)
                    nc.vector.tensor_tensor(v[:, t, :], ps[:, 2 + t % 2, 0:F + 1], gbv[:], ALU.add).then_inc(g_v, 1)
                dve.wait_ge(g_gid, NC + 1)
                dve.wait_ge(g_v, RT)
                nc.vector.tensor_copy(crow[:], v[:, :, F]).then_inc(g_chain, 1)
                dve.wait_ge(g_chain, 1)
                nc.vector.memset(stat[:], 0.0).then_inc(g_max, 1)
                nc.vector.memset(gfin[:], 0.0).then_inc(g_fin, 1)
                LINKS = 3 * NC + 8
                with dve.Fori(0, RT) as i:
                    links = [0]

                    def link(ins):
                        links[0] += 1
                        ins.then_inc(g_chain, 1)
                        dve.wait_ge(g_chain, i * LINKS + (links[0] + 1))

                    gid_i, c_i = gid_col[:, bass.ds(i, 1)], crow[:, bass.ds(i, 1)]
                    dve.wait_ge(g_adj, 16 * i + 16)
                    for c in range(NC):
                        cols = slice(c * CW, (c + 1) * CW)
                        dve.wait_ge(g_s_ps, NC * i + c + 1)
                        link(nc.vector.scalar_tensor_tensor(inside[:], ps[:, c, :], c_i, adjr[:, cols], ALU.add, ALU.add))
                        nc.vector.tensor_scalar(sc[:, cols], adjr[:, cols], 2 * NEG, None, ALU.mult)
                        nc.vector.tensor_scalar(same[:], gid_row[:, cols], gid_i, None, ALU.is_equal)
                        link(nc.vector.tensor_tensor(inside[:], inside[:], adjr[:, cols], ALU.add))
                        nc.vector.memset(gsettled[:], 0.0)
                        link(nc.vector.copy_predicated(sc[:, cols], same[:].bitcast(I32), inside[:]))
                    nc.vector.tensor_reduce(stat[:, 0:1], sc[:], AX.X, ALU.max, negate=True).then_inc(g_max, 1)
                    dve.wait_ge(g_exp, i + 1)
                    nc.vector.scalar_tensor_tensor(sc[:], gid_row[:], gid_i, sc[:], ALU.is_equal, ALU.mult).then_inc(g_p, 1)
                    link(nc.vector.reciprocal(stat[:, 3:4], stat[:, 1:2]))
                    dve.wait_ge(g_o_ps, i + 1)
                    link(nc.vector.scalar_tensor_tensor(gres[:], ps[:, 0, 0:F], stat[:, 3:4], y[:, i, :], ALU.mult, ALU.add))
                    link(nc.vector.bn_stats(bstat[:], gres[:]))
                    nc.vector.memset(gsettled[:], 0.0)
                    link(nc.vector.bn_aggr(stat[:, 6:8], bstat[:]))
                    nc.vector.tensor_scalar(stat[:, 4:5], stat[:, 7:8], EPS, None, ALU.add).then_inc(g_var, 1)
                    dve.wait_ge(g_std, i + 1)
                    link(nc.vector.reciprocal(stat[:, 9:10], stat[:, 5:6]))
                    link(nc.vector.scalar_tensor_tensor(stat[:, 9:10], stat[:, 9:10], stat[:, 4:5], stat[:, 5:6], ALU.mult, ALU.add))
                    link(nc.vector.tensor_scalar(stat[:, 9:10], stat[:, 9:10], 0.5, None, ALU.mult))
                    link(nc.vector.reciprocal(stat[:, 10:11], stat[:, 9:10]))
                    nc.vector.tensor_scalar(gfin[:], gres[:], stat[:, 6:7], stat[:, 10:11], ALU.subtract, ALU.mult).then_inc(g_fin, 1)
                    assert links[0] == LINKS, links


def kernel(x, adj, L0_gnn_W, L0_gnn_b, L1_gnn_ptr, L1_gnn_Wq, L1_gnn_bq, L1_gnn_Wk, L1_gnn_bk, L1_gnn_Wv, L1_gnn_bv):
    import numpy as np
    import concourse.bacc as bacc
    from concourse.bass_utils import run_bass_kernel_spmd

    nc = bacc.Bacc("TRN2", target_bir_lowering=False, num_devices=1)
    arrays, args = {}, []
    for name, a in dict(x=x, adj=adj, W0=L0_gnn_W, b0=L0_gnn_b, ptr=L1_gnn_ptr, Wq=L1_gnn_Wq, bq=L1_gnn_bq,
                        Wk=L1_gnn_Wk, bk=L1_gnn_bk, Wv=L1_gnn_Wv, bv=L1_gnn_bv).items():
        a = np.ascontiguousarray(a)
        arrays[f"in_{name}"] = a
        args.append(nc.dram_tensor(f"in_{name}", a.shape, mybir.dt.from_np(a.dtype), kind="ExternalInput").ap())
    out = nc.dram_tensor("out", tuple(x.shape), mybir.dt.float32, kind="ExternalOutput").ap()
    gnn_then_graph_attention(nc, *args, out)
    r = run_bass_kernel_spmd(nc, [arrays], core_ids=[0])
    return r.results[0]["out"]
```

```python
import concourse.bass as bass
from concourse import mybir
from contextlib import ExitStack


def gnn_then_graph_attention(nc, x, adj, W0, b0, ptr, Wq, bq, Wk, bk, Wv, bv, out):
    F32, F32R, BF16, I32 = mybir.dt.float32, mybir.dt.float32r, mybir.dt.bfloat16, mybir.dt.int32
    ALU, ACT, AX = mybir.AluOpType, mybir.ActivationFunctionType, mybir.AxisListType

    P = 128
    N, F = x.shape
    NPTR = ptr.shape[0]
    GRAPH = 2048 // (NPTR - 1)
    KT = F // P
    RT = N // P
    ST = 8
    NS = RT // ST
    CW = 512
    NC = N // CW
    JT = CW // P
    SLOTS = 4
    DT = (NPTR - 1) * GRAPH // P
    DN = N - DT * P
    DC = DN // CW
    PAIRS = DT // 2
    assert DT == RT // 2 and 2 * GRAPH == P
    SCALE = float(F) ** -0.5
    EPS = 1e-5
    OUTSIDE = 1e30
    NEG = -1e6
    BLOCKS = (2, 3, 0, 1)

    adj_chunks = adj.rearrange("(s t p) (c w) -> s c p t w", t=ST, p=P, w=CW)
    x_tiles = x.rearrange("(t p) f -> p t f", p=P)
    out_tiles = out.rearrange("(t p) f -> t p f", p=P)
    out_pairs = out.rearrange("(m e p) f -> m p e f", e=2, p=P)
    adj_rows = adj.rearrange("(t p) j -> t p j", p=P)
    adj_blocks = adj.rearrange("(t p) (u q) -> t u p q", p=P, q=P)

    def column_chunk(n):
        return (n + NC - DC) & (NC - 1)

    def has_outside(s, n):
        return BLOCKS[s] < 2 or n >= DC

    def outside_count(s, n):
        return sum(has_outside(a, b) for a in range(NS) for b in range(NC) if (a, b) <= (s, n))

    ctx = ExitStack()
    with ctx:
        def sem(name):
            return ctx.enter_context(nc.semaphore(name))

        def tensors(stack):
            return lambda name, shape, dt: stack.enter_context(nc.sbuf_tensor(name, shape, dt))

        sb = tensors(ctx)
        y = sb("y", [P, RT, F], F32)
        ident = sb("ident", [P, P], F32)
        identb = sb("identb", [P, P], BF16)
        zerob = sb("zerob", [P, CW], BF16)
        degp = sb("degp", [P, RT, NS], F32)
        deg = sb("deg", [P, RT], F32)
        rdeg = sb("rdeg", [P, RT], F32)
        least = sb("least", [P, RT, NC], F32)
        zpart = sb("zpart", [P, RT, NC], F32)
        ebias = sb("ebias", [P, SLOTS, ST], F32)
        g_hi = sb("g_hi", [P, KT, F], F32R)
        g_lo = sb("g_lo", [P, KT, F], F32R)
        wv_hi = sb("wv_hi", [P, KT, F + 2], F32R)
        wv_lo = sb("wv_lo", [P, KT, F + 2], F32R)
        gv = sb("gv", [P, KT], F32)
        bqbk = sb("bqbk", [P, 1], F32)
        bvs = sb("bvs", [P, F], F32)
        half_stats = sb("half_stats", [P, 16 + 2 + 4, 6], F32)
        row_stats = sb("row_stats", [P, 160], F32)
        row_consts = sb("row_consts", [P, 128], F32)
        consts = sb("consts", [P, 4, 8], F32)
        settled = sb("settled", [P, 4], F32)
        irregular = sb("irregular", [1, 1], I32)
        ps = ctx.enter_context(nc.psum_tensor("ps", [P, 8, 512], F32))

        layer1 = ExitStack()
        sb1 = tensors(layer1)
        hid = sb1("hid", [P, RT, 2 * F], F32R)
        adjb = sb1("adjb", [P, SLOTS, ST, CW], F32)
        anat = sb1("anat", [P, 2, ST, CW], BF16)
        at = sb1("at", [P, JT, ST * P], F32R)
        layer1.close()
        early = ExitStack()
        sbe = tensors(early)
        sbe("hid_", [P, RT, 2 * F], F32R)
        sbe("adjb_", [P, SLOTS, ST, CW], F32)
        sbe("anat_", [P, ST, CW], BF16)
        hsum = sbe("hsum", [P, 4, F], F32)
        w0_hi = sbe("w0_hi", [P, KT, F], F32R)
        w0_lo = sbe("w0_lo", [P, KT, F], F32R)
        xT_hi = sbe("xT_hi", [P, 2, KT, 4 * P], F32R)
        xT_lo = sbe("xT_lo", [P, 2, KT, 4 * P], F32R)
        early.close()
        wq_in, wk_in, wv_in = (adjb[:, 3, q, :].rearrange("p (k f) -> p k f", k=KT) for q in range(3))
        vecs = adjb[:, 3, 3, :]
        bq_in, bk_in, bb_in = vecs[:, 0:2], vecs[:, 2:4], vecs[:, 4:6]
        ptr_f, ptr_d = vecs[0:NPTR, 6:7], vecs[0:NPTR, 7:8]
        ptr_in, ptr_want = vecs[0:NPTR, 8:9].bitcast(I32), vecs[0:NPTR, 9:10].bitcast(I32)
        ones_in = adjb[:, 3, 4, 0:P]
        wcols = adjb[:, 3, 5, 0:8]
        b0b = adjb[:, 3, 6, 0:F]
        w0f = adjb[:, 3, 7, :].rearrange("p (k f) -> p k f", k=KT)

        regular = ExitStack()
        sbr = tensors(regular)
        xd_hi = sbr("xd_hi", [P, KT, DN], F32R)
        xd_lo = sbr("xd_lo", [P, KT, DN], F32R)
        vd = sbr("vd", [P, DN // P, 2 * F], F32R)
        td_hi = sbr("td_hi", [P, KT, 2 * P], F32R)
        td_lo = sbr("td_lo", [P, KT, 2 * P], F32R)
        res = sbr("res", [P, 4, F], F32)
        fin = sbr("fin", [P, 4, F], F32)
        ts_hi = sbr("ts_hi", [P, KT, 2 * P], F32R)
        ts_lo = sbr("ts_lo", [P, KT, 2 * P], F32R)
        xs_again = sbr("xs_again", [P, DT, F], F32)
        adjd = sbr("adjd", [P, 2, DN], F32)
        ptd_hi = sbr("ptd_hi", [P, 2, CW], F32R)
        ptd_lo = sbr("ptd_lo", [P, 2, CW], F32R)
        sadj = sbr("sadj", [P, 2, P], F32)
        sadjm = sbr("sadjm", [P, 2, P], F32)
        cross = sbr("cross", [P, 2, P], F32)
        xs = sbr("xs", [P, 2, F], F32)
        regular_fill = sbr("regular_fill", [P, 2 * ST * CW - 2 * DN - 4 * CW - 6 * P - 2 * F], F32)
        xst_hi = sbr("xst_hi", [P, KT, 2 * P], F32R)
        xst_lo = sbr("xst_lo", [P, KT, 2 * P], F32R)
        vs_hi = sbr("vs_hi", [P, 2, F], F32R)
        vs_lo = sbr("vs_lo", [P, 2, F], F32R)
        small_p = sbr("small_p", [P, 2, P], F32)
        pts_hi = sbr("pts_hi", [P, 2 * P], F32R)
        pts_lo = sbr("pts_lo", [P, 2 * P], F32R)
        small_raw = sbr("small_raw", [P, 2, F], F32)
        a_fill = sbr("a_fill", [P, 4096 - 4 * KT * P - 4 * F - 2 * P - 4 * P - 2 * F], F32)
        scd = sbr("scd", [P, 2, DN], F32)
        regular.close()
        again = adjb[:, 0, :, :].rearrange("p t w -> p (t w)").rearrange("p (t f) -> p t f", f=F)

        general = ExitStack()
        sbg = tensors(general)
        xT = sbg("xT", [P, KT, N], F32)
        v = sbg("v", [P, RT, F + 1], F32)
        gid_row = sbg("gid_row", [P, N], F32)
        gid_col = sbg("gid_col", [P, RT], F32)
        adjr = sbg("adjr", [P, N], F32)
        sc = sbg("sc", [P, N], F32)
        pT = sbg("pT", [P, RT, P], F32)
        tT = sbg("tT", [P, KT, P], F32)
        inside = sbg("inside", [P, CW], F32)
        same = sbg("same", [P, CW], F32)
        wqf = sbg("wqf", [P, KT, F], F32)
        wkf = sbg("wkf", [P, KT, F], F32)
        wvf = sbg("wvf", [P, KT, F], F32)
        gmat = sbg("gmat", [P, KT, F], F32)
        wvT = sbg("wvT", [P, KT, F + 1], F32)
        bqc = sbg("bqc", [P, KT], F32)
        bkc = sbg("bkc", [P, KT], F32)
        gvec = sbg("gvec", [P, KT], F32)
        gbv = sbg("bvb", [P, F + 1], F32)
        crow = sbg("crow", [P, RT], F32)
        ptri = sbg("ptri", [64, 1], I32)
        ptrf = sbg("ptrf", [64, 1], F32)
        iota = adjr[0:64, :].bitcast(I32)
        geq = sc[0:64, :]
        ones = sbg("ones", [P, P], F32)
        gsettled = sbg("gsettled", [P, 1], F32)
        bkc2 = sbg("bkc2", [P, KT], F32)
        stat = sbg("stat", [P, 16], F32)
        gres = sbg("gres", [P, F], F32)
        gfin = sbg("gfin", [P, F], F32)
        bstat = sbg("bstat", [P, 6], F32)
        general.close()

        lnb = ExitStack()
        sbl = tensors(lnb)
        xre = sbl("xre", [P, RT, F], F32)
        bst = sbl("bst", [P, RT, 6], F32)
        lnt = sbl("lnt", [P, 6, RT], F32)
        lnb.close()

        ident_ready = sem("ident_ready")
        identb_ready = sem("identb_ready")
        ident_zeroed = sem("ident_zeroed")
        x_loaded = [sem(f"x_loaded{q}") for q in range(5)]
        w0_loaded = sem("w0_loaded")
        w0_split = sem("w0_split")
        xt_done = sem("xt_done")
        xt_hi_ready = sem("xt_hi_ready")
        xt_lo_ready = sem("xt_lo_ready")
        hid_done = sem("hid_done")
        hsum_ready = sem("hsum_ready")
        hid_hi_ready = sem("hid_hi_ready")
        hid_lo_ready = sem("hid_lo_ready")
        slot_loaded = [sem(f"slot_loaded{q}") for q in range(SLOTS)]
        a_ready = sem("a_ready")
        t_done = sem("t_done")
        at_ready = [sem(f"at_ready{j}") for j in range(JT)]
        mm_done = sem("mm_done")
        acc_free = sem("acc_free")
        y_raw = sem("y_raw")
        y_stats = sem("y_stats")
        xre_loaded = sem("xre_loaded")
        deg_ready = sem("deg_ready")
        ln = sem("ln")
        std_ready = sem("std_ready")
        xn_ready = sem("xn_ready")

        g_loaded = sem("g_loaded")
        g_ones = sem("g_ones")
        g_iota = sem("g_iota")
        g_ptrf = sem("g_ptrf")
        g_geq = sem("g_geq")
        g_bb = sem("g_bb")
        g_wps = sem("g_wps")
        g_wsb = sem("g_wsb")
        g_gid_ps = sem("g_gid_ps")
        g_gid = sem("g_gid")
        g_xt_ps = sem("g_xt_ps")
        g_xt = sem("g_xt")
        g_v_ps = sem("g_v_ps")
        g_v = sem("g_v")
        g_adj = sem("g_adj")
        g_t_ps = sem("g_t_ps")
        g_t = sem("g_t")
        g_s_ps = sem("g_s_ps")
        g_chain = sem("g_chain")
        g_max = sem("g_max")
        g_exp = sem("g_exp")
        g_p = sem("g_p")
        g_pt_ps = sem("g_pt_ps")
        g_pt = sem("g_pt")
        g_o_ps = sem("g_o_ps")
        g_var = sem("g_var")
        g_std = sem("g_std")
        g_fin = sem("g_fin")
        g_stored = sem("g_stored")
        g_out = sem("g_out")

        weights_loaded = sem("weights_loaded")
        ones_ready = sem("ones_ready")
        weights_sums = sem("weights_sums")
        weights_products = sem("weights_products")
        weights_hi = sem("weights_hi")
        weights_split = sem("weights_split")
        ptr_step = sem("ptr_step")
        ptr_far = sem("ptr_far")
        branch_ready = sem("branch_ready")
        outside_cleared = sem("outside_cleared")
        masked = sem("masked")
        least_ready = sem("least_ready")
        ebias_ready = sem("ebias_ready")
        outside_done = sem("outside_done")

        again_loaded = sem("again_loaded")
        small_again_loaded = sem("small_again_loaded")
        consts_ready = sem("consts_ready")
        cross_ready = sem("cross_ready")
        dense_residual_rest = sem("dense_residual_rest")
        dense_stats_ready = sem("dense_stats_ready")
        pool_step = sem("pool_step")
        dense_rstd_ready = sem("dense_rstd_ready")
        dense_x_ready = [sem(f"dense_x_ready{q}") for q in range(2)]
        dense_deg_ready = sem("dense_deg_ready")
        small_deg_ready = sem("small_deg_ready")
        sums_done = sem("sums_done")
        dense_residual_first = sem("dense_residual_first")
        dense_scaled = sem("dense_scaled")
        xd_ps = sem("xd_ps")
        xd_hi_ready = sem("xd_hi_ready")
        xd_lo_ready = sem("xd_lo_ready")
        vd_ps = sem("vd_ps")
        vd_hi_ready = sem("vd_hi_ready")
        vd_free = sem("vd_free")
        out_step = sem("out_step")
        out_weights = sem("out_weights")
        adjd_loaded = [sem(f"adjd_loaded{e}") for e in range(2)]
        sadj_loaded = sem("sadj_loaded")
        sadj_masked = sem("sadj_masked")
        t_ps = sem("t_ps")
        t_hi = sem("t_hi")
        t_lo = sem("t_lo")
        s_ps = sem("s_ps")
        scores = sem("scores")
        max_step = sem("max_step")
        probs = sem("probs")
        out_exp = sem("out_exp")
        z_step = sem("z_step")
        pt_ps = sem("pt_ps")
        pt_hi = sem("pt_hi")
        pt_lo = sem("pt_lo")
        pv_done = sem("pv_done")
        o_step = sem("o_step")
        res_d = sem("res_d")
        res_s = sem("res_s")
        bn_ready = sem("bn_ready")
        rstd_ready = sem("rstd_ready")
        normed = sem("normed")
        fin_free = sem("fin_free")
        stored = sem("stored")
        small_raw_ready = sem("small_raw_ready")
        small_stats_ready = sem("small_stats_ready")
        small_rstd_ready = sem("small_rstd_ready")
        xs_ready = sem("xs_ready")
        xs_kept = sem("xs_kept")
        xst_ps = sem("xst_ps")
        xst_hi_ready = sem("xst_hi_ready")
        xst_lo_ready = sem("xst_lo_ready")
        ts_ps = sem("ts_ps")
        ts_hi_ready = sem("ts_hi_ready")
        ts_lo_ready = sem("ts_lo_ready")
        vs_ps = sem("vs_ps")
        vs_hi_ready = sem("vs_hi_ready")
        vs_lo_ready = sem("vs_lo_ready")
        ss_ps = sem("ss_ps")
        sscores = sem("sscores")
        smax_step = sem("smax_step")
        sprobs = sem("sprobs")
        sout_exp = sem("sout_exp")
        sz_step = sem("sz_step")
        spt_ps = sem("spt_ps")
        spt_hi = sem("spt_hi")
        spt_lo = sem("spt_lo")
        spv_done = sem("spv_done")
        so_step = sem("so_step")

        block = ctx.enter_context(nc.Block())

        def hid_bank(g, q):
            return 4 + 2 * (g % 2) + q // 2, (q % 2) * F

        DG = DT // 4
        RSTD_GROUPS = ((0, 8), (8, 12), (12, 16))

        def dense_stat(e, name):
            at_, n = dict(z4=(0, 4), mx4=(4, 4), mx=(8, 1), m=(9, 1), bias=(10, 1), out=(11, 1), zs=(12, 1),
                          z=(13, 1), rz=(14, 1))[name]
            return row_stats[:, 16 * e + at_:16 * e + at_ + n]

        def small_stat(name, u=None):
            at_ = 32 + 2 * ("mx", "t", "m", "bias", "dm", "out", "zs", "z", "rz").index(name)
            return row_stats[:, at_:at_ + 2] if u is None else row_stats[:, at_ + u:at_ + u + 1]

        rstd_d, shift_d = row_stats[:, 50:66], row_stats[:, 66:82]
        rstd_s, shift_s = row_stats[:, 82:84], row_stats[:, 84:86]
        rstd_r, shift_r = row_stats[:, 86:90], row_stats[:, 90:94]
        scratch = [[row_stats[:, 94 + 24 * par + 8 * q:102 + 24 * par + 8 * q] for q in range(3)] for par in range(2)]
        out_max, out_sum, dense_const, small_const, lowest = row_consts[:, 0:RT], row_consts[:, RT:2 * RT], row_consts[:, 64:80], row_consts[:, 80:82], row_consts[:, 96:96 + RT]

        x_parts = ((0, 1), (1, 2), (2, 4), (4, 6), (6, 8))

        @block.sync
        def _(sp):
            for q, (a, z) in enumerate(x_parts):
                sp.dma_start(y[:, 4 * a:4 * z, :], x_tiles[:, 4 * a:4 * z, :]).then_inc(x_loaded[q], 16)
                if q == 0:
                    sp.dma_start(w0f, W0.rearrange("(k p) f -> p k f", p=P)).then_inc(w0_loaded, 16)
                    sp.dma_start(b0b, b0[None, :].to_broadcast((P, F))).then_inc(w0_loaded, 16)
            for w, dram in ((wq_in, Wq), (wk_in, Wk), (wv_in, Wv)):
                sp.dma_start(w, dram.rearrange("(k p) f -> p k f", p=P)).then_inc(weights_loaded, 16)
            with nc.allow_non_contiguous_dma("short columns"):
                sp.dma_start(bq_in, bq.rearrange("(k p) -> p k", p=P)).then_inc(weights_loaded, 16)
                sp.dma_start(bk_in, bk.rearrange("(k p) -> p k", p=P)).then_inc(weights_loaded, 16)
                sp.dma_start(ptr_in, ptr[:, None]).then_inc(weights_loaded, 16)
            sp.dma_start(bvs[:], bv[None, :].to_broadcast((P, F))).then_inc(weights_loaded, 16)
            for s in range(NS):
                for n in range(NC):
                    k = NC * s + n
                    if k >= SLOTS:
                        before = divmod(k - SLOTS, NC)
                        sp.wait_ge(a_ready, k - SLOTS + 1)
                        if has_outside(*before):
                            sp.wait_ge(outside_done, outside_count(*before))
                    if k == SLOTS - 1:
                        sp.wait_ge(weights_split, 2)
                        sp.wait_ge(branch_ready, 1)
                    sp.dma_start(adjb[:, n % SLOTS], adj_chunks[BLOCKS[s], column_chunk(n)]).then_inc(slot_loaded[n % SLOTS], 16)

            sp.wait_ge(branch_ready, 1)
            flag = sp.value_load(irregular[0:1, 0:1], min_val=0, max_val=1)
            with sp.If(flag == 0):
                outside_all = outside_count(NS - 1, NC - 1)
                sp.wait_ge(outside_done, outside_all - 3)
                sp.dma_start(again, x_tiles[:, DT:RT, :]).then_inc(again_loaded, 16)
                sp.wait_ge(outside_done, outside_all - 2)
                sp.dma_start(xs_again[:], x_tiles[:, 0:DT, :]).then_inc(small_again_loaded, 16)
                sp.wait_ge(outside_done, outside_all)

                def load_dense(i, e):
                    sp.dma_start(adjd[:, e, :], adj_rows[i + DT, :, DT * P:N]).then_inc(adjd_loaded[e], 16)

                def load_small(m):
                    for u in range(2):
                        sp.dma_start(sadj[:, u, :], adj_blocks[2 * m + u, 2 * m + u]).then_inc(sadj_loaded, 16)

                def store(m):
                    sp.wait_ge(normed, 4 * m + 8)
                    sp.dma_start(out_pairs[m + PAIRS], fin[:, 0:2, :]).then_inc(stored, 16)
                    sp.dma_start(out_pairs[m], fin[:, 2:4, :]).then_inc(stored, 16)
                    sp.wait_ge(stored, 32 * m + 32)
                    sp.sem_inc(fin_free, 1)

                def body(m, first=False, last=False):
                    if not last:
                        sp.wait_ge(sadj_masked, m + 1)
                        load_small(m + 1)
                        for e in range(2):
                            sp.wait_ge(scores, 8 * m + 4 * e + 4)
                            load_dense(2 * m + 2 + e, e)
                    if not first:
                        store(m - 1)

                load_dense(0, 0)
                load_dense(1, 1)
                load_small(0)
                body(0, first=True)
                with sp.Fori(1, PAIRS - 1) as m:
                    body(m)
                body(PAIRS - 1, last=True)
                for rows, rows_of, count in ((out_pairs[PAIRS - 1], slice(2, 4), 4 * PAIRS + 2),
                                             (out_pairs[2 * PAIRS - 1], slice(0, 2), 4 * PAIRS + 4)):
                    sp.wait_ge(normed, count)
                    sp.dma_start(rows, fin[:, rows_of, :]).then_inc(stored, 16)
                sp.wait_ge(stored, 32 * PAIRS)
            with sp.Else():
                sp.wait_ge(mm_done, JT * NC * NS)
                sp.dma_start(xre[:], x_tiles).then_inc(xre_loaded, 16)
                sp.wait_ge(xn_ready, RT)
                sp.dma_start(wqf[:], Wq.rearrange("(k p) f -> p k f", p=P)).then_inc(g_loaded, 16)
                sp.dma_start(wkf[:], Wk.rearrange("(k p) f -> p k f", p=P)).then_inc(g_loaded, 16)
                sp.dma_start(wvf[:], Wv.rearrange("(k p) f -> p k f", p=P)).then_inc(g_loaded, 16)
                with nc.allow_non_contiguous_dma("two short columns"):
                    sp.dma_start(bqc[:], bq.rearrange("(k p) -> p k", p=P)).then_inc(g_loaded, 16)
                    sp.dma_start(bkc[:], bk.rearrange("(k p) -> p k", p=P)).then_inc(g_loaded, 16)
                sp.dma_start(gbv[:, 0:F], bv[None, :].to_broadcast((P, F))).then_inc(g_loaded, 16)
                sp.dma_start(ptri[0:NPTR, :], ptr[:, None]).then_inc(g_loaded, 16)
                with sp.Fori(0, RT) as i:
                    sp.wait_ge(g_max, i + 1)
                    sp.dma_start(adjr[:], adj_rows[i]).then_inc(g_adj, 16)
                    sp.wait_ge(g_fin, i + 2)
                    sp.dma_start(out_tiles[i], gfin[:]).then_inc(g_out, 16)
                    sp.wait_ge(g_out, 16 * i + 16)
                    sp.sem_inc(g_stored, 1)

        @block.gpsimd
        def _(pool):
            nc.gpsimd.memset(ident[:], 0.0).then_inc(ident_zeroed, 1)
            nc.gpsimd.memset(zerob[:], 0.0).then_inc(ident_zeroed, 1)
            nc.gpsimd.memset(ones_in, 1.0).then_inc(ones_ready, 1)
            nc.gpsimd.iota(ptr_want, pattern=[[0, 1]], base=0, channel_multiplier=GRAPH).then_inc(ones_ready, 1)
            pool.wait_ge(ident_zeroed, 2)
            nc.gpsimd.affine_select(out=ident[:], in_=ident[:], compare_op=ALU.not_equal, fill=1.0, base=0,
                                    pattern=[[-1, P]], channel_multiplier=1).then_inc(ident_ready, 1)
            nc.gpsimd.memset(least[:], OUTSIDE).then_inc(outside_cleared, 1)
            nc.gpsimd.memset(zpart[:], 0.0).then_inc(outside_cleared, 1)
            for q, value in enumerate((float(F // 4) ** 0.5, F * EPS, float(F) ** 0.5, -0.5)):
                last = nc.gpsimd.memset(consts[:, q, :], value)
            last.then_inc(consts_ready, 1)
            pool.wait_ge(slot_loaded[0], 16)
            nc.gpsimd.tensor_scalar(anat[:, 0], adjb[:, 0], 0.0, 1.0, ALU.is_equal, ALU.is_lt).then_inc(a_ready, 1)
            def mask_diagonal(i):
                s, n = BLOCKS.index(i // 2), DC + i
                pool.wait_ge(a_ready, NC * s + n + 1)
                for h in range(2):
                    rows = slice(h * GRAPH, (h + 1) * GRAPH)
                    for q in range(JT):
                        cols = slice(q * P + h * GRAPH, q * P + (h + 1) * GRAPH)
                        last = nc.gpsimd.memset(adjb[rows, n % SLOTS, JT * (i % 2) + q, cols], OUTSIDE)
                last.then_inc(masked, 1)

            for i in range(3):
                mask_diagonal(i)

            pool.wait_ge(branch_ready, 1)
            flag = pool.value_load(irregular[0:1, 0:1], min_val=0, max_val=1)
            with pool.If(flag == 0):
                pool.wait_ge(consts_ready, 1)
                half_d, f_eps, root_f, minus_half = (consts[:, q, :] for q in range(4))

                def reciprocal_std(group, par, n, stats, rstd, shift, ready):
                    d, v, mean = (q[:, 0:n] for q in scratch[par])
                    step = [6 * group]

                    def link(ins):
                        step[0] = step[0] + 1
                        ins.then_inc(pool_step, 1)
                        pool.wait_ge(pool_step, step[0])

                    tt = nc.gpsimd.tensor_tensor
                    tt(d, stats[:, :, 1], stats[:, :, 4], ALU.subtract)
                    tt(v, stats[:, :, 2], stats[:, :, 5], ALU.add)
                    link(tt(mean, stats[:, :, 1], stats[:, :, 4], ALU.add))
                    tt(d, d, half_d[:, 0:n], ALU.mult)
                    tt(v, v, f_eps[:, 0:n], ALU.add)
                    link(tt(mean, mean, minus_half[:, 0:n], ALU.mult))
                    link(tt(d, d, d, ALU.mult))
                    link(tt(v, v, d, ALU.add))
                    link(tt(rstd, v, minus_half[:, 0:n], ALU.pow))
                    link(tt(rstd, rstd, root_f[:, 0:n], ALU.mult))
                    tt(shift, mean, rstd, ALU.mult).then_inc(ready, 1)

                def mask_small(m):
                    pool.wait_ge(sadj_loaded, 32 * m + 32)
                    if not (isinstance(m, int) and m == 0):
                        pool.wait_ge(sscores, m)
                    nc.gpsimd.tensor_tensor(sadjm[:], sadj[:], cross[:], ALU.add).then_inc(sadj_masked, 1)

                pool.wait_ge(dense_deg_ready, 2)
                pool.wait_ge(again_loaded, 16)
                pool.wait_ge(masked, 3)
                for t in range(8):
                    if t == 4:
                        pool.wait_ge(dense_residual_first, t)
                        mask_diagonal(3)
                        pool.wait_ge(masked, 4)
                    y_t = y[:, DT + t, :]
                    nc.gpsimd.tensor_scalar(y_t, y_t, rdeg[:, DT + t:DT + t + 1], None, ALU.mult).then_inc(dense_scaled, 1)
                    pool.wait_ge(dense_scaled, t + 1)
                    nc.gpsimd.tensor_tensor(y_t, y_t, again[:, t, :], ALU.add).then_inc(dense_residual_first, 1)
                for g, (a, z) in enumerate(RSTD_GROUPS):
                    pool.wait_ge(dense_stats_ready, z)
                    reciprocal_std(g, g % 2, z - a, half_stats[:, a:z, :], rstd_d[:, a:z], shift_d[:, a:z], dense_rstd_ready)
                before = len(RSTD_GROUPS)
                pool.wait_ge(outside_done, outside_count(NS - 1, NC - 1))
                nc.gpsimd.memset(cross[:], 0.0).then_inc(cross_ready, 1)
                pool.wait_ge(cross_ready, 1)
                nc.gpsimd.memset(cross[0:GRAPH, :, GRAPH:P], -OUTSIDE)
                nc.gpsimd.memset(cross[GRAPH:P, :, 0:GRAPH], -OUTSIDE).then_inc(cross_ready, 1)
                pool.wait_ge(cross_ready, 2)
                pool.wait_ge(small_stats_ready, 2)
                reciprocal_std(before, 1, 2, half_stats[:, 16:18, :], rstd_s, shift_s, small_rstd_ready)
                mask_small(0)
                nc.gpsimd.memset(fin[:, 0, 0:1], 0.0).then_inc(normed, 4)
                nc.gpsimd.memset(fin[:, 1, 0:1], 0.0).then_inc(fin_free, 1)

                def results_std(m, group, par, a=0, z=4):
                    pool.wait_ge(bn_ready, 4 * m + (2 if a else 4))
                    reciprocal_std(group, par, z - a, half_stats[:, 18 + a:18 + z, :], rstd_r[:, a:z], shift_r[:, a:z], rstd_ready)

                def body(m, first=False, last=False):
                    if not first:
                        results_std(m - 1, before + 2 * m, 1)
                    if not last:
                        pool.wait_ge(small_stats_ready, 2 * m + 4)
                        reciprocal_std(before + 1 + 2 * m, 0, 2, half_stats[:, 16:18, :], rstd_s, shift_s, small_rstd_ready)
                        mask_small(m + 1)

                body(0, first=True)
                with pool.Fori(1, PAIRS - 1) as m:
                    body(m)
                body(PAIRS - 1, last=True)
                results_std(PAIRS - 1, before + 2 * PAIRS - 1, 0, a=2)
                results_std(PAIRS - 1, before + 2 * PAIRS, 1, z=2)
            with pool.Else():
                mask_diagonal(3)
                pool.wait_ge(masked, 4)
                pool.wait_ge(xn_ready, RT)
                nc.gpsimd.memset(ones[:], 1.0).then_inc(g_ones, 1)
                nc.gpsimd.iota(iota[0:NPTR, :], pattern=[[1, N]], base=0, channel_multiplier=0).then_inc(g_iota, 1)

        @block.tensor
        def _(pe):
            def hi_lo_passes(operands):
                (a_hi, a_lo), (b_hi, b_lo) = operands
                return [(a, b, k) for a, b in ((a_hi, b_hi), (a_hi, b_lo), (a_lo, b_hi)) for k in range(KT)]

            def product(out_, passes, stationary, moving):
                for i, (a, b, k) in enumerate(passes):
                    last = nc.tensor.matmul(out_, stationary(a, k), moving(b, k), start=(i == 0), stop=(i == len(passes) - 1))
                return last

            pe.wait_ge(ident_ready, 1)

            def transpose_x(g):
                for q, (a, _) in enumerate(x_parts):
                    if a == g:
                        pe.wait_ge(x_loaded[q], 16)
                if g >= 2:
                    pe.wait_ge(xt_lo_ready, 2 * (g - 1))
                for k in range(KT):
                    for q in range(4):
                        last = nc.tensor.transpose(ps[:, 2 * (g % 2) + k, q * P:(q + 1) * P],
                                                   y[:, 4 * g + q, k * P:(k + 1) * P], ident[:])
                    last.then_inc(xt_done, 1)

            def hidden(g):
                if g == 0:
                    pe.wait_ge(w0_split, 2)
                pe.wait_ge(xt_lo_ready, 2 * (g + 1))
                if g >= 2:
                    pe.wait_ge(hsum_ready, 2 * (g - 1))
                for q in range(4):
                    bank, col = hid_bank(g, q)
                    product(ps[:, bank, col:col + F], hi_lo_passes(((xT_hi, xT_lo), (w0_hi, w0_lo))),
                            lambda xt, k: xt[:, g % 2, k, q * P:(q + 1) * P],
                            lambda w, k: w[:, k, :]).then_inc(hid_done, 1)

            def weights():
                pe.wait_ge(weights_loaded, 16 * 7)
                pe.wait_ge(ones_ready, 2)
                pe.wait_ge(xt_lo_ready, KT * RT // 4)
                pe.wait_ge(weights_products, 1)
                for m in range(KT):
                    cols = slice(m * P, (m + 1) * P)
                    for k in range(KT):
                        nc.tensor.matmul(ps[:, 0, m * F:(m + 1) * F], wq_in[:, k, cols], wk_in[:, k, :],
                                         start=(k == 0), stop=(k == KT - 1))
                    for k in range(KT):
                        nc.tensor.transpose(ps[:, 1, m * F + k * P:m * F + (k + 1) * P], wv_in[:, k, cols], ident[:])
                for m in range(KT):
                    cols = slice(m * P, (m + 1) * P)
                    for col, w, b in ((m, wk_in, bq_in), (KT + m, wq_in, bk_in)):
                        for k in range(KT):
                            nc.tensor.matmul(ps[:, 2, col:col + 1], w[:, k, cols], b[:, k:k + 1],
                                             start=(k == 0), stop=(k == KT - 1))
                for k in range(KT):
                    nc.tensor.matmul(ps[:, 2, 4:5], ones_in, bb_in[:, k:k + 1], start=(k == 0), stop=(k == KT - 1))
                pe.wait_ge(ptr_far, 1)
                nc.tensor.matmul(ps[0:1, 2, 5:6], ones_in[0:NPTR, 0:1], ptr_d, start=True, stop=True).then_inc(weights_sums, 1)

            transpose_x(0)
            for g in range(RT // 4):
                if g + 1 < RT // 4:
                    transpose_x(g + 1)
                hidden(g)
            weights()

            pe.wait_ge(identb_ready, 1)
            pe.wait_ge(hsum_ready, RT // 2)

            def transposes(k, par, j):
                pe.wait_ge(a_ready, k + 1)
                for t in range(ST):
                    last = nc.tensor.transpose(ps[:, 4 + j, :].bitcast(BF16)[:, t * P:(t + 1) * P],
                                               anat[:, par, t, j * P:(j + 1) * P], identb[:])
                last.then_inc(t_done, 1)

            def clear_sums(bank):
                nc.tensor.matmul(ps[:, bank, :], identb[:], zerob[:], start=True, stop=True, skip_group_check=True)

            def products(k, c, j, clear=None, done=False):
                pe.wait_ge(at_ready[j], k + 1)
                for t in range(ST):
                    if clear and t % 2 == 0:
                        clear(t // 2)
                    for half in range(2):
                        last = nc.tensor.matmul(ps[:, t // 2, (t % 2) * F:(t % 2 + 1) * F],
                                                at[:, j, t * P:(t + 1) * P],
                                                hid[:, JT * c + j, half * F:(half + 1) * F],
                                                start=False, stop=False, skip_group_check=True)
                    if done and t in (1, 3, 5):
                        last.then_inc(sums_done, 1)
                last.then_inc(mm_done, 1)

            def chunk(s, n, par, ahead=True, clear=None, done=False):
                for j in range(JT):
                    products(NC * s + n, column_chunk(n), j, clear=clear if j == 0 else None,
                             done=done and j == JT - 1)
                    if ahead:
                        transposes(NC * s + n + 1, 1 - par, j)

            for j in range(JT):
                transposes(0, 0, j)
            pe.wait_ge(weights_split, 2)
            pe.wait_ge(hid_lo_ready, RT // 2)

            def row_block(s, clear, last=False):
                chunk(s, 0, 0, clear=clear)
                chunk(s, 1, 1)
                with pe.Fori(2, NC - 2, 2) as n:
                    chunk(s, n, 0)
                    chunk(s, n + 1, 1)
                chunk(s, NC - 2, 0)
                chunk(s, NC - 1, 1, ahead=not last, done=True)

            def clear_after(s):
                def clear(bank):
                    pe.wait_ge(acc_free, 4 * s - 3 + bank)
                    clear_sums(bank)
                return clear

            row_block(0, clear_sums)
            with pe.Fori(1, NS - 1) as s:
                row_block(s, clear_after(s))
            row_block(NS - 1, clear_after(NS - 1), last=True)

            pe.wait_ge(branch_ready, 1)
            flag = pe.value_load(irregular[0:1, 0:1], min_val=0, max_val=1)
            with pe.If(flag == 0):
                dense_x = (xd_hi, xd_lo)

                def transpose_dense(g):
                    pe.wait_ge(dense_x_ready[g % 2], 4 * (g // 2) + 4)
                    for k in range(KT):
                        if g >= 2:
                            pe.wait_ge(xd_lo_ready, 2 * (g - 2) + k + 1)
                        for q in range(4):
                            last = nc.tensor.transpose(ps[:, 4 + 2 * (g % 2) + k, q * P:(q + 1) * P],
                                                       y[:, DT + 4 * g + q, k * P:(k + 1) * P], ident[:])
                        last.then_inc(xd_ps, 1)

                def dense_value(g):
                    pe.wait_ge(xd_lo_ready, 2 * g + 2)
                    for q in range(4):
                        t = 4 * g + q
                        if t >= 4:
                            pe.wait_ge(vd_free, t - 3)
                        product(ps[:, q, 0:F + 2], hi_lo_passes((dense_x, (wv_hi, wv_lo))),
                                lambda a, k: a[:, k, t * P:(t + 1) * P], lambda b, k: b[:, k, :]).then_inc(vd_ps, 1)

                def dense_t(m):
                    for f in range(KT):
                        last = product(ps[:, 7, f * 2 * P:(f + 1) * 2 * P], hi_lo_passes(((g_hi, g_lo), dense_x)),
                                       lambda a, k: a[:, k, f * P:(f + 1) * P],
                                       lambda b, k: b[:, k, bass.ts(m, 2 * P)])
                    last.then_inc(t_ps, 1)

                def dense_scores(m, e, first):
                    pe.wait_ge(t_lo, m + 1)
                    for c in range(DC):
                        if not first or e:
                            pe.wait_ge(scores, 8 * m + 4 * e + c - 3)
                        if e:
                            pe.wait_ge((xst_lo_ready, ts_lo_ready, vs_lo_ready, vs_lo_ready)[c],
                                       (m + 1, m + 1, 2 * m + 1, 2 * m + 2)[c])
                        elif not first and c < 2:
                            pe.wait_ge((sscores, spt_lo)[c], m)
                        if first and not e:
                            pe.wait_ge(vd_free, DT - 3 + c)
                        product(ps[:, c, :], hi_lo_passes(((td_hi, td_lo), dense_x)),
                                lambda a, k: a[:, k, e * P:(e + 1) * P],
                                lambda b, k: b[:, k, c * CW:(c + 1) * CW]).then_inc(s_ps, 1)

                def pt(j, e, c, first):
                    pe.wait_ge(probs, 4 * j + c + 1)
                    if not first or c >= 2:
                        pe.wait_ge(pt_lo, 4 * j + c - 1)
                    for q in range(JT):
                        last = nc.tensor.transpose(ps[:, 4 + c % 2, q * P:(q + 1) * P],
                                                   scd[:, e, c * CW + q * P:c * CW + (q + 1) * P], ident[:])
                    last.then_inc(pt_ps, 1)

                def pv(j, c, first):
                    pe.wait_ge(pt_lo, 4 * j + c + 1)
                    if c == 0 and not first:
                        pe.wait_ge(res_d, j)
                    for q in range(JT):
                        v_q = vd[:, JT * c + q, :]
                        for i, (p_, v_) in enumerate(((ptd_hi, v_q[:, 0:F]), (ptd_hi, v_q[:, F:2 * F]), (ptd_lo, v_q[:, 0:F]))):
                            last = nc.tensor.matmul(ps[:, 6, 0:F], p_[:, c % 2, q * P:(q + 1) * P], v_,
                                                    start=(c == 0 and q == 0 and i == 0),
                                                    stop=(c == DC - 1 and q == JT - 1 and i == 2))
                    last.then_inc(pv_done, 1)

                def small_transposes(m):
                    pe.wait_ge(xs_ready, 2 * m + 2)
                    pe.wait_ge(scores, 8 * m + 1)
                    for k in range(KT):
                        for u in range(2):
                            last = nc.tensor.transpose(ps[:, 0, (2 * k + u) * P:(2 * k + u + 1) * P],
                                                       xs[:, u, k * P:(k + 1) * P], ident[:])
                    last.then_inc(xst_ps, 1)

                def small_projections(m):
                    small_x = (xst_hi, xst_lo)
                    pe.wait_ge(xst_lo_ready, m + 1)
                    pe.wait_ge(scores, 8 * m + 4)
                    for f in range(KT):
                        last = product(ps[:, 1, f * 2 * P:(f + 1) * 2 * P], hi_lo_passes(((g_hi, g_lo), small_x)),
                                       lambda a, k: a[:, k, f * P:(f + 1) * P], lambda b, k: b[:, k, :])
                    last.then_inc(ts_ps, 1)
                    for u in range(2):
                        product(ps[:, 2 + u, 0:F + 2], hi_lo_passes((small_x, (wv_hi, wv_lo))),
                                lambda a, k: a[:, k, u * P:(u + 1) * P], lambda b, k: b[:, k, :]).then_inc(vs_ps, 1)

                def small_scores(m):
                    pe.wait_ge(ts_lo_ready, m + 1)
                    pe.wait_ge(scores, 8 * m + 5)
                    for u in range(2):
                        last = product(ps[:, 0, u * 2 * P:(u + 1) * 2 * P], hi_lo_passes(((ts_hi, ts_lo), (xst_hi, xst_lo))),
                                       lambda a, k: a[:, k, u * P:(u + 1) * P], lambda b, k: b[:, k, :])
                    last.then_inc(ss_ps, 1)

                def small_pt(m):
                    pe.wait_ge(sprobs, 2 * m + 2)
                    pe.wait_ge(scores, 8 * m + 6)
                    for u in range(2):
                        last = nc.tensor.transpose(ps[:, 1, u * P:(u + 1) * P], small_p[:, u, :], ident[:])
                    last.then_inc(spt_ps, 1)

                def small_pv(m):
                    pe.wait_ge(spt_lo, m + 1)
                    for u in range(2):
                        cols = slice(u * P, (u + 1) * P)
                        for i, (p_, v_) in enumerate(((pts_hi, vs_hi), (pts_hi, vs_lo), (pts_lo, vs_hi))):
                            last = nc.tensor.matmul(ps[:, 7, u * F:(u + 1) * F], p_[:, cols], v_[:, u, :],
                                                    start=(i == 0), stop=(i == 2))
                    last.then_inc(spv_done, 1)

                def attend(j, e, first=False, between=None, late=None):
                    pv(j, 0, first)
                    pt(j, e, 2, first)
                    pv(j, 1, first)
                    if between:
                        between()
                    pt(j, e, 3, first)
                    pv(j, 2, first)
                    pv(j, 3, first)
                    if late:
                        late()

                def start_attend(j, e, first=False):
                    pt(j, e, 0, first)
                    pt(j, e, 1, first)

                def body(m, first=False, last=False):
                    dense_scores(m, 0, first)
                    if not first:
                        small_pv(m - 1)
                    small_transposes(m)
                    if first:
                        small_projections(m)
                    else:
                        attend(2 * m - 1, 1, between=lambda: small_projections(m))
                    start_attend(2 * m, 0, first=first)
                    dense_scores(m, 1, first)
                    if not last:
                        if not first:
                            pe.wait_ge(res_s, 2 * m)
                        dense_t(m + 1)
                    small_scores(m)
                    attend(2 * m, 0, first=first, late=lambda: small_pt(m))
                    start_attend(2 * m + 1, 1)

                for j in range(JT):
                    pe.wait_ge(at_ready[j], NC * NS)
                transpose_dense(0)
                transpose_dense(1)
                pe.wait_ge(acc_free, 4 * NS)
                dense_value(0)
                transpose_dense(2)
                dense_value(1)
                transpose_dense(3)
                dense_value(2)
                pe.wait_ge(xd_lo_ready, 2 * DG)
                dense_t(0)
                dense_value(3)
                body(0, first=True)
                with pe.Fori(1, PAIRS - 1) as m:
                    body(m)
                body(PAIRS - 1, last=True)
                pe.wait_ge(res_s, 2 * (PAIRS - 1))
                small_pv(PAIRS - 1)
                attend(2 * PAIRS - 1, 1)
            with pe.Else():
                pe.wait_ge(xn_ready, RT)
                pe.wait_ge(g_loaded, 16 * 7)
                pe.wait_ge(g_ones, 1)
                pe.wait_ge(g_bb, 1)
                pe.wait_ge(acc_free, 4 * NS)
                for m in range(KT):
                    for k in range(KT):
                        nc.tensor.matmul(ps[:, m, 0:F], wqf[:, k, m * P:(m + 1) * P], wkf[:, k, :],
                                         start=(k == 0), stop=(k == KT - 1))
                    for k in range(KT):
                        nc.tensor.transpose(ps[:, 2 + m, k * P:(k + 1) * P], wvf[:, k, m * P:(m + 1) * P], ident[:])
                    for col, w, b in ((m, wkf, bqc), (2 + m, wqf, bkc)):
                        for k in range(KT):
                            nc.tensor.matmul(ps[:, 4, col:col + 1], w[:, k, m * P:(m + 1) * P], b[:, k:k + 1],
                                             start=(k == 0), stop=(k == KT - 1))
                for k in range(KT):
                    last = nc.tensor.matmul(ps[:, 4, 4:5], ones[:], bkc2[:, k:k + 1], start=(k == 0), stop=(k == KT - 1))
                last.then_inc(g_wps, 1)
                pe.wait_ge(g_geq, 1)
                for t in range(RT):
                    last = nc.tensor.matmul(ps[:, 5, t:t + 1], geq[0:NPTR, t * P:(t + 1) * P], ones[0:NPTR, 0:1],
                                            start=True, stop=True)
                last.then_inc(g_gid_ps, 1)
                for c in range(NC):
                    pe.wait_ge(g_gid, c + 1)
                    nc.tensor.matmul(ps[:, 6, :], ones[0:NPTR, :], geq[0:NPTR, c * CW:(c + 1) * CW],
                                     start=True, stop=True).then_inc(g_gid_ps, 1)
                for g in range(RT // 4):
                    for k in range(KT):
                        if g >= 1:
                            pe.wait_ge(g_xt, 2 * (g - 1) + k + 1)
                        else:
                            pe.wait_ge(g_wsb, 1)
                        for q in range(4):
                            last = nc.tensor.transpose(ps[:, k, q * P:(q + 1) * P], y[:, 4 * g + q, k * P:(k + 1) * P], ident[:])
                        last.then_inc(g_xt_ps, 1)
                pe.wait_ge(g_xt, 2 * (RT // 4))
                for t in range(RT):
                    if t >= 2:
                        pe.wait_ge(g_v, t - 1)
                    for k in range(KT):
                        last = nc.tensor.matmul(ps[:, 2 + t % 2, 0:F + 1], xT[:, k, t * P:(t + 1) * P], wvT[:, k, :],
                                                start=(k == 0), stop=(k == KT - 1))
                    last.then_inc(g_v_ps, 1)
                pe.wait_ge(g_v, RT)
                with pe.Fori(0, RT) as i:
                    pe.wait_ge(g_fin, i + 1)
                    for m in range(KT):
                        for k in range(KT):
                            last = nc.tensor.matmul(ps[:, 0, m * P:(m + 1) * P], gmat[:, k, m * P:(m + 1) * P],
                                                    xT[:, k, bass.ts(i, P)], start=(k == 0), stop=(k == KT - 1))
                    last.then_inc(g_t_ps, 1)
                    pe.wait_ge(g_t, i + 1)
                    for c in range(NC):
                        for k in range(KT):
                            last = nc.tensor.matmul(ps[:, c, :], tT[:, k, :], xT[:, k, c * CW:(c + 1) * CW],
                                                    start=(k == 0), stop=(k == KT - 1))
                        last.then_inc(g_s_ps, 1)
                    pe.wait_ge(g_p, i + 1)
                    for c in range(NC):
                        for q in range(JT):
                            j = JT * c + q
                            last = nc.tensor.transpose(ps[:, c, q * P:(q + 1) * P], sc[:, j * P:(j + 1) * P], ident[:])
                        last.then_inc(g_pt_ps, 1)
                    pe.wait_ge(g_pt, NC * i + NC)
                    for j in range(RT):
                        last = nc.tensor.matmul(ps[:, 0, 0:F], pT[:, j, :], v[:, j, 0:F], start=(j == 0), stop=(j == RT - 1))
                    last.then_inc(g_o_ps, 1)

        @block.scalar
        def _(act):
            act.wait_ge(w0_loaded, 32)
            nc.scalar.copy(w0_hi[:], w0f).then_inc(w0_split, 1)
            act.wait_ge(ident_ready, 1)
            nc.scalar.copy(identb[:], ident[:]).then_inc(identb_ready, 1)

            def xt_hi(g):
                for k in range(KT):
                    act.wait_ge(xt_done, 2 * g + k + 1)
                    if g >= 2:
                        act.wait_ge(hid_done, 4 * (g - 1))
                    nc.scalar.copy(xT_hi[:, g % 2, k, :], ps[:, 2 * (g % 2) + k, :]).then_inc(xt_hi_ready, 1)

            xt_hi(0)
            for g in range(RT // 4):
                if g + 1 < RT // 4:
                    xt_hi(g + 1)
                for h in range(2):
                    act.wait_ge(hsum_ready, 2 * g + h + 1)
                    t = 4 * g + 2 * h
                    nc.scalar.copy(hid[:, t:t + 2, 0:F], hsum[:, 2 * h:2 * h + 2, :]).then_inc(hid_hi_ready, 1)
            act.wait_ge(weights_sums, 1)
            nc.scalar.mul(g_hi[:], ps[:, 0, :].rearrange("p (k f) -> p k f", f=F), SCALE / 2)
            nc.scalar.copy(wv_hi[:, :, 0:F], ps[:, 1, :].rearrange("p (k f) -> p k f", f=F))
            nc.scalar.mul(wcols[:, 0:5], ps[:, 2, 0:5], SCALE).then_inc(weights_hi, 1)

            def evacuate(s, n, j):
                k = NC * s + n
                act.wait_ge(t_done, JT * k + j + 1)
                if k >= 1:
                    act.wait_ge(mm_done, JT * (k - 1) + j + 1)
                nc.scalar.activation(at[:, j, :], ps[:, 4 + j, :].bitcast(BF16), ACT.Copy,
                                     accum_out=degp[:, JT * column_chunk(n) + j, s:s + 1]).then_inc(at_ready[j], 1)

            def outside(s, n, tiles):
                if not has_outside(s, n):
                    return
                if tiles[0] == 0:
                    act.wait_ge(ebias_ready, outside_count(s, n))
                for t in tiles:
                    row = ST * BLOCKS[s] + t
                    w = adjb[:, n % SLOTS, t, :]
                    last = nc.scalar.activation(w, w, ACT.Exp, scale=2 * NEG,
                                                bias=ebias[:, n % SLOTS, t:t + 1], accum_out=zpart[:, row, n:n + 1])
                if tiles[-1] == ST - 1:
                    last.then_inc(outside_done, 1)

            def take_sums(s, banks=range(4)):
                row = ST * BLOCKS[s]
                for b in banks:
                    if b < 3:
                        act.wait_ge(sums_done, 3 * s + b + 1)
                    else:
                        act.wait_ge(mm_done, JT * NC * (s + 1))
                    nc.scalar.copy(y[:, row + 2 * b:row + 2 * b + 2, :],
                                   ps[:, b, :].rearrange("p (t f) -> p t f", f=F)).then_inc(acc_free, 1)

            act.wait_ge(hid_done, RT)
            act.wait_ge(outside_cleared, 2)
            for s in range(NS):
                for n in range(NC):
                    evacuate(s, n, 0)
                    outside(s, n, range(0, 3))
                    evacuate(s, n, 1)
                    if s >= 1 and n == 0:
                        evacuate(s, n, 2)
                        take_sums(s - 1)
                    outside(s, n, range(3, 6))
                    if not (s >= 1 and n == 0):
                        evacuate(s, n, 2)
                    outside(s, n, range(6, ST))

            act.wait_ge(branch_ready, 1)
            flag = act.value_load(irregular[0:1, 0:1], min_val=0, max_val=1)
            with act.If(flag == 0):
                def normalise_dense(g):
                    act.wait_ge(dense_rstd_ready, max(g, 1))
                    for q in range(4):
                        t = 4 * g + q
                        nc.scalar.activation(y[:, DT + t, :], y[:, DT + t, :], ACT.Identity, scale=rstd_d[:, t:t + 1],
                                             bias=shift_d[:, t:t + 1]).then_inc(dense_x_ready[1], 1)

                def split_dense(g):
                    for k in range(KT):
                        act.wait_ge(xd_ps, 2 * g + k + 1)
                        nc.scalar.copy(xd_hi[:, k, g * CW:(g + 1) * CW], ps[:, 4 + 2 * (g % 2) + k, :]).then_inc(xd_hi_ready, 1)

                def value_dense(g):
                    for q in range(4):
                        t = 4 * g + q
                        act.wait_ge(vd_ps, t + 1)
                        nc.scalar.copy(vd[:, t, 0:F], ps[:, q, 0:F]).then_inc(vd_hi_ready, 1)

                def split_t(m):
                    act.wait_ge(t_ps, m + 1)
                    for f in range(KT):
                        last = nc.scalar.activation(td_hi[:, f, :], ps[:, 7, f * 2 * P:(f + 1) * 2 * P], ACT.Identity,
                                                    bias=gv[:, f:f + 1])
                    last.then_inc(t_hi, 1)

                def pt_split(j, c):
                    act.wait_ge(pt_ps, 4 * j + c + 1)
                    nc.scalar.copy(ptd_hi[:, c % 2, :], ps[:, 4 + c % 2, :]).then_inc(pt_hi, 1)

                def exp_dense(i, e, c):
                    if c == 0:
                        act.wait_ge(max_step, 3 * i + 3)
                    cols = scd[:, e, c * CW:(c + 1) * CW]
                    nc.scalar.activation(cols, cols, ACT.Exp, bias=dense_stat(e, "bias"),
                                         accum_out=dense_stat(e, "z4")[:, c:c + 1]).then_inc(probs, 1)

                def exp_outside(i, e):
                    nc.scalar.activation(dense_stat(e, "out"), dense_stat(e, "m"), ACT.Exp, scale=-1.0,
                                         bias=out_max[:, bass.ds(i + DT, 1)]).then_inc(out_exp, 1)

                def small_x(m):
                    act.wait_ge(small_rstd_ready, m + 1)
                    if not (isinstance(m, int) and m == 0):
                        act.wait_ge(xst_ps, m)
                    for u in range(2):
                        nc.scalar.activation(xs[:, u, :], small_raw[:, u, :], ACT.Identity, scale=rstd_s[:, u:u + 1],
                                             bias=shift_s[:, u:u + 1]).then_inc(xs_ready, 1)
                    for u in range(2):
                        nc.scalar.activation(y[:, 2 * m + u, :], small_raw[:, u, :], ACT.Identity, scale=rstd_s[:, u:u + 1],
                                             bias=shift_s[:, u:u + 1]).then_inc(xs_kept, 1)

                def small_pt_split(m):
                    act.wait_ge(spt_ps, m + 1)
                    nc.scalar.copy(pts_hi[:], ps[:, 1, 0:2 * P]).then_inc(spt_hi, 1)

                def small_split(m):
                    act.wait_ge(ts_ps, m + 1)
                    for f in range(KT):
                        last = nc.scalar.activation(ts_hi[:, f, :], ps[:, 1, f * 2 * P:(f + 1) * 2 * P], ACT.Identity,
                                                    bias=gv[:, f:f + 1])
                    last.then_inc(ts_hi_ready, 1)
                    for u in range(2):
                        act.wait_ge(vs_ps, 2 * m + u + 1)
                        nc.scalar.copy(vs_hi[:, u, :], ps[:, 2 + u, 0:F]).then_inc(vs_hi_ready, 1)

                def small_exp(m):
                    act.wait_ge(smax_step, 4 * m + 4)
                    for u in range(2):
                        nc.scalar.activation(small_p[:, u, :], small_p[:, u, :], ACT.Exp, scale=2.0, bias=small_stat("bias", u),
                                             accum_out=small_stat("zs", u)).then_inc(sprobs, 1)
                    nc.scalar.activation(small_stat("out"), small_stat("dm"), ACT.Exp).then_inc(sout_exp, 1)

                def normalise_results(m, results=range(4), count=1):
                    act.wait_ge(rstd_ready, m + count)
                    act.wait_ge(fin_free, m + 1)
                    for q in results:
                        nc.scalar.activation(fin[:, q, :], res[:, q, :], ACT.Identity, scale=rstd_r[:, q:q + 1],
                                             bias=shift_r[:, q:q + 1]).then_inc(normed, 1)

                def body(m, first=False, last=False):
                    if not first:
                        pt_split(2 * m - 1, 0)
                        pt_split(2 * m - 1, 1)
                        small_x(m)
                    act.wait_ge(xst_ps, m + 1)
                    nc.scalar.copy(xst_hi[:], ps[:, 0, :].rearrange("p (k w) -> p k w", k=KT)).then_inc(xst_hi_ready, 1)
                    exp_dense(2 * m, 0, 0)
                    exp_dense(2 * m, 0, 1)
                    if not first:
                        pt_split(2 * m - 1, 2)
                    exp_dense(2 * m, 0, 2)
                    exp_dense(2 * m, 0, 3)
                    exp_outside(2 * m, 0)
                    small_split(m)
                    if not first:
                        pt_split(2 * m - 1, 3)
                    pt_split(2 * m, 0)
                    pt_split(2 * m, 1)
                    if not first:
                        normalise_results(m - 1)
                    if not last:
                        split_t(m + 1)
                    exp_dense(2 * m + 1, 1, 0)
                    exp_dense(2 * m + 1, 1, 1)
                    pt_split(2 * m, 2)
                    exp_dense(2 * m + 1, 1, 2)
                    exp_dense(2 * m + 1, 1, 3)
                    pt_split(2 * m, 3)
                    small_exp(m)
                    exp_outside(2 * m + 1, 1)
                    small_pt_split(m)

                normalise_dense(1)
                take_sums(NS - 1)
                split_dense(0)
                split_dense(1)
                value_dense(0)
                split_dense(2)
                normalise_dense(3)
                value_dense(1)
                split_dense(3)
                act.wait_ge(out_step, 3)
                nc.scalar.activation(least[:], least[:], ACT.Exp, scale=2 * NEG).then_inc(out_weights, 1)
                value_dense(2)
                split_t(0)
                value_dense(3)
                small_x(0)
                body(0, first=True)
                with act.Fori(1, PAIRS - 1) as m:
                    body(m)
                body(PAIRS - 1, last=True)
                for c in range(DC):
                    pt_split(2 * PAIRS - 1, c)
                normalise_results(PAIRS - 1, (2, 3))
                normalise_results(PAIRS - 1, (0, 1), count=2)
            with act.Else():
                take_sums(NS - 1)
                act.wait_ge(ln, 3)
                nc.scalar.activation(lnt[:, 3, :], lnt[:, 2, :], ACT.Sqrt).then_inc(std_ready, 1)

                act.wait_ge(g_wps, 1)
                for m in range(KT):
                    act.wait_ge(xn_ready, RT)
                    nc.scalar.mul(gmat[:, m, :], ps[:, m, 0:F], SCALE)
                    nc.scalar.copy(wvT[:, m, 0:F], ps[:, 2 + m, 0:F])
                nc.scalar.mul(gvec[:], ps[:, 4, 0:KT], SCALE)
                nc.scalar.mul(wvT[:, :, F], ps[:, 4, 2:2 + KT], SCALE)
                nc.scalar.mul(gbv[:, F:F + 1], ps[:, 4, 4:5], SCALE).then_inc(g_wsb, 1)
                for g in range(RT // 4):
                    for k in range(KT):
                        act.wait_ge(g_xt_ps, 2 * g + k + 1)
                        nc.scalar.copy(xT[:, k, g * CW:(g + 1) * CW], ps[:, k, :]).then_inc(g_xt, 1)
                with act.Fori(0, RT) as i:
                    act.wait_ge(g_t_ps, i + 1)
                    for m in range(KT):
                        last = nc.scalar.activation(tT[:, m, :], ps[:, 0, m * P:(m + 1) * P], ACT.Identity, bias=gvec[:, m:m + 1])
                    last.then_inc(g_t, 1)
                    act.wait_ge(g_max, i + 2)
                    nc.scalar.activation(sc[:], sc[:], ACT.Exp, bias=stat[:, 0:1], accum_out=stat[:, 1:2]).then_inc(g_exp, 1)
                    for c in range(NC):
                        act.wait_ge(g_pt_ps, NC * i + c + 1)
                        nc.scalar.copy(pT[:, JT * c:JT * (c + 1), :], ps[:, c, :].rearrange("p (t w) -> p t w", w=P)).then_inc(g_pt, 1)
                    act.wait_ge(g_var, i + 1)
                    nc.scalar.activation(stat[:, 5:6], stat[:, 4:5], ACT.Sqrt).then_inc(g_std, 1)

        @block.vector
        def _(dve):
            dve.wait_ge(w0_split, 1)
            nc.vector.tensor_tensor(w0_lo[:], w0f, w0_hi[:].bitcast(F32), ALU.subtract).then_inc(w0_split, 1)

            def xt_lo(g):
                for k in range(KT):
                    dve.wait_ge(xt_hi_ready, 2 * g + k + 1)
                    if g >= 2:
                        dve.wait_ge(hid_done, 4 * (g - 1))
                    nc.vector.tensor_tensor(xT_lo[:, g % 2, k, :], ps[:, 2 * (g % 2) + k, :],
                                            xT_hi[:, g % 2, k, :].bitcast(F32), ALU.subtract).then_inc(xt_lo_ready, 1)

            def weights_products_and_ptr():
                dve.wait_ge(weights_loaded, 16 * 7)
                dve.wait_ge(ones_ready, 2)
                nc.vector.tensor_tensor(bb_in, bq_in, bk_in, ALU.mult).then_inc(weights_products, 1)
                nc.vector.tensor_copy(ptr_f, ptr_in).then_inc(ptr_step, 1)
                nc.vector.tensor_copy(ptr_d, ptr_want).then_inc(ptr_step, 1)
                dve.wait_ge(ptr_step, 2)
                nc.vector.tensor_tensor(ptr_f, ptr_f, ptr_d, ALU.subtract).then_inc(ptr_step, 1)
                dve.wait_ge(ptr_step, 3)
                nc.vector.tensor_tensor(ptr_d, ptr_f, ptr_f, ALU.mult).then_inc(ptr_far, 1)

            xt_lo(0)
            for g in range(RT // 4):
                if g + 1 < RT // 4:
                    xt_lo(g + 1)
                if g == 4:
                    weights_products_and_ptr()
                for h in range(2):
                    bank, _ = hid_bank(g, 2 * h)
                    dve.wait_ge(hid_done, 4 * g + 2 * h + 2)
                    if g >= 1:
                        dve.wait_ge(hid_lo_ready, 2 * g + h - 1)
                    nc.vector.tensor_tensor(hsum[:, 2 * h:2 * h + 2, :], ps[:, bank, :].rearrange("p (t f) -> p t f", f=F),
                                            b0b[:, None, :].to_broadcast((P, 2, F)), ALU.add).then_inc(hsum_ready, 1)
                for h in range(2):
                    t = 4 * g + 2 * h
                    dve.wait_ge(hid_hi_ready, 2 * g + h + 1)
                    nc.vector.tensor_tensor(hid[:, t:t + 2, F:2 * F], hsum[:, 2 * h:2 * h + 2, :],
                                            hid[:, t:t + 2, 0:F].bitcast(F32), ALU.subtract).then_inc(hid_lo_ready, 1)
            def make_a(s, n):
                k = NC * s + n
                dve.wait_ge(slot_loaded[n % SLOTS], 16 * (k // SLOTS + 1))
                if k == 1:
                    dve.wait_ge(a_ready, 1)
                if k >= 2:
                    dve.wait_ge(t_done, JT * (k - 1))
                nc.vector.tensor_scalar(anat[:, n % 2], adjb[:, n % SLOTS], 0.0, None, ALU.not_equal).then_inc(a_ready, 1)

            def outside(s, n):
                if not has_outside(s, n):
                    return
                if BLOCKS[s] < 2 and column_chunk(n) // 2 == BLOCKS[s]:
                    dve.wait_ge(masked, column_chunk(n) + 1)
                rows = slice(ST * BLOCKS[s], ST * (BLOCKS[s] + 1))
                nc.vector.tensor_reduce(least[:, rows, n], adjb[:, n % SLOTS], AX.X, ALU.min).then_inc(least_ready, 1)
                dve.wait_ge(least_ready, outside_count(s, n))
                nc.vector.tensor_scalar(ebias[:, n % SLOTS, :], least[:, rows, n], -2 * NEG, None, ALU.mult).then_inc(ebias_ready, 1)

            def evacuate(s, n):
                k, j = NC * s + n, JT - 1
                dve.wait_ge(t_done, JT * k + j + 1)
                if k >= 1:
                    dve.wait_ge(mm_done, JT * (k - 1) + j + 1)
                nc.vector.tensor_scalar(at[:, j, :], ps[:, 4 + j, :].bitcast(BF16), 1.0, None, ALU.mult, ALU.add,
                                        accum_out=degp[:, JT * column_chunk(n) + j, s:s + 1]).then_inc(at_ready[j], 1)

            dve.wait_ge(hid_done, RT)
            dve.wait_ge(hid_lo_ready, RT // 2)
            dve.wait_ge(outside_cleared, 2)
            make_a(0, 1)
            dve.wait_ge(weights_hi, 1)
            for m in range(KT):
                nc.vector.scalar_tensor_tensor(g_lo[:, m, :], ps[:, 0, m * F:(m + 1) * F], SCALE / 2,
                                               g_hi[:, m, :].bitcast(F32), ALU.mult, ALU.subtract)
                nc.vector.tensor_tensor(wv_lo[:, m, 0:F], ps[:, 1, m * F:(m + 1) * F], wv_hi[:, m, 0:F].bitcast(F32), ALU.subtract)
            nc.vector.memset(wv_hi[:, :, F + 1].bitcast(F32), 0.0)
            nc.vector.memset(wv_lo[:, :, F + 1].bitcast(F32), 0.0)
            nc.vector.tensor_scalar(gv[:], wcols[:, 0:KT], 0.5, None, ALU.mult)
            nc.vector.tensor_scalar(bqbk[:], wcols[:, 4:5], 1.0, None, ALU.mult)
            nc.vector.tensor_scalar(irregular[:], ps[0:1, 2, 5:6], 1.0, None, ALU.min).then_inc(branch_ready, 1)
            nc.vector.tensor_copy(wv_hi[:, :, F], wcols[:, KT:2 * KT]).then_inc(weights_split, 1)
            dve.wait_ge(weights_split, 1)
            nc.vector.tensor_tensor(wv_lo[:, :, F], wcols[:, KT:2 * KT], wv_hi[:, :, F].bitcast(F32), ALU.subtract).then_inc(weights_split, 1)
            for s in range(NS):
                for n in range(NC):
                    k = NC * s + n
                    if k >= 2:
                        evacuate(*divmod(k - 2, NC))
                        make_a(s, n)
                    if k == NC * (NS - 1) + DC + 2:
                        for j in range(JT):
                            dve.wait_ge(at_ready[j], k - 2)
                        nc.vector.reduce_sum(deg[:, DT:RT], degp[:, DT:RT, :], AX.X).then_inc(dense_deg_ready, 1)
                        dve.wait_ge(dense_deg_ready, 1)
                        nc.vector.reciprocal(rdeg[:, DT:RT], deg[:, DT:RT]).then_inc(dense_deg_ready, 1)
                    outside(s, n)

            dve.wait_ge(branch_ready, 1)
            flag = dve.value_load(irregular[0:1, 0:1], min_val=0, max_val=1)
            with dve.If(flag == 0):
                stt, tt, ts = nc.vector.scalar_tensor_tensor, nc.vector.tensor_tensor, nc.vector.tensor_scalar

                def dense_residual(g):
                    for q in range(4):
                        t = DT + 4 * g + q
                        stt(y[:, t, :], y[:, t, :], rdeg[:, t:t + 1], again[:, 4 * g + q, :], ALU.mult, ALU.add).then_inc(dense_residual_rest, 1)

                def dense_stats(g):
                    for q in range(4):
                        t = 4 * g + q
                        if g < 2:
                            dve.wait_ge(dense_residual_first, t + 1)
                        else:
                            dve.wait_ge(dense_residual_rest, t - 7)
                        nc.vector.bn_stats(half_stats[:, t, :], y[:, DT + t, :]).then_inc(dense_stats_ready, 1)

                def normalise_dense(g):
                    dve.wait_ge(dense_rstd_ready, max(g, 1))
                    for q in range(4):
                        t = 4 * g + q
                        ts(y[:, DT + t, :], y[:, DT + t, :], rstd_d[:, t:t + 1], shift_d[:, t:t + 1],
                           ALU.mult, ALU.add).then_inc(dense_x_ready[0], 1)

                def split_dense(g):
                    for k in range(KT):
                        dve.wait_ge(xd_hi_ready, 2 * g + k + 1)
                        cols = slice(g * CW, (g + 1) * CW)
                        tt(xd_lo[:, k, cols], ps[:, 4 + 2 * (g % 2) + k, :], xd_hi[:, k, cols].bitcast(F32),
                           ALU.subtract).then_inc(xd_lo_ready, 1)

                def value_dense(g):
                    for q in range(4):
                        t = 4 * g + q
                        dve.wait_ge(vd_hi_ready, t + 1)
                        tt(vd[:, t, F:2 * F], ps[:, q, 0:F], vd[:, t, 0:F].bitcast(F32), ALU.subtract)
                        tt(dense_const[:, t:t + 1], ps[:, q, F:F + 1], bqbk[:], ALU.add).then_inc(vd_free, 1)

                def split_t(m):
                    dve.wait_ge(t_hi, m + 1)
                    for f in range(KT):
                        last = stt(td_lo[:, f, :], ps[:, 7, f * 2 * P:(f + 1) * 2 * P], gv[:, f:f + 1],
                                   td_hi[:, f, :].bitcast(F32), ALU.add, ALU.subtract)
                    last.then_inc(t_lo, 1)

                def make_scores(i, e, m, between=None):
                    dve.wait_ge(adjd_loaded[e], 16 * m + 16)
                    for c in range(DC):
                        cols = slice(c * CW, (c + 1) * CW)
                        dve.wait_ge(s_ps, 4 * i + c + 1)
                        nc.vector.memset(settled[:, c:c + 1], 0.0)
                        nc.vector.tensor_tensor_reduce(out=scd[:, e, cols], in0=ps[:, c, :], in1=adjd[:, e, cols], scale=2.0,
                                                       scalar=-3e38, op0=ALU.add, op1=ALU.max,
                                                       accum_out=dense_stat(e, "mx4")[:, c:c + 1]).then_inc(scores, 1)
                        if between and c == 0:
                            between()
                    dve.wait_ge(scores, 4 * i + 4)
                    c_i = dense_const[:, bass.ds(i, 1)]
                    nc.vector.reduce_max(dense_stat(e, "mx"), dense_stat(e, "mx4"), AX.X).then_inc(max_step, 1)
                    dve.wait_ge(max_step, 3 * i + 1)
                    ts(dense_stat(e, "m"), dense_stat(e, "mx"), c_i, out_max[:, bass.ds(i + DT, 1)], ALU.add, ALU.max).then_inc(max_step, 1)
                    dve.wait_ge(max_step, 3 * i + 2)
                    tt(dense_stat(e, "bias"), c_i, dense_stat(e, "m"), ALU.subtract).then_inc(max_step, 1)

                def split_pt(j, c):
                    dve.wait_ge(pt_hi, 4 * j + c + 1)
                    tt(ptd_lo[:, c % 2, :], ps[:, 4 + c % 2, :], ptd_hi[:, c % 2, :].bitcast(F32), ALU.subtract).then_inc(pt_lo, 1)

                def sums_dense(j, e):
                    dve.wait_ge(out_exp, j + 1)
                    nc.vector.reduce_sum(dense_stat(e, "zs"), dense_stat(e, "z4"), AX.X).then_inc(z_step, 1)
                    dve.wait_ge(z_step, 3 * j + 1)
                    stt(dense_stat(e, "z"), dense_stat(e, "out"), out_sum[:, bass.ds(j + DT, 1)], dense_stat(e, "zs"),
                        ALU.mult, ALU.add).then_inc(z_step, 1)
                    dve.wait_ge(z_step, 3 * j + 2)
                    nc.vector.reciprocal(dense_stat(e, "rz"), dense_stat(e, "z")).then_inc(z_step, 1)

                def finish_dense(j, e):
                    dve.wait_ge(pv_done, 4 * j + 4)
                    dve.wait_ge(normed, 2 * (j - e) + e + 1)
                    stt(res[:, e, :], bvs[:], dense_stat(e, "zs"), ps[:, 6, 0:F], ALU.mult, ALU.add).then_inc(res_d, 1)
                    dve.wait_ge(z_step, 3 * j + 3)
                    dve.wait_ge(res_d, j + 1)
                    stt(res[:, e, :], res[:, e, :], dense_stat(e, "rz"), y[:, j + DT, :], ALU.mult, ALU.add).then_inc(o_step, 1)

                def results_stats(m, results=range(4)):
                    if 0 in results:
                        dve.wait_ge(o_step, 2 * m + 2)
                    if 2 in results:
                        dve.wait_ge(so_step, 2 * m + 2)
                    for q in results:
                        nc.vector.bn_stats(half_stats[:, 18 + q, :], res[:, q, :]).then_inc(bn_ready, 1)

                def small_residual(m, first=False):
                    dve.wait_ge(small_again_loaded, 16)
                    if not first:
                        dve.wait_ge(xs_kept, 2 * m)
                    for u in range(2):
                        stt(small_raw[:, u, :], y[:, 2 * m + u, :], rdeg[:, bass.ds(2 * m + u, 1)], xs_again[:, 2 * m + u, :],
                            ALU.mult, ALU.add).then_inc(small_raw_ready, 1)
                    for u in range(2):
                        dve.wait_ge(small_raw_ready, 2 * m + u + 1)
                        nc.vector.bn_stats(half_stats[:, 16 + u, :], small_raw[:, u, :]).then_inc(small_stats_ready, 1)

                def small_split_x(m):
                    dve.wait_ge(xst_hi_ready, m + 1)
                    tt(xst_lo[:], ps[:, 0, :].rearrange("p (k w) -> p k w", k=KT), xst_hi[:].bitcast(F32),
                       ALU.subtract).then_inc(xst_lo_ready, 1)

                def small_split_t(m):
                    dve.wait_ge(ts_hi_ready, m + 1)
                    for f in range(KT):
                        last = stt(ts_lo[:, f, :], ps[:, 1, f * 2 * P:(f + 1) * 2 * P], gv[:, f:f + 1],
                                   ts_hi[:, f, :].bitcast(F32), ALU.add, ALU.subtract)
                    last.then_inc(ts_lo_ready, 1)

                def small_split_v(m):
                    for u in range(2):
                        dve.wait_ge(vs_hi_ready, 2 * m + u + 1)
                        tt(vs_lo[:, u, :], ps[:, 2 + u, 0:F], vs_hi[:, u, :].bitcast(F32), ALU.subtract)
                        tt(small_const[:, u:u + 1], ps[:, 2 + u, F:F + 1], bqbk[:], ALU.add).then_inc(vs_lo_ready, 1)

                def small_scores(m):
                    dve.wait_ge(ss_ps, m + 1)
                    dve.wait_ge(sadj_masked, m + 1)
                    for u in range(2):
                        last = tt(small_p[:, u, :], ps[:, 0, u * 3 * P:u * 3 * P + P], sadjm[:, u, :], ALU.add)
                    last.then_inc(sscores, 1)
                    dve.wait_ge(sscores, m + 1)
                    dve.wait_ge(vs_lo_ready, 2 * m + 2)
                    nc.vector.reduce_max(small_stat("mx"), small_p[:], AX.X).then_inc(smax_step, 1)
                    dve.wait_ge(smax_step, 4 * m + 1)
                    mout_m = out_max[:, bass.ds(2 * m, 2)]
                    stt(small_stat("t"), small_stat("mx"), 2.0, small_const, ALU.mult, ALU.add).then_inc(smax_step, 1)
                    dve.wait_ge(smax_step, 4 * m + 2)
                    tt(small_stat("m"), small_stat("t"), mout_m, ALU.max).then_inc(smax_step, 1)
                    dve.wait_ge(smax_step, 4 * m + 3)
                    tt(small_stat("dm"), mout_m, small_stat("m"), ALU.subtract)
                    tt(small_stat("bias"), small_const, small_stat("m"), ALU.subtract).then_inc(smax_step, 1)

                def small_split_pt(m):
                    dve.wait_ge(spt_hi, m + 1)
                    tt(pts_lo[:], ps[:, 1, 0:2 * P], pts_hi[:].bitcast(F32), ALU.subtract).then_inc(spt_lo, 1)

                def finish_small(m):
                    dve.wait_ge(sout_exp, m + 1)
                    tt(small_stat("z"), small_stat("out"), out_sum[:, bass.ds(2 * m, 2)], ALU.mult).then_inc(sz_step, 1)
                    dve.wait_ge(sz_step, 3 * m + 1)
                    tt(small_stat("z"), small_stat("z"), small_stat("zs"), ALU.add).then_inc(sz_step, 1)
                    dve.wait_ge(sz_step, 3 * m + 2)
                    nc.vector.reciprocal(small_stat("rz"), small_stat("z")).then_inc(sz_step, 1)
                    dve.wait_ge(spv_done, m + 1)
                    dve.wait_ge(normed, 4 * m + 4)
                    for u in range(2):
                        stt(res[:, 2 + u, :], bvs[:], small_stat("zs", u), ps[:, 7, u * F:(u + 1) * F], ALU.mult, ALU.add).then_inc(res_s, 1)
                    dve.wait_ge(sz_step, 3 * m + 3)
                    dve.wait_ge(xs_kept, 2 * m + 2)
                    for u in range(2):
                        dve.wait_ge(res_s, 2 * m + u + 1)
                        stt(res[:, 2 + u, :], res[:, 2 + u, :], small_stat("rz", u), y[:, 2 * m + u, :], ALU.mult, ALU.add).then_inc(so_step, 1)

                def body(m, first=False, last=False):
                    if not first:
                        split_pt(2 * m - 1, 0)
                        split_pt(2 * m - 1, 1)
                        make_scores(2 * m, 0, m, between=lambda: sums_dense(2 * m - 1, 1))
                        small_split_x(m)
                        finish_small(m - 1)
                        split_pt(2 * m - 1, 2)
                        small_split_t(m)
                        split_pt(2 * m - 1, 3)
                        small_split_v(m)
                        finish_dense(2 * m - 1, 1)
                        results_stats(m - 1)
                    else:
                        make_scores(2 * m, 0, m)
                        small_split_x(m)
                        small_split_t(m)
                        small_split_v(m)
                    split_pt(2 * m, 0)
                    make_scores(2 * m + 1, 1, m, between=lambda: split_pt(2 * m, 1))
                    if not last:
                        split_t(m + 1)
                    small_scores(m)
                    split_pt(2 * m, 2)
                    split_pt(2 * m, 3)
                    if not last:
                        small_residual(m + 1)
                    small_split_pt(m)
                    sums_dense(2 * m, 0)
                    finish_dense(2 * m, 0)

                dve.wait_ge(dense_deg_ready, 2)
                dve.wait_ge(again_loaded, 16)
                evacuate(NS - 1, NC - 2)
                dense_stats(0)
                dense_stats(1)
                dense_residual(2)
                dense_stats(2)
                evacuate(NS - 1, NC - 1)
                normalise_dense(0)
                dense_residual(3)
                split_dense(0)
                dense_stats(3)
                normalise_dense(2)
                split_dense(1)
                value_dense(0)
                split_dense(2)
                value_dense(1)
                split_dense(3)
                nc.vector.tensor_reduce(lowest, least[:], AX.X, ALU.min).then_inc(out_step, 1)
                dve.wait_ge(out_step, 1)
                ts(out_max, lowest, 2 * NEG, None, ALU.mult).then_inc(out_step, 1)
                tt(least[:], least[:], lowest[:, :, None].to_broadcast((P, RT, NC)), ALU.subtract).then_inc(out_step, 1)
                dve.wait_ge(acc_free, 4 * NS)
                for j in range(JT):
                    dve.wait_ge(at_ready[j], NC * NS)
                nc.vector.reduce_sum(deg[:, 0:DT], degp[:, 0:DT, :], AX.X).then_inc(small_deg_ready, 1)
                dve.wait_ge(small_deg_ready, 1)
                nc.vector.reciprocal(rdeg[:, 0:DT], deg[:, 0:DT]).then_inc(small_deg_ready, 1)
                dve.wait_ge(small_deg_ready, 2)
                small_residual(0, first=True)
                value_dense(2)
                dve.wait_ge(out_weights, 1)
                tt(zpart[:], zpart[:], least[:], ALU.mult).then_inc(out_step, 1)
                dve.wait_ge(out_step, 4)
                nc.vector.reduce_sum(out_sum, zpart[:], AX.X).then_inc(out_step, 1)
                split_t(0)
                value_dense(3)
                dve.wait_ge(vd_free, DT)
                dve.wait_ge(out_step, 5)
                body(0, first=True)
                with dve.Fori(1, PAIRS - 1) as m:
                    body(m)
                body(PAIRS - 1, last=True)
                sums_dense(2 * PAIRS - 1, 1)
                split_pt(2 * PAIRS - 1, 0)
                split_pt(2 * PAIRS - 1, 1)
                finish_small(PAIRS - 1)
                split_pt(2 * PAIRS - 1, 2)
                results_stats(PAIRS - 1, (2, 3))
                split_pt(2 * PAIRS - 1, 3)
                finish_dense(2 * PAIRS - 1, 1)
                results_stats(PAIRS - 1, (0, 1))
            with dve.Else():
                evacuate(NS - 1, NC - 2)
                evacuate(NS - 1, NC - 1)
                for j in range(JT):
                    dve.wait_ge(at_ready[j], NC * NS)
                nc.vector.reduce_sum(deg[:], degp[:], AX.X).then_inc(deg_ready, 1)
                dve.wait_ge(deg_ready, 1)
                nc.vector.reciprocal(rdeg[:], deg[:]).then_inc(deg_ready, 1)
                dve.wait_ge(deg_ready, 2)
                dve.wait_ge(acc_free, 4 * NS)
                dve.wait_ge(xre_loaded, 16)
                with dve.Fori(0, RT) as t:
                    nc.vector.scalar_tensor_tensor(y[:, t, :], y[:, t, :], rdeg[:, bass.ds(t, 1)], xre[:, t, :],
                                                   ALU.mult, ALU.add).then_inc(y_raw, 1)
                    dve.wait_ge(y_raw, t + 1)
                    nc.vector.bn_stats(bst[:, t, :], y[:, t, :]).then_inc(y_stats, 1)
                dve.wait_ge(y_stats, RT)
                d, m2, var, sd, mean, rsd = (lnt[:, q, :] for q in range(6))
                nc.vector.tensor_tensor(d, bst[:, :, 1], bst[:, :, 4], ALU.subtract)
                nc.vector.tensor_tensor(m2, bst[:, :, 2], bst[:, :, 5], ALU.add)
                nc.vector.tensor_tensor(mean, bst[:, :, 1], bst[:, :, 4], ALU.add).then_inc(ln, 1)
                dve.wait_ge(ln, 1)
                nc.vector.tensor_scalar(m2, m2, 1.0 / F, EPS, ALU.mult, ALU.add)
                nc.vector.tensor_scalar(mean, mean, 0.5, None, ALU.mult)
                nc.vector.scalar_tensor_tensor(d, d, 0.25, d, ALU.mult, ALU.mult).then_inc(ln, 1)
                dve.wait_ge(ln, 2)
                nc.vector.tensor_tensor(var, d, m2, ALU.add).then_inc(ln, 1)
                dve.wait_ge(std_ready, 1)
                nc.vector.reciprocal(rsd, sd).then_inc(ln, 1)
                dve.wait_ge(ln, 4)
                nc.vector.tensor_tensor(rsd, rsd, var, ALU.mult).then_inc(ln, 1)
                dve.wait_ge(ln, 5)
                nc.vector.tensor_tensor(rsd, rsd, sd, ALU.add).then_inc(ln, 1)
                dve.wait_ge(ln, 6)
                nc.vector.tensor_scalar(rsd, rsd, 0.5, None, ALU.mult).then_inc(ln, 1)
                dve.wait_ge(ln, 7)
                nc.vector.reciprocal(rsd, rsd).then_inc(ln, 1)
                dve.wait_ge(ln, 8)
                with dve.Fori(0, RT) as t:
                    nc.vector.tensor_scalar(y[:, t, :], y[:, t, :], lnt[:, 4, bass.ds(t, 1)], lnt[:, 5, bass.ds(t, 1)],
                                            ALU.subtract, ALU.mult).then_inc(xn_ready, 1)

                dve.wait_ge(g_loaded, 16 * 7)
                dve.wait_ge(xn_ready, RT)
                nc.vector.tensor_tensor(bkc2[:], bqc[:], bkc[:], ALU.mult).then_inc(g_bb, 1)
                nc.vector.tensor_copy(ptrf[0:NPTR, :], ptri[0:NPTR, :]).then_inc(g_ptrf, 1)
                dve.wait_ge(g_ptrf, 1)
                dve.wait_ge(g_iota, 1)
                nc.vector.tensor_scalar(geq[0:NPTR, :], iota[0:NPTR, :], ptrf[0:NPTR, 0:1], None, ALU.is_ge).then_inc(g_geq, 1)
                dve.wait_ge(g_gid_ps, 1)
                nc.vector.tensor_copy(gid_col[:], ps[:, 5, 0:RT]).then_inc(g_gid, 1)
                for c in range(NC):
                    dve.wait_ge(g_gid_ps, c + 2)
                    nc.vector.tensor_copy(gid_row[:, c * CW:(c + 1) * CW], ps[:, 6, :]).then_inc(g_gid, 1)
                dve.wait_ge(g_wsb, 1)
                for t in range(RT):
                    dve.wait_ge(g_v_ps, t + 1)
                    nc.vector.tensor_tensor(v[:, t, :], ps[:, 2 + t % 2, 0:F + 1], gbv[:], ALU.add).then_inc(g_v, 1)
                dve.wait_ge(g_gid, NC + 1)
                dve.wait_ge(g_v, RT)
                nc.vector.tensor_copy(crow[:], v[:, :, F]).then_inc(g_chain, 1)
                dve.wait_ge(g_chain, 1)
                nc.vector.memset(stat[:], 0.0).then_inc(g_max, 1)
                nc.vector.memset(gfin[:], 0.0).then_inc(g_fin, 1)
                LINKS = 3 * NC + 8
                with dve.Fori(0, RT) as i:
                    links = [0]

                    def link(ins):
                        links[0] += 1
                        ins.then_inc(g_chain, 1)
                        dve.wait_ge(g_chain, i * LINKS + (links[0] + 1))

                    gid_i, c_i = gid_col[:, bass.ds(i, 1)], crow[:, bass.ds(i, 1)]
                    dve.wait_ge(g_adj, 16 * i + 16)
                    for c in range(NC):
                        cols = slice(c * CW, (c + 1) * CW)
                        dve.wait_ge(g_s_ps, NC * i + c + 1)
                        link(nc.vector.scalar_tensor_tensor(inside[:], ps[:, c, :], c_i, adjr[:, cols], ALU.add, ALU.add))
                        nc.vector.tensor_scalar(sc[:, cols], adjr[:, cols], 2 * NEG, None, ALU.mult)
                        nc.vector.tensor_scalar(same[:], gid_row[:, cols], gid_i, None, ALU.is_equal)
                        link(nc.vector.tensor_tensor(inside[:], inside[:], adjr[:, cols], ALU.add))
                        nc.vector.memset(gsettled[:], 0.0)
                        link(nc.vector.copy_predicated(sc[:, cols], same[:].bitcast(I32), inside[:]))
                    nc.vector.tensor_reduce(stat[:, 0:1], sc[:], AX.X, ALU.max, negate=True).then_inc(g_max, 1)
                    dve.wait_ge(g_exp, i + 1)
                    nc.vector.scalar_tensor_tensor(sc[:], gid_row[:], gid_i, sc[:], ALU.is_equal, ALU.mult).then_inc(g_p, 1)
                    link(nc.vector.reciprocal(stat[:, 3:4], stat[:, 1:2]))
                    dve.wait_ge(g_o_ps, i + 1)
                    link(nc.vector.scalar_tensor_tensor(gres[:], ps[:, 0, 0:F], stat[:, 3:4], y[:, i, :], ALU.mult, ALU.add))
                    link(nc.vector.bn_stats(bstat[:], gres[:]))
                    nc.vector.memset(gsettled[:], 0.0)
                    link(nc.vector.bn_aggr(stat[:, 6:8], bstat[:]))
                    nc.vector.tensor_scalar(stat[:, 4:5], stat[:, 7:8], EPS, None, ALU.add).then_inc(g_var, 1)
                    dve.wait_ge(g_std, i + 1)
                    link(nc.vector.reciprocal(stat[:, 9:10], stat[:, 5:6]))
                    link(nc.vector.scalar_tensor_tensor(stat[:, 9:10], stat[:, 9:10], stat[:, 4:5], stat[:, 5:6], ALU.mult, ALU.add))
                    link(nc.vector.tensor_scalar(stat[:, 9:10], stat[:, 9:10], 0.5, None, ALU.mult))
                    link(nc.vector.reciprocal(stat[:, 10:11], stat[:, 9:10]))
                    nc.vector.tensor_scalar(gfin[:], gres[:], stat[:, 6:7], stat[:, 10:11], ALU.subtract, ALU.mult).then_inc(g_fin, 1)
                    assert links[0] == LINKS, links


def kernel(x, adj, L0_gnn_W, L0_gnn_b, L1_gnn_ptr, L1_gnn_Wq, L1_gnn_bq, L1_gnn_Wk, L1_gnn_bk, L1_gnn_Wv, L1_gnn_bv):
    import numpy as np
    import concourse.bacc as bacc
    from concourse.bass_utils import run_bass_kernel_spmd

    nc = bacc.Bacc("TRN2", target_bir_lowering=False, num_devices=1)
    arrays, args = {}, []
    for name, a in dict(x=x, adj=adj, W0=L0_gnn_W, b0=L0_gnn_b, ptr=L1_gnn_ptr, Wq=L1_gnn_Wq, bq=L1_gnn_bq,
                        Wk=L1_gnn_Wk, bk=L1_gnn_bk, Wv=L1_gnn_Wv, bv=L1_gnn_bv).items():
        a = np.ascontiguousarray(a)
        arrays[f"in_{name}"] = a
        args.append(nc.dram_tensor(f"in_{name}", a.shape, mybir.dt.from_np(a.dtype), kind="ExternalInput").ap())
    out = nc.dram_tensor("out", tuple(x.shape), mybir.dt.float32, kind="ExternalOutput").ap()
    gnn_then_graph_attention(nc, *args, out)
    r = run_bass_kernel_spmd(nc, [arrays], core_ids=[0])
    return r.results[0]["out"]
```
